# Optimizing a Trainium2 kernel written in Bass

```python
import numpy as np
import jax
import jax.numpy as jnp

def _softmax(x, axis=-1):
    return jax.nn.softmax(x, axis=axis)

def _gelu(x):
    return jax.nn.gelu(x, approximate=True)

def _silu(x):
    return jax.nn.silu(x)

def _sigmoid(x):
    return jax.nn.sigmoid(x)

def _layernorm(x, axis=-1, eps=1e-05):
    m = jnp.mean(x, axis=axis, keepdims=True)
    v = jnp.var(x, axis=axis, keepdims=True)
    return (x - m) / jnp.sqrt(v + eps)

def _scatter_add(tgt, idx, src, axis=0):
    return tgt.at[idx].add(src)

def _segment_sum(src, seg, n):
    return jax.ops.segment_sum(src, seg, n)
kernel_name = 'mk_gnn_preln_d4_gnn_r8_a684e5'

def setup_inputs(seed: int=0):
    np.random.seed(seed)
    _w = jnp.asarray

    def _rec_inputs():
        import jax
        import jax.numpy as jnp
        _gk = jax.random.key(seed)
        x = -0.0009044 + 1 * jax.random.normal(jax.random.fold_in(_gk, 1), (12500, 32), jnp.float32)
        src = jax.random.randint(jax.random.fold_in(_gk, 2), (400000,), 0, 12500, jnp.int32)
        dst = jax.random.randint(jax.random.fold_in(_gk, 3), (400000,), 0, 12500, jnp.int32)
        _o = jnp.argsort(dst, stable=True)
        src = src[_o]
        dst = dst[_o]
        edge_attr_16 = 0.000196303 + 1.00016 * jax.random.normal(jax.random.fold_in(_gk, 12), (400000, 16), jnp.float32)
        edge_weight = 0.000452788 + 0.999756 * jax.random.normal(jax.random.fold_in(_gk, 14), (400000,), jnp.float32)
        return (x, src, dst, edge_attr_16, edge_weight)
    x, src, dst, edge_attr_16, edge_weight = _rec_inputs()

    def _L0_gnn_setup():
        import jax, jax.numpy as jnp
        import numpy as np
        N_NODES = 6250
        N_EDGES = 200000
        D_NODE = 32
        D_EDGE = 16
        H = 64
        F_OUT = 32
        N_OUT = 32

        def _mlp_params(key, d_in, d_h, d_out):
            k1, k2 = jax.random.split(key)
            s1 = 1.0 / np.sqrt(d_in)
            s2 = 1.0 / np.sqrt(d_h)
            return (jax.random.uniform(k1, (d_in, d_h), jnp.float32, -s1, s1), jnp.zeros((d_h,), jnp.float32), jax.random.uniform(k2, (d_h, d_out), jnp.float32, -s2, s2), jnp.zeros((d_out,), jnp.float32))

        def _mlp(h, W1, b1, W2, b2):
            return jax.nn.relu(jax.nn.relu(h @ W1 + b1) @ W2 + b2)
        key = jax.random.key(seed)
        kx, ke, ka, kf, kb, kn = jax.random.split(key, 6)
        x = jax.random.normal(kx, (N_NODES, D_NODE), jnp.float32)
        edge_index = jax.random.randint(ke, (2, N_EDGES), 0, N_NODES, jnp.int64)
        edge_attr = jax.random.normal(ka, (N_EDGES, D_EDGE), jnp.float32)
        d_flow_in = 2 * D_NODE + D_EDGE
        W1f, b1f, W2f, b2f = _mlp_params(kf, d_flow_in, H, F_OUT)
        W1b, b1b, W2b, b2b = _mlp_params(kb, d_flow_in, H, F_OUT)
        W1n, b1n, W2n, b2n = _mlp_params(kn, 2 * F_OUT, H, N_OUT)
        return dict(x=x, edge_index=edge_index, edge_attr=edge_attr, W1f=W1f, b1f=b1f, W2f=W2f, b2f=b2f, W1b=W1b, b1b=b1b, W2b=W2b, b2b=b2b, W1n=W1n, b1n=b1n, W2n=W2n, b2n=b2n)
    _L0_gnn_all = _L0_gnn_setup()
    _L0_gnn_in = {k: v for k, v in _L0_gnn_all.items() if k in ('W1f', 'b1f', 'W2f', 'b2f', 'W1b', 'b1b', 'W2b', 'b2b', 'W1n', 'b1n', 'W2n', 'b2n')}
    del _L0_gnn_all

    def _L1_gnn_setup():
        import jax, jax.numpy as jnp
        import numpy as np
        N_NODES = 12500
        N_EDGES = 200000
        D_FEAT = 32
        key = jax.random.key(seed)
        k1, k2, k3 = jax.random.split(key, 3)
        x = jax.random.normal(k1, (N_NODES, D_FEAT), dtype=jnp.float32)
        a = jax.random.randint(k2, (2, N_EDGES), 0, N_NODES, dtype=jnp.int64)
        e = jax.random.normal(k3, (N_EDGES,), dtype=jnp.float32)
        return {'x': x, 'a': a, 'e': e}
    _L1_gnn_all = _L1_gnn_setup()
    _L1_gnn_in = {k: v for k, v in _L1_gnn_all.items() if k in ()}
    del _L1_gnn_all

    def _L2_gnn_setup():
        import jax, jax.numpy as jnp
        import numpy as np
        N_NODES = 12500
        N_EDGES = 200000
        D_FEAT = 32
        key = jax.random.key(seed)
        k_feat, k_src, k_dst = jax.random.split(key, 3)
        feat = jax.random.normal(k_feat, (N_NODES, D_FEAT), dtype=jnp.float32)
        eps = jnp.zeros((1,), dtype=jnp.float32)
        edge_src = jax.random.randint(k_src, (N_EDGES,), 0, N_NODES, dtype=jnp.int32)
        edge_dst = jax.random.randint(k_dst, (N_EDGES,), 0, N_NODES, dtype=jnp.int32)
        return {'feat': feat, 'eps': eps, 'edge_src': edge_src, 'edge_dst': edge_dst}
    _L2_gnn_all = _L2_gnn_setup()
    _L2_gnn_in = {k: v for k, v in _L2_gnn_all.items() if k in ('eps',)}
    del _L2_gnn_all

    def _L3_gnn_setup():
        import jax, jax.numpy as jnp
        import numpy as np
        N_NODES = 12500
        N_EDGES = 200000
        NUM_FEATURES = 32
        HIDDEN = 64

        def _gcn_conv(h, W, b, src, dst, norm, inv_deg, n_nodes):
            h = h @ W
            msg = h[src] * norm[:, None]
            agg = jax.ops.segment_sum(msg, dst, num_segments=n_nodes)
            agg = agg + h * inv_deg[:, None]
            return agg + b
        key = jax.random.key(seed)
        k_x, k_e, k_w1, k_b1, k_w2, k_b2 = jax.random.split(key, 6)
        X = jax.random.normal(k_x, (N_NODES, NUM_FEATURES), dtype=jnp.float32)
        connections = jax.random.randint(k_e, (2, N_EDGES), 0, N_NODES, dtype=jnp.int64)
        W1 = jax.random.normal(k_w1, (NUM_FEATURES, HIDDEN), dtype=jnp.float32) / np.sqrt(NUM_FEATURES)
        b1 = jnp.zeros((HIDDEN,), dtype=jnp.float32)
        W2 = jax.random.normal(k_w2, (HIDDEN, NUM_FEATURES), dtype=jnp.float32) / np.sqrt(HIDDEN)
        b2 = jnp.zeros((NUM_FEATURES,), dtype=jnp.float32)
        return {'X': X, 'connections': connections, 'W1': W1, 'b1': b1, 'W2': W2, 'b2': b2}
    _L3_gnn_all = _L3_gnn_setup()
    _L3_gnn_in = {k: v for k, v in _L3_gnn_all.items() if k in ('W1', 'b1', 'W2', 'b2')}
    del _L3_gnn_all
    return {'x': x, 'src': src, 'dst': dst, 'edge_attr_16': edge_attr_16, 'edge_weight': edge_weight, 'L0_gnn_W1f': _L0_gnn_in['W1f'], 'L0_gnn_b1f': _L0_gnn_in['b1f'], 'L0_gnn_W2f': _L0_gnn_in['W2f'], 'L0_gnn_b2f': _L0_gnn_in['b2f'], 'L0_gnn_W1b': _L0_gnn_in['W1b'], 'L0_gnn_b1b': _L0_gnn_in['b1b'], 'L0_gnn_W2b': _L0_gnn_in['W2b'], 'L0_gnn_b2b': _L0_gnn_in['b2b'], 'L0_gnn_W1n': _L0_gnn_in['W1n'], 'L0_gnn_b1n': _L0_gnn_in['b1n'], 'L0_gnn_W2n': _L0_gnn_in['W2n'], 'L0_gnn_b2n': _L0_gnn_in['b2n'], 'L2_gnn_eps': _L2_gnn_in['eps'], 'L3_gnn_W1': _L3_gnn_in['W1'], 'L3_gnn_b1': _L3_gnn_in['b1'], 'L3_gnn_W2': _L3_gnn_in['W2'], 'L3_gnn_b2': _L3_gnn_in['b2']}

def reference(x, src, dst, edge_attr_16, edge_weight, L0_gnn_W1f, L0_gnn_b1f, L0_gnn_W2f, L0_gnn_b2f, L0_gnn_W1b, L0_gnn_b1b, L0_gnn_W2b, L0_gnn_b2b, L0_gnn_W1n, L0_gnn_b1n, L0_gnn_W2n, L0_gnn_b2n, L2_gnn_eps, L3_gnn_W1, L3_gnn_b1, L3_gnn_W2, L3_gnn_b2):
    import jax
    import jax.numpy as jnp

    def _L0_gnn_ref(x, edge_index, edge_attr, W1f, b1f, W2f, b2f, W1b, b1b, W2b, b2b, W1n, b1n, W2n, b2n):
        import jax, jax.numpy as jnp
        import numpy as np
        N_NODES = 6250
        N_EDGES = 200000
        D_NODE = 32
        D_EDGE = 16
        H = 64
        F_OUT = 32
        N_OUT = 32

        def _mlp_params(key, d_in, d_h, d_out):
            k1, k2 = jax.random.split(key)
            s1 = 1.0 / np.sqrt(d_in)
            s2 = 1.0 / np.sqrt(d_h)
            return (jax.random.uniform(k1, (d_in, d_h), jnp.float32, -s1, s1), jnp.zeros((d_h,), jnp.float32), jax.random.uniform(k2, (d_h, d_out), jnp.float32, -s2, s2), jnp.zeros((d_out,), jnp.float32))

        def _mlp(h, W1, b1, W2, b2):
            return jax.nn.relu(jax.nn.relu(h @ W1 + b1) @ W2 + b2)
        past, future = (edge_index[0], edge_index[1])
        x_past = x[past]
        x_future = x[future]
        fwd_in = jnp.concatenate([x_future, x_past, edge_attr], axis=1)
        flow_fwd = _mlp(fwd_in, W1f, b1f, W2f, b2f)
        fwd_agg = jax.ops.segment_sum(flow_fwd, future, num_segments=x.shape[0])
        bwd_in = jnp.concatenate([x_past, x_future, edge_attr], axis=1)
        flow_bwd = _mlp(bwd_in, W1b, b1b, W2b, b2b)
        bwd_agg = jax.ops.segment_sum(flow_bwd, past, num_segments=x.shape[0])
        flow_total = jnp.concatenate([fwd_agg, bwd_agg], axis=1)
        return _mlp(flow_total, W1n, b1n, W2n, b2n)

    def _L1_gnn_ref(x, a, e):
        import jax, jax.numpy as jnp
        import numpy as np
        N_NODES = 12500
        N_EDGES = 200000
        D_FEAT = 32
        src = a[0]
        tgt = a[1]
        msgs = x[src] * e[:, None]
        out = jax.ops.segment_sum(msgs, tgt, num_segments=x.shape[0])
        return out

    def _L2_gnn_ref(feat, eps, edge_src, edge_dst):
        import jax, jax.numpy as jnp
        import numpy as np
        N_NODES = 12500
        N_EDGES = 200000
        D_FEAT = 32
        neigh = jax.ops.segment_sum(feat[edge_src], edge_dst, num_segments=feat.shape[0])
        return (1.0 + eps) * feat + neigh

    def _L3_gnn_ref(X, connections, W1, b1, W2, b2):
        import jax, jax.numpy as jnp
        import numpy as np
        N_NODES = 12500
        N_EDGES = 200000
        NUM_FEATURES = 32
        HIDDEN = 64

        def _gcn_conv(h, W, b, src, dst, norm, inv_deg, n_nodes):
            h = h @ W
            msg = h[src] * norm[:, None]
            agg = jax.ops.segment_sum(msg, dst, num_segments=n_nodes)
            agg = agg + h * inv_deg[:, None]
            return agg + b
        n_nodes = X.shape[0]
        src, dst = (connections[0], connections[1])
        ones = jnp.ones(src.shape[0], dtype=X.dtype)
        deg = jax.ops.segment_sum(ones, dst, num_segments=n_nodes) + 1.0
        inv_sqrt = jax.lax.rsqrt(deg)
        norm = inv_sqrt[src] * inv_sqrt[dst]
        inv_deg = 1.0 / deg
        h = _gcn_conv(X, W1, b1, src, dst, norm, inv_deg, n_nodes)
        h = _gcn_conv(h, W2, b2, src, dst, norm, inv_deg, n_nodes)
        return jax.nn.relu(h)
    edge_index = jnp.stack([src, dst])
    h = jnp.maximum(_layernorm(x, axis=-1), 0.0)
    x = x + _L0_gnn_ref(h, edge_index, edge_attr_16, L0_gnn_W1f, L0_gnn_b1f, L0_gnn_W2f, L0_gnn_b2f, L0_gnn_W1b, L0_gnn_b1b, L0_gnn_W2b, L0_gnn_b2b, L0_gnn_W1n, L0_gnn_b1n, L0_gnn_W2n, L0_gnn_b2n)
    h = jnp.maximum(_layernorm(x, axis=-1), 0.0)
    x = x + _L1_gnn_ref(h, edge_index, edge_weight)
    h = jnp.maximum(_layernorm(x, axis=-1), 0.0)
    x = x + _L2_gnn_ref(h, L2_gnn_eps, src, dst)
    h = jnp.maximum(_layernorm(x, axis=-1), 0.0)
    x = x + _L3_gnn_ref(h, edge_index, L3_gnn_W1, L3_gnn_b1, L3_gnn_W2, L3_gnn_b2)
    return x

_drawn_inputs = setup_inputs


def setup_inputs(seed=0):
    import zlib

    import numpy as np

    out = dict(_drawn_inputs(seed))
    spreads = {'L0_gnn_b1f': (0.0, 0.1),
     'L0_gnn_b2f': (0.0, 0.1),
     'L0_gnn_b1b': (0.0, 0.1),
     'L0_gnn_b2b': (0.0, 0.1),
     'L0_gnn_b1n': (0.0, 0.34),
     'L0_gnn_b2n': (0.0, 0.1),
     'L3_gnn_b1': (0.0, 0.8),
     'L3_gnn_b2': (0.0, 0.8)}
    factors = {}
    for name, (base, spread) in spreads.items():
        noise = np.random.default_rng([zlib.crc32(name.encode()), seed]).standard_normal(out[name].shape)
        drawn = base * np.exp(spread * noise) if base else spread * noise
        out[name] = jnp.asarray(drawn.astype(out[name].dtype))
    for name, factor in factors.items():
        out[name] = (out[name] * factor).astype(out[name].dtype)
    return out
```

```python
from contextlib import ExitStack

import numpy as np
import concourse.bass as bass
from concourse import mybir

F32 = mybir.dt.float32
BF16 = mybir.dt.bfloat16
I32 = mybir.dt.int32
ALU = mybir.AluOpType
ACT = mybir.ActivationFunctionType
AX = mybir.AxisListType.X

P = 128
TILES = 25
GROUP = P * TILES
CHUNK = 5
CHUNKS = TILES // CHUNK
COLS = CHUNK * P
BANK = 512
D = 32
DE = 16
H = 64
WINDOW = P - DE
LANES = 125
EPS = 1e-5
DMA = 16


def build(nc, a, out, n_nodes, n_edges):
    PER = n_nodes // LANES
    NG = n_edges // GROUP
    PAIRS = (NG - 1) // 2
    assert PER * LANES == n_nodes and NG * GROUP == n_edges and NG % 2 == 1 and NG <= P
    ROWS = -(-(n_nodes + P) // P) * P
    FILL = ROWS // P

    def dram(name, shape, dt=F32):
        return nc.dram_tensor(name, shape, dt).ap()

    src_rows = dram("src_rows", [NG, TILES, P])
    src_cols = dram("src_cols", [NG, P, TILES])
    local_rows = dram("local_rows", [NG, TILES, P], BF16)
    local_cols = dram("local_cols", [NG, P, TILES])
    dst_rows = dram("dst_rows", [NG, TILES, P])
    dst_cols = dram("dst_cols", [NG, P, TILES])
    bases = dram("bases", [NG, 1], I32)
    spans = dram("spans", [NG, 1])
    pre_src = dram("pre_src", [n_nodes, P])
    pre_dst = dram("pre_dst", [ROWS, P])
    feats = [dram(f"feats{n}", [n_nodes, D]) for n in range(4)]
    widths = [D, D + 1, D, D]
    sums = [dram(f"sums{n}", [ROWS, w]) for n, w in enumerate(widths)]
    fwd_sum = dram("fwd_sum", [ROWS, D])
    bwd_sum = [dram(f"bwd_sum{n}", [ROWS, D]) for n in range(CHUNK)]

    ctx = ExitStack()
    with ctx:
        def sb(name, shape, dt=F32, c=ctx):
            return c.enter_context(nc.sbuf_tensor(name, shape, dt))

        def sem(name, c=ctx):
            return c.enter_context(nc.semaphore(name))

        x = sb("x", [LANES, PER, D])
        h = sb("h", [LANES, PER, D])
        identity = sb("identity", [P, P])
        column = sb("column", [P, P])
        row_id = sb("row_id", [P, 1])
        before = sb("before", [P, P])
        spare = sb("spare", [P, 1])
        base_row = sb("base_row", [1, NG], I32)
        flag = sb("flag", [1, 1], I32)
        inv_deg = sb("inv_deg", [LANES, PER])
        inv_sqrt = sb("inv_sqrt", [LANES, PER])

        class Chain:

            def __init__(self, eng, s):
                self.eng, self.s, self.n = eng, s, 0

            def __call__(self, ins):
                self.n += 1
                ins.then_inc(self.s, 1)
                self.eng.wait_ge(self.s, self.n)

        with ExitStack() as c:
            zero = sb("zero", [P, FILL * (D + 1)], c=c)
            ints = sb("ints", [P, P], I32, c=c)
            z_ready, filled, made, v = (sem(n) for n in ("z_ready", "filled", "made", "const_v"))
            with nc.Block() as block:
                @block.vector
                def _(dve):
                    dve.memset(zero[:, :], 0.0).then_inc(z_ready, 1)
                    step = Chain(dve, v)
                    dve.wait_ge(made, 2)
                    step(nc.vector.tensor_copy(column[:, :], ints[:, :]))
                    step(nc.vector.tensor_copy(row_id[:, :], spare.ap().bitcast(I32)))
                    step(nc.vector.tensor_scalar(before[:, :], column[:, :], row_id[:, 0:1], None, ALU.is_lt))
                    step(nc.vector.tensor_scalar(identity[:, :], column[:, :], row_id[:, 0:1], None, ALU.is_equal))
                    step(nc.vector.tensor_scalar(spare[:, :], row_id[:, :], float(n_nodes), None, ALU.add))

                @block.gpsimd
                def _(pool):
                    nc.gpsimd.iota(ints[:, :], pattern=[[1, P]], base=0, channel_multiplier=0).then_inc(made, 1)
                    nc.gpsimd.iota(spare.ap().bitcast(I32), pattern=[[1, 1]], base=0, channel_multiplier=1).then_inc(made, 1)

                @block.sync
                def _(sp):
                    sp.wait_ge(z_ready, 1)
                    tables = [(t, D) for t in (fwd_sum, *bwd_sum)] + list(zip(sums, widths))
                    for t, w in tables:
                        sp.dma_start(t.rearrange("(p r) c -> p (r c)", p=P), zero[:, 0:FILL * w]).then_inc(filled, DMA)
                    sp.dma_start(pre_dst[n_nodes:ROWS].rearrange("r c -> (r c)").rearrange("(a b) -> a b", a=P),
                                 zero[:, 0:ROWS - n_nodes]).then_inc(filled, DMA)
                    sp.wait_ge(filled, DMA * (len(tables) + 1))

        with ExitStack() as c:
            src_i = sb("src_i", [NG, P, TILES], I32, c=c)
            dst_i = sb("dst_i", [NG, P, TILES], I32, c=c)
            src_f = sb("src_f", [NG, P, TILES], c=c)
            dst_f = sb("dst_f", [NG, P, TILES], c=c)
            loc_f = sb("loc_f", [NG, P, TILES], c=c)
            src_t = sb("src_t", [NG, TILES, P], c=c)
            dst_t = sb("dst_t", [NG, TILES, P], c=c)
            loc_t = sb("loc_t", [NG, TILES, P], BF16, c=c)
            low = sb("low", [NG, 1], c=c)
            high = sb("high", [NG, 1], c=c)
            low_i = sb("low_i", [NG, 1], I32, c=c)
            span_row = sb("span_row", [1, NG], c=c)
            widest = sb("widest", [1, 1], c=c)
            loaded, v, stored, back = (sem(n) for n in ("idx_loaded", "idx_v", "idx_stored", "idx_back"))
            with nc.Block() as block:
                @block.sync
                def _(sp):
                    sp.dma_start(src_i[:, :, :], a["src"]).then_inc(loaded, DMA)
                    sp.dma_start(dst_i[:, :, :], a["dst"]).then_inc(loaded, DMA)
                    sp.dma_start(x[:, :, :], a["x"].rearrange("(p j) f -> p j f", p=LANES)).then_inc(loaded, DMA)
                    sp.wait_ge(v, 10)
                    pairs = [(src_cols, src_f), (src_rows, src_t), (dst_cols, dst_f), (dst_rows, dst_t),
                             (local_cols, loc_f), (local_rows, loc_t)]
                    for table, tile in pairs:
                        sp.dma_start(table, tile[:, :, :]).then_inc(stored, DMA)
                    sp.dma_start(bases, low_i[:, :]).then_inc(stored, DMA)
                    sp.dma_start(spans, high[:, :]).then_inc(stored, DMA)
                    sp.wait_ge(stored, DMA * (len(pairs) + 2))
                    sp.dma_start(base_row[:, :], bases.rearrange("g o -> o g")).then_inc(back, DMA)
                    sp.dma_start(span_row[:, :], spans.rearrange("g o -> o g")).then_inc(back, DMA)
                    sp.wait_ge(back, 2 * DMA)

                @block.vector
                def _(dve):
                    step = Chain(dve, v)
                    dve.wait_ge(loaded, 3 * DMA)
                    step(nc.vector.tensor_copy(src_f[:, :, :], src_i[:, :, :]))
                    step(nc.vector.tensor_copy(dst_f[:, :, :], dst_i[:, :, :]))
                    step(nc.vector.tensor_copy(src_t[:, :, :], src_f[:, :, :].rearrange("g p t -> g t p")))
                    step(nc.vector.tensor_copy(dst_t[:, :, :], dst_f[:, :, :].rearrange("g p t -> g t p")))
                    flat = dst_f[:, :, :].rearrange("g p t -> g (p t)")
                    step(nc.vector.tensor_reduce(low[:, :], flat, AX, ALU.min))
                    step(nc.vector.tensor_reduce(high[:, :], flat, AX, ALU.max))
                    step(nc.vector.tensor_scalar(loc_f[:, :, :], dst_f[:, :, :], low[:, 0:1], None, ALU.subtract))
                    step(nc.vector.tensor_copy(loc_t[:, :, :], loc_f[:, :, :].rearrange("g p t -> g t p")))
                    step(nc.vector.tensor_copy(low_i[:, :], low[:, :]))
                    step(nc.vector.tensor_scalar(high[:, :], high[:, :], low[:, 0:1], None, ALU.subtract))
                    dve.wait_ge(back, 2 * DMA)
                    step(nc.vector.tensor_reduce(widest[:, :], span_row[:, :], AX, ALU.max))
                    step(nc.vector.tensor_scalar(widest[:, :], widest[:, :], float(WINDOW), None, ALU.is_lt))
                    step(nc.vector.tensor_copy(flag[:, :], widest[:, :]))

        def over(ap):
            return ap[:, :].unsqueeze(2).to_broadcast([LANES, PER, D])

        def layernorm(step, act_done, dve_ready, n, t):
            mean, var, xc, sq = t
            step(nc.vector.tensor_reduce(mean[:, :], x[:, :, :], AX, ALU.add))
            step(nc.vector.tensor_scalar(mean[:, :], mean[:, :], 1.0 / D, None, ALU.mult))
            step(nc.vector.tensor_tensor(xc[:, :, :], x[:, :, :], over(mean), ALU.subtract))
            step(nc.vector.tensor_tensor(sq[:, :, :], xc[:, :, :], xc[:, :, :], ALU.mult))
            step(nc.vector.tensor_reduce(var[:, :], sq[:, :, :], AX, ALU.add))
            step(nc.vector.tensor_scalar(var[:, :], var[:, :], 1.0 / D, EPS, ALU.mult, ALU.add))
            step.eng.sem_inc(dve_ready, 1)
            step.eng.wait_ge(act_done, n)
            step(nc.vector.reciprocal(var[:, :], var[:, :]))
            step(nc.vector.tensor_tensor(xc[:, :, :], xc[:, :, :], over(var), ALU.mult))
            step(nc.vector.tensor_scalar(h[:, :, :], xc[:, :, :], 0.0, None, ALU.max))

        def root(act, dve_ready, act_done, ap, n):
            act.wait_ge(dve_ready, n)
            nc.scalar.activation(ap, ap, ACT.Sqrt).then_inc(act_done, 1)

        def scratch(c, tag):
            return (sb(f"mean{tag}", [LANES, PER], c=c), sb(f"var{tag}", [LANES, PER], c=c),
                    sb(f"xc{tag}", [LANES, PER, D], c=c), sb(f"sq{tag}", [LANES, PER, D], c=c))

        QUAD = 4
        TURNS = PER // QUAD
        assert TURNS * QUAD == PER

        with ExitStack() as c:
            t = scratch(c, "0")
            w_pre = sb("w_pre", [D, 2 * P], c=c)
            cols = sb("cols0", [LANES, QUAD, D], c=c)
            feat = sb("feat0", [D, QUAD * LANES], c=c)
            rows = sb("rows0", [LANES, QUAD, 2 * P], c=c)
            p_t = c.enter_context(nc.psum_tensor("p_t0", [D, BANK], F32))
            p_o = c.enter_context(nc.psum_tensor("p_o0", [LANES, QUAD, 2 * P], F32))
            names = ("n0_w", "n0_v", "n0_ready", "n0_root", "n0_cols", "n0_turned", "n0_feat", "n0_product", "n0_rows", "n0_stored")
            w_in, v, ready, rooted, s_cols, s_tr, s_feat, s_mm, s_out, s_st = (sem(n) for n in names)
            with nc.Block() as block:
                @block.sync
                def _(sp):
                    w1f, w1b = a["L0_gnn_W1f"], a["L0_gnn_W1b"]
                    for n, part in enumerate((w1f[D:2 * D], w1b[0:D], w1f[0:D], w1b[D:2 * D])):
                        sp.dma_start(w_pre[:, n * H:(n + 1) * H], part).then_inc(w_in, DMA)
                    with sp.Fori(0, TURNS) as i:
                        sp.wait_ge(s_out, i * 2 + 2)
                        for n, table in enumerate((pre_src, pre_dst)):
                            sp.dma_start(table[0:n_nodes].rearrange("(p j) f -> p j f", p=LANES)[:, bass.ds(i * QUAD, QUAD)],
                                         rows[:, :, n * P:(n + 1) * P]).then_inc(s_st, DMA)
                    sp.wait_ge(s_st, 2 * DMA * TURNS)

                @block.vector
                def _(dve):
                    step = Chain(dve, v)
                    layernorm(step, rooted, ready, 1, t)
                    with dve.Fori(0, TURNS) as i:
                        nc.vector.tensor_copy(cols[:, :, :], h[:, bass.ds(i * QUAD, QUAD), :]).then_inc(s_cols, 1)
                        dve.wait_ge(s_tr, i + 1)
                        nc.vector.tensor_copy(feat[:, :], p_t[:, 0:QUAD * LANES]).then_inc(s_feat, 1)
                        dve.wait_ge(s_mm, i + 1)
                        nc.vector.tensor_copy(rows[:, 0:2, :], p_o[:, 0:2, :]).then_inc(s_out, 1)
                        dve.wait_ge(s_st, i * (2 * DMA) + 2 * DMA)

                @block.scalar
                def _(act):
                    root(act, ready, rooted, t[1][:, :], 1)
                    with act.Fori(0, TURNS) as i:
                        act.wait_ge(s_mm, i + 1)
                        nc.scalar.activation(rows[:, 2:4, :], p_o[:, 2:4, :], ACT.Copy).then_inc(s_out, 1)
                        act.wait_ge(s_st, i * (2 * DMA) + 2 * DMA)

                @block.tensor
                def _(pe):
                    pe.wait_ge(w_in, 4 * DMA)
                    with pe.Fori(0, TURNS) as i:
                        pe.wait_ge(s_cols, i + 1)
                        for q in range(QUAD):
                            last = nc.tensor.transpose(p_t[:, q * LANES:(q + 1) * LANES], cols[:, q, :], identity[0:LANES, 0:LANES])
                        last.then_inc(s_tr, 1)
                        pe.wait_ge(s_feat, i + 1)
                        for q in range(QUAD):
                            last = nc.tensor.matmul(p_o[:, q, :], feat[:, q * LANES:(q + 1) * LANES], w_pre[:, :],
                                                    start=True, stop=True)
                        last.then_inc(s_mm, 1)

        def node_mlp(tag, given, k, w1, b1, w2, fn, taken):
            with ExitStack() as c:
                w1_s = sb(f"w1_{tag}", [k, H], c=c)
                w2_s = sb(f"w2_{tag}", [H, D], c=c)
                b1_s = sb(f"b1_{tag}", [H, 1], c=c)
                cols = sb(f"cols_{tag}", [LANES, QUAD, k], c=c)
                feat = sb(f"feat_{tag}", [k, QUAD * LANES], c=c)
                hid = sb(f"hid_{tag}", [H, QUAD * LANES], c=c)
                p_t = c.enter_context(nc.psum_tensor(f"p_t_{tag}", [k, BANK], F32))
                p_h = c.enter_context(nc.psum_tensor(f"p_h_{tag}", [H, BANK], F32))
                p_o = c.enter_context(nc.psum_tensor(f"p_o_{tag}", [LANES, BANK], F32))
                names = ("weights", "cols", "turned", "feat", "hidden", "activated", "product", "taken", "turn")
                w_in, s_cols, s_tr, s_feat, s_hid, s_act, s_mm, s_out, s_turn = (sem(f"{tag}_{n}") for n in names)
                with nc.Block() as block:
                    @block.sync
                    def _(sp):
                        sp.dma_start(w1_s[:, :], w1).then_inc(w_in, DMA)
                        sp.dma_start(w2_s[:, :], w2).then_inc(w_in, DMA)
                        sp.dma_start(b1_s[:, :], b1.rearrange("(h o) -> h o", o=1)).then_inc(w_in, DMA)

                    @block.vector
                    def _(dve):
                        with dve.Fori(0, TURNS) as i:
                            nc.vector.tensor_copy(cols[:, :, :], given[:, bass.ds(i * QUAD, QUAD), :]).then_inc(s_cols, 1)
                            dve.wait_ge(s_tr, i + 1)
                            nc.vector.tensor_copy(feat[:, :], p_t[:, 0:QUAD * LANES]).then_inc(s_feat, 1)
                            dve.wait_ge(s_mm, i + 1)
                            nc.vector.tensor_copy(taken[:, bass.ds(i * QUAD, QUAD), :],
                                                  p_o[:, 0:QUAD * D].rearrange("p (q f) -> p q f", q=QUAD)).then_inc(s_out, 1)

                    @block.scalar
                    def _(act):
                        act.wait_ge(w_in, 3 * DMA)
                        with act.Fori(0, TURNS) as i:
                            act.wait_ge(s_hid, i + 1)
                            nc.scalar.activation(hid[:, :], p_h[:, 0:QUAD * LANES], fn, bias=b1_s[:, 0:1]).then_inc(s_act, 1)

                    @block.tensor
                    def _(pe):
                        pe.wait_ge(w_in, 3 * DMA)
                        with pe.Fori(0, TURNS) as i:
                            pe.wait_ge(s_cols, i + 1)
                            pe.sem_inc(s_turn, 1)
                            for q in range(QUAD):
                                last = nc.tensor.transpose(p_t[:, q * LANES:(q + 1) * LANES], cols[:, q, :], identity[0:LANES, 0:LANES])
                            last.then_inc(s_tr, 1)
                            pe.wait_ge(s_feat, i + 1)
                            pe.sem_inc(s_turn, 1)
                            nc.tensor.matmul(p_h[:, 0:QUAD * LANES], w1_s[:, :], feat[:, :], start=True, stop=True).then_inc(s_hid, 1)
                            pe.wait_ge(s_act, i + 1)
                            for q in range(QUAD):
                                last = nc.tensor.matmul(p_o[:, q * D:(q + 1) * D], hid[:, q * LANES:(q + 1) * LANES], w2_s[:, :],
                                                        start=True, stop=True)
                            last.then_inc(s_mm, 1)

        def window_rows(sp, table, base):
            return table[bass.ds(base, WINDOW)]

        def fetch_base(eng, g):
            at = base_row[0:1, g:g + 1] if isinstance(g, int) else base_row[0:1, bass.ds(g, 1)]
            return eng.value_load(at, min_val=0, max_val=n_nodes - 1)

        def at_group(table, g):
            return table[g] if isinstance(g, int) else table[bass.ds(g, 1)].rearrange("o p t -> (o p) t")

        def row_group(table, g, first=0, count=TILES):
            flat = table.rearrange("g t p -> g (t p)")
            one = flat[g:g + 1] if isinstance(g, int) else flat[bass.ds(g, 1)]
            return one[:, first * P:(first + count) * P].to_broadcast([P, count * P])

        def both_paths(eng, fast, general):
            fits = eng.value_load(flag[0:1, 0:1], min_val=0, max_val=1)
            with eng.If(fits > 0):
                fast()
            with eng.Else():
                general()

        def merge_steps(dve, s, count, cols, row, same, earlier, twin, away, to_row, rest=6):
            def add(ins, n):
                ins.then_inc(s, 1)
                dve.wait_ge(s, count + n)
            shape = [P, CHUNK, P]
            add(nc.vector.tensor_tensor(same[:, :, :], row[:, :, :], cols.unsqueeze(2).to_broadcast(shape), ALU.is_equal), 1)
            add(nc.vector.tensor_tensor(earlier[:, :, :], same[:, :, :], before[:, :].unsqueeze(1).to_broadcast(shape), ALU.mult), 2)
            add(nc.vector.tensor_reduce(twin[:, :], earlier[:, :, :], AX, ALU.add), 3)
            add(nc.vector.tensor_scalar(away[:, :], cols, -1.0, spare[:, 0:1], ALU.mult, ALU.add), 4)
            add(nc.vector.scalar_tensor_tensor(out=away[:, :], in0=twin[:, :], scalar=0.0, in1=away[:, :], op0=ALU.is_gt, op1=ALU.mult), 5)
            add(nc.vector.tensor_tensor(to_row[:, :], away[:, :], cols, ALU.add), 6)

        def aggregate(tag, feats_table, total, width, weights):
            with ExitStack() as c:
                loads = 3 if weights is not None else 2
                src_i = [sb(f"{tag}_src{k}", [P, TILES], I32, c=c) for k in range(2)]
                local = [sb(f"{tag}_local{k}", [P, TILES], c=c) for k in range(2)]
                wgt = [sb(f"{tag}_wgt{k}", [P, TILES], c=c) for k in range(2)]
                got = [sb(f"{tag}_got{k}", [P, TILES, D + 1], c=c) for k in range(2)]
                hot = [sb(f"{tag}_hot{k}", [P, TILES, WINDOW], c=c) for k in range(2)]
                old = [sb(f"{tag}_old{k}", [WINDOW, width], c=c) for k in range(2)]
                new = [sb(f"{tag}_new{k}", [WINDOW, width], c=c) for k in range(2)]
                p_sum = [c.enter_context(nc.psum_tensor(f"{tag}_p{k}", [WINDOW, BANK], F32)) for k in range(2)]
                same_row = sb(f"{tag}_same_row", [P, CHUNK, P], c=c)
                same = sb(f"{tag}_same", [P, CHUNK, P], c=c)
                earlier = sb(f"{tag}_earlier", [P, CHUNK, P], c=c)
                twin = sb(f"{tag}_twin", [P, CHUNK], c=c)
                away = sb(f"{tag}_away", [P, CHUNK], c=c)
                to_row = sb(f"{tag}_to_row", [P, CHUNK], I32, c=c)
                merged = sb(f"{tag}_merged", [P, CHUNK, width], c=c)
                p_merged = c.enter_context(nc.psum_tensor(f"{tag}_pm", [P, BANK], F32))

                s_in, s_got, s_hot, s_summed, s_used, s_old = ([sem(f"{tag}_{n}{k}") for k in range(2)]
                                                              for n in ("in", "got", "hot", "summed", "used", "old"))
                s_stored, s_turn = sem(f"{tag}_stored"), sem(f"{tag}_turn")
                g_in, g_got, g_step, g_merged, g_copied, g_added, g_free = (
                    s_in[0], s_got[0], s_hot[0], s_summed[0], s_hot[1], s_got[1], s_summed[1])
                per_group = 2 if weights is not None else 1

                with nc.Block() as block:
                    @block.sync
                    def _(sp):
                        def load(k, g, i):
                            sp.wait_ge(s_summed[k], i + 1)
                            sp.dma_start(src_i[k][:, :], at_group(a["src"], g)).then_inc(s_in[k], DMA)
                            sp.dma_start(local[k][:, :], at_group(local_cols, g)).then_inc(s_in[k], DMA)
                            if weights is not None:
                                sp.dma_start(wgt[k][:, :], at_group(weights, g)).then_inc(s_in[k], DMA)

                        def add_window(k, g, i):
                            base = fetch_base(sp, g)
                            rows = window_rows(sp, total, base)
                            sp.dma_start(old[k][:, :], rows).then_inc(s_old[k], DMA)
                            sp.wait_ge(s_used[k], i + 2)
                            sp.dma_start(rows, new[k][:, :]).then_inc(s_stored, DMA)
                            sp.wait_ge(s_stored, (g + 1) * DMA)
                            sp.sem_inc(s_turn, 1)

                        def fast():
                            load(0, 0, 0)
                            with sp.Fori(0, PAIRS) as i:
                                load(1, i * 2 + 1, i)
                                add_window(0, i * 2, i)
                                load(0, i * 2 + 2, i + 1)
                                add_window(1, i * 2 + 1, i)
                            add_window(0, NG - 1, PAIRS)

                        def general():
                            with sp.Fori(0, NG) as g:
                                for m in range(CHUNKS):
                                    part = slice(m * CHUNK, (m + 1) * CHUNK)
                                    sp.wait_ge(g_free, g * CHUNKS + (m + 1))
                                    sp.dma_start(src_i[0][:, 0:CHUNK], at_group(a["src"], g)[:, part]).then_inc(g_in, DMA)
                                    sp.dma_start(local[0][:, 0:CHUNK], at_group(dst_cols, g)[:, part]).then_inc(g_in, DMA)
                                    sp.dma_start(same_row[:, :, :].rearrange("p t e -> p (t e)"),
                                                 row_group(dst_rows, g, m * CHUNK, CHUNK)).then_inc(g_in, DMA)
                                    if weights is not None:
                                        sp.dma_start(wgt[0][:, 0:CHUNK], at_group(weights, g)[:, part]).then_inc(g_in, DMA)

                        both_paths(sp, fast, general)

                    @block.gpsimd
                    def _(pool):
                        def gather(k, i):
                            pool.wait_ge(s_in[k], i * (loads * DMA) + loads * DMA)
                            pool.sem_inc(s_turn, 1)
                            for t in range(TILES):
                                nc.gpsimd.indirect_dma_start(
                                    out=got[k][:, t, 0:D], out_offset=None, in_=feats_table,
                                    in_offset=bass.IndirectOffsetOnAxis(ap=src_i[k][:, t:t + 1], axis=0)).then_inc(s_got[k], DMA)

                        def fast():
                            with pool.Fori(0, PAIRS) as i:
                                gather(0, i)
                                gather(1, i)
                            gather(0, PAIRS)

                        def general():
                            pool.sem_inc(g_free, 1)
                            with pool.Fori(0, NG) as g:
                                for m in range(CHUNKS):
                                    n = g * CHUNKS + m
                                    pool.wait_ge(g_in, n * ((loads + 1) * DMA) + (loads + 1) * DMA)
                                    pool.sem_inc(s_turn, 1)
                                    for t in range(CHUNK):
                                        nc.gpsimd.indirect_dma_start(
                                            out=got[0][:, t, 0:D], out_offset=None, in_=feats_table,
                                            in_offset=bass.IndirectOffsetOnAxis(ap=src_i[0][:, t:t + 1], axis=0)).then_inc(g_got, DMA)
                                    pool.wait_ge(g_copied, n + 1)
                                    pool.sem_inc(s_turn, 1)
                                    for t in range(CHUNK):
                                        nc.gpsimd.indirect_dma_start(
                                            out=total, out_offset=bass.IndirectOffsetOnAxis(ap=to_row[:, t:t + 1], axis=0),
                                            in_=merged[:, t, :], in_offset=None, compute_op=ALU.add).then_inc(g_added, DMA)
                                        pool.wait_ge(g_added, n * (CHUNK * DMA) + (t + 1) * DMA)
                                        pool.sem_inc(s_turn, 1)
                                    pool.sem_inc(g_free, 1)

                        both_paths(pool, fast, general)

                    @block.vector
                    def _(dve):
                        def one_hot(k, i):
                            dve.wait_ge(s_in[k], i * (loads * DMA) + loads * DMA)
                            nc.vector.tensor_tensor(
                                hot[k][:, :, :], column[:, 0:WINDOW].unsqueeze(1).to_broadcast([P, TILES, WINDOW]),
                                local[k][:, :].unsqueeze(2).to_broadcast([P, TILES, WINDOW]), ALU.is_equal).then_inc(s_hot[k], 1)
                            if weights is not None:
                                dve.wait_ge(s_hot[k], i * per_group + 1)
                                nc.vector.tensor_tensor(
                                    hot[k][:, :, :], hot[k][:, :, :],
                                    wgt[k][:, :].unsqueeze(2).to_broadcast([P, TILES, WINDOW]), ALU.mult).then_inc(s_hot[k], 1)

                        def add_old(k, i):
                            dve.wait_ge(s_summed[k], i + 2)
                            dve.wait_ge(s_old[k], i * DMA + DMA)
                            nc.vector.tensor_tensor(new[k][:, :], p_sum[k][:, 0:width], old[k][:, :], ALU.add).then_inc(s_used[k], 1)

                        for k in range(2):
                            nc.vector.memset(got[k][:, :, D:D + 1], 1.0).then_inc(s_used[k], 1)

                        def fast():
                            one_hot(0, 0)
                            with dve.Fori(0, PAIRS) as i:
                                one_hot(1, i)
                                add_old(0, i)
                                one_hot(0, i + 1)
                                add_old(1, i)
                            add_old(0, PAIRS)

                        def general():
                            steps = 7 if weights is not None else 6
                            with dve.Fori(0, NG) as g:
                                for m in range(CHUNKS):
                                    n = g * CHUNKS + m
                                    dve.wait_ge(g_in, n * ((loads + 1) * DMA) + (loads + 1) * DMA)
                                    merge_steps(dve, g_step, n * steps, local[0][:, 0:CHUNK], same_row, same, earlier, twin, away, to_row)
                                    if weights is not None:
                                        dve.wait_ge(g_got, n * (CHUNK * DMA) + CHUNK * DMA)
                                        nc.vector.tensor_tensor(
                                            got[0][:, 0:CHUNK, 0:D], got[0][:, 0:CHUNK, 0:D],
                                            wgt[0][:, 0:CHUNK].unsqueeze(2).to_broadcast([P, CHUNK, D]), ALU.mult).then_inc(g_step, 1)
                                    dve.wait_ge(g_merged, n + 1)
                                    nc.vector.tensor_copy(merged[:, :, :], p_merged[:, 0:CHUNK * width].rearrange(
                                        "p (t w) -> p t w", t=CHUNK)).then_inc(g_copied, 1)

                        both_paths(dve, fast, general)

                    @block.tensor
                    def _(pe):
                        def sum_group(k, i):
                            pe.wait_ge(s_got[k], i * (TILES * DMA) + TILES * DMA)
                            pe.wait_ge(s_hot[k], i * per_group + per_group)
                            pe.wait_ge(s_used[k], i + 1)
                            for t in range(TILES):
                                last = nc.tensor.matmul(p_sum[k][:, 0:width], hot[k][:, t, :], got[k][:, t, 0:width],
                                                        start=t == 0, stop=t == TILES - 1)
                            last.then_inc(s_summed[k], 1)

                        def fast():
                            for k in range(2):
                                pe.sem_inc(s_summed[k], 1)
                            with pe.Fori(0, PAIRS) as i:
                                sum_group(0, i)
                                sum_group(1, i)
                            sum_group(0, PAIRS)

                        def general():
                            steps = 7 if weights is not None else 6
                            with pe.Fori(0, NG) as g:
                                for m in range(CHUNKS):
                                    n = g * CHUNKS + m
                                    pe.wait_ge(g_got, n * (CHUNK * DMA) + CHUNK * DMA)
                                    pe.wait_ge(g_step, n * steps + steps)
                                    for t in range(CHUNK):
                                        last = nc.tensor.matmul(p_merged[:, t * width:(t + 1) * width], same[:, t, :],
                                                                got[0][:, t, 0:width], start=True, stop=True)
                                    last.then_inc(g_merged, 1)

                        both_paths(pe, fast, general)

        with ExitStack() as c:
            w_e = [sb(f"e_w1{k}", [P, P], c=c) for k in range(2)]
            hot_t = [sb(f"e_hot_t{k}", [P, TILES, P], c=c) for k in range(2)]
            local_row = [sb(f"e_local_row{k}", [P, TILES, P], BF16, c=c) for k in range(2)]
            src_row = [sb(f"e_src_row{k}", [P, TILES, P], c=c) for k in range(2)]
            src_i = [sb(f"e_src_i{k}", [P, TILES], I32, c=c) for k in range(2)]
            src_c = [sb(f"e_src_c{k}", [P, TILES], c=c) for k in range(2)]
            local = [sb(f"e_local{k}", [P, TILES], c=c) for k in range(2)]
            got = [sb(f"e_got{k}", [P, TILES, P], c=c) for k in range(2)]
            hot = [sb(f"e_hot{k}", [P, CHUNK, WINDOW], c=c) for k in range(2)]
            same = [sb(f"e_same{k}", [P, CHUNK, P], c=c) for k in range(2)]
            earlier = sb("e_earlier", [P, CHUNK, P], c=c)
            twin = sb("e_twin", [P, CHUNK], c=c)
            away = sb("e_away", [P, CHUNK], c=c)
            to_row = [sb(f"e_to_row{k}", [P, CHUNK], I32, c=c) for k in range(2)]
            hidden = sb("e_hidden", [P, COLS], c=c)
            flow = sb("e_flow", [P, CHUNK, 2 * D], c=c)
            merged = [sb(f"e_merged{k}", [P, CHUNK, D], c=c) for k in range(2)]
            b1 = sb("e_b1", [P, 1], c=c)
            w2 = sb("e_w2", [P, 2 * D], c=c)
            b2 = sb("e_b2", [1, CHUNK, 2 * D], c=c)
            one_row = sb("e_one_row", [1, P], c=c)
            old = [sb(f"e_old{k}", [WINDOW, D], c=c) for k in range(2)]
            new = [sb(f"e_new{k}", [WINDOW, D], c=c) for k in range(2)]
            p_hidden = c.enter_context(nc.psum_tensor("e_p_hidden", [P, 2, BANK], F32))
            p_flow = c.enter_context(nc.psum_tensor("e_p_flow", [P, BANK], F32))
            p_merged = c.enter_context(nc.psum_tensor("e_p_merged", [P, BANK], F32))
            p_sum = [c.enter_context(nc.psum_tensor(f"e_p_sum{k}", [WINDOW, BANK], F32)) for k in range(2)]
            dst_i = sb("e_dst_i", [P, CHUNK], I32, c=c)
            dst_c = sb("e_dst_c", [P, CHUNK], c=c)

            s_in, s_got, s_used, s_old = ([sem(f"e_{n}{k}") for k in range(2)] for n in ("in", "got", "used", "old"))
            s_tables = [sem(f"e_table{t}") for t in range(CHUNK)]
            (s_w, s_const, s_hot_t, s_step, s_hidden, s_relu, s_flow, s_flowed, s_summed, s_merged, s_sent, s_stored,
             s_turn) = (sem(f"e_{n}") for n in ("weights", "const", "hot_t", "step", "hidden", "relu", "flow", "flowed",
                                                 "summed", "merged", "sent", "stored", "turn"))
            g_in, g_got, g_step, g_hidden, g_relu, g_flow, g_flowed, g_merged, g_copied, g_added, g_free = (
                s_in[0], s_got[0], s_step, s_hidden, s_relu, s_flow, s_flowed, s_summed, s_merged, s_got[1], s_sent)
            LOADS = 7
            STEPS = 7
            BANKS = [(0, 3), (3, CHUNK)]

            def flat(ap):
                return ap.rearrange("p t e -> p (t e)")

            with nc.Block() as block:
                @block.sync
                def _(sp):
                    for k in range(2):
                        for n, w1 in enumerate((a["L0_gnn_W1f"], a["L0_gnn_W1b"])):
                            sp.dma_start(w_e[k][WINDOW:P, n * H:(n + 1) * H], w1[2 * D:2 * D + DE]).then_inc(s_w, DMA)
                    sp.wait_ge(s_const, 1)
                    for n, (w, b, bb) in enumerate((("W2f", "b1f", "b2f"), ("W2b", "b1b", "b2b"))):
                        sp.dma_start(w2[n * H:(n + 1) * H, n * D:(n + 1) * D], a[f"L0_gnn_{w}"]).then_inc(s_w, DMA)
                        sp.dma_start(b1[n * H:(n + 1) * H, :], a[f"L0_gnn_{b}"].rearrange("(h o) -> h o", o=1)).then_inc(s_w, DMA)
                        for t in range(CHUNK):
                            sp.dma_start(b2[0:1, t, n * D:(n + 1) * D], a[f"L0_gnn_{bb}"].rearrange("(o h) -> o h", o=1)).then_inc(s_w, DMA)
                    sp.wait_ge(s_w, (4 + 2 * (2 + CHUNK)) * DMA)

                    def attributes(g):
                        return a["edge_attr_16"][g] if isinstance(g, int) else a["edge_attr_16"][bass.ds(g, 1)].rearrange("o f n -> (o f) n")

                    def load(k, g, i):
                        base = fetch_base(sp, g)
                        sp.wait_ge(s_used[k], i + 1)
                        sp.dma_start(src_i[k][:, :], at_group(a["src"], g)).then_inc(s_in[k], DMA)
                        sp.dma_start(src_c[k][:, :], at_group(src_cols, g)).then_inc(s_in[k], DMA)
                        sp.dma_start(local[k][:, :], at_group(local_cols, g)).then_inc(s_in[k], DMA)
                        sp.dma_start(flat(local_row[k][:, :, :]), row_group(local_rows, g)).then_inc(s_in[k], DMA)
                        sp.dma_start(flat(src_row[k][:, :, :]), row_group(src_rows, g)).then_inc(s_in[k], DMA)
                        sp.dma_start(flat(hot_t[k][WINDOW:P, :, :]), attributes(g)).then_inc(s_in[k], DMA)
                        sp.dma_start(w_e[k][0:WINDOW, :], window_rows(sp, pre_dst, base)).then_inc(s_in[k], DMA)

                    def add_window(k, g, i):
                        base = fetch_base(sp, g)
                        rows = window_rows(sp, fwd_sum, base)
                        sp.dma_start(old[k][:, :], rows).then_inc(s_old[k], DMA)
                        sp.wait_ge(s_used[k], i + 2)
                        sp.dma_start(rows, new[k][:, :]).then_inc(s_stored, DMA)
                        sp.wait_ge(s_stored, (g + 1) * DMA)
                        sp.sem_inc(s_turn, 1)

                    def fast():
                        load(0, 0, 0)
                        with sp.Fori(0, PAIRS) as i:
                            load(1, i * 2 + 1, i)
                            add_window(0, i * 2, i)
                            load(0, i * 2 + 2, i + 1)
                            add_window(1, i * 2 + 1, i)
                        add_window(0, NG - 1, PAIRS)

                    def general():
                        with sp.Fori(0, NG) as g:
                            for m in range(CHUNKS):
                                part = slice(m * CHUNK, (m + 1) * CHUNK)
                                sp.wait_ge(g_free, g * CHUNKS + (m + 1))
                                sp.dma_start(src_i[0][:, 0:CHUNK], at_group(a["src"], g)[:, part]).then_inc(g_in, DMA)
                                sp.dma_start(dst_i[:, :], at_group(a["dst"], g)[:, part]).then_inc(g_in, DMA)
                                sp.dma_start(src_c[0][:, 0:CHUNK], at_group(src_cols, g)[:, part]).then_inc(g_in, DMA)
                                sp.dma_start(dst_c[:, :], at_group(dst_cols, g)[:, part]).then_inc(g_in, DMA)
                                for n, rows in enumerate((src_rows, dst_rows)):
                                    sp.dma_start(flat(src_row[n][:, 0:CHUNK, :]), row_group(rows, g, m * CHUNK, CHUNK)).then_inc(g_in, DMA)
                                sp.dma_start(flat(hot_t[0][WINDOW:P, 0:CHUNK, :]), attributes(g)[:, m * COLS:(m + 1) * COLS]).then_inc(g_in, DMA)

                    both_paths(sp, fast, general)

                @block.gpsimd
                def _(pool):
                    def gather(table, index, tile, s):
                        nc.gpsimd.indirect_dma_start(out=tile, out_offset=None, in_=table,
                                                     in_offset=bass.IndirectOffsetOnAxis(ap=index, axis=0)).then_inc(s, DMA)

                    def scatter(table, index, tile, s):
                        nc.gpsimd.indirect_dma_start(out=table, out_offset=bass.IndirectOffsetOnAxis(ap=index, axis=0),
                                                     in_=tile, in_offset=None, compute_op=ALU.add).then_inc(s, DMA)

                    def fast():
                        pool.sem_inc(s_sent, 1)
                        pool.wait_ge(s_in[0], LOADS * DMA)
                        for t in range(TILES):
                            gather(pre_src, src_i[0][:, t:t + 1], got[0][:, t, :], s_got[0])

                        def group(k, i, following):
                            if following is not None:
                                pool.wait_ge(s_in[1 - k], following * (LOADS * DMA) + LOADS * DMA)
                                pool.sem_inc(s_turn, 1)
                            for m in range(CHUNKS):
                                if following is not None:
                                    for t in range(m * CHUNK, (m + 1) * CHUNK):
                                        gather(pre_src, src_i[1 - k][:, t:t + 1], got[1 - k][:, t, :], s_got[1 - k])
                                j = k * CHUNKS + m
                                n = i * (2 * CHUNKS) + j
                                pool.wait_ge(s_merged, n + 2)
                                pool.wait_ge(s_step, n * STEPS + STEPS)
                                pool.sem_inc(s_turn, 1)
                                for t in range(CHUNK):
                                    if not isinstance(n, int) or n:
                                        pool.wait_ge(s_tables[t], n * DMA)
                                        pool.sem_inc(s_turn, 1)
                                    scatter(bwd_sum[t], to_row[j % 2][:, t:t + 1], merged[j % 2][:, t, :], s_tables[t])
                                pool.sem_inc(s_sent, 1)

                        group(0, 0, 0)
                        group(1, 0, 1)
                        with pool.Fori(1, PAIRS) as i:
                            group(0, i, i)
                            group(1, i, i + 1)
                        group(0, PAIRS, None)
                        for t in range(CHUNK):
                            pool.wait_ge(s_tables[t], NG * CHUNKS * DMA)

                    def general():
                        pool.sem_inc(g_free, 1)
                        with pool.Fori(0, NG) as g:
                            for m in range(CHUNKS):
                                n = g * CHUNKS + m
                                pool.wait_ge(g_in, n * (7 * DMA) + 7 * DMA)
                                pool.sem_inc(s_turn, 1)
                                for t in range(CHUNK):
                                    gather(pre_src, src_i[0][:, t:t + 1], got[0][:, t, :], g_got)
                                    gather(pre_dst[0:n_nodes], dst_i[:, t:t + 1], got[1][:, t, :], g_got)
                                pool.wait_ge(g_copied, n * 2 + 2)
                                pool.sem_inc(s_turn, 1)
                                for t in range(CHUNK):
                                    for d, table in enumerate((fwd_sum, bwd_sum[0])):
                                        scatter(table, to_row[d][:, t:t + 1], merged[d][:, t, :], g_added)
                                    pool.wait_ge(g_added, n * (2 * CHUNK * DMA) + (t + 1) * (2 * DMA))
                                    pool.sem_inc(s_turn, 1)
                                pool.sem_inc(g_free, 1)

                    both_paths(pool, fast, general)

                @block.vector
                def _(dve):
                    nc.vector.memset(w2[:, :], 0.0).then_inc(s_const, 1)
                    nc.vector.memset(one_row[:, :], 1.0).then_inc(s_const, 1)

                    def chunk(k, m, i):
                        j = k * CHUNKS + m
                        n = i * (2 * CHUNKS) + j
                        q = j % 2
                        part = slice(m * CHUNK, (m + 1) * CHUNK)
                        shape = [P, CHUNK, P]
                        cols = src_c[k][:, part]
                        nc.vector.tensor_scalar(hot_t[k][0:WINDOW, part, :], local_row[k][0:WINDOW, part, :],
                                                row_id[0:WINDOW, 0:1], None, ALU.is_equal).then_inc(s_hot_t, 1)
                        dve.wait_ge(s_summed, n + 1)
                        nc.vector.tensor_tensor(hot[q][:, :, :], column[:, 0:WINDOW].unsqueeze(1).to_broadcast([P, CHUNK, WINDOW]),
                                                local[k][:, part].unsqueeze(2).to_broadcast([P, CHUNK, WINDOW]), ALU.is_equal).then_inc(s_step, 1)
                        dve.wait_ge(s_sent, n + 1)
                        merge_steps(dve, s_step, n * STEPS + 1, cols, src_row[k][:, part, :], same[q], earlier, twin, away, to_row[q])

                    def add_old(k, i):
                        dve.wait_ge(s_summed, (i * 2 + (k + 1)) * CHUNKS + 2)
                        dve.wait_ge(s_old[k], i * DMA + DMA)
                        nc.vector.tensor_tensor(new[k][:, :], p_sum[k][:, 0:D], old[k][:, :], ALU.add).then_inc(s_used[k], 1)

                    def fast():
                        for k in range(2):
                            dve.sem_inc(s_used[k], 1)
                        dve.wait_ge(s_in[0], LOADS * DMA)
                        with dve.Fori(0, PAIRS) as i:
                            for k in range(2):
                                dve.wait_ge(s_in[k], i * (LOADS * DMA) + LOADS * DMA)
                                for m in range(CHUNKS):
                                    chunk(k, m, i)
                                add_old(k, i)
                        dve.wait_ge(s_in[0], (PAIRS + 1) * LOADS * DMA)
                        for m in range(CHUNKS):
                            chunk(0, m, PAIRS)
                        add_old(0, PAIRS)

                    def general():
                        nc.vector.memset(hot_t[0][0:WINDOW, 0:CHUNK, :], 0.0).then_inc(s_hot_t, 1)
                        nc.vector.memset(w_e[0][0:WINDOW, :], 0.0).then_inc(s_hot_t, 1)
                        with dve.Fori(0, NG) as g:
                            for m in range(CHUNKS):
                                n = g * CHUNKS + m
                                dve.wait_ge(g_in, n * (7 * DMA) + 7 * DMA)
                                merge_steps(dve, g_step, n * 12, dst_c[:, :], src_row[1][:, 0:CHUNK, :], same[0], earlier, twin, away, to_row[0])
                                merge_steps(dve, g_step, n * 12 + 6, src_c[0][:, 0:CHUNK], src_row[0][:, 0:CHUNK, :], same[1], earlier, twin, away, to_row[1])
                                dve.wait_ge(g_merged, n + 1)
                                for d in range(2):
                                    nc.vector.tensor_copy(merged[d][:, :, :], p_merged[:, d * CHUNK * D:(d + 1) * CHUNK * D].rearrange(
                                        "p (t f) -> p t f", t=CHUNK)).then_inc(g_copied, 1)

                    both_paths(dve, fast, general)

                @block.scalar
                def _(act):
                    act.wait_ge(s_w, (4 + 2 * (2 + CHUNK)) * DMA)

                    def relus(n, pe_hidden, relued, pe_flow, flowed):
                        act.wait_ge(pe_hidden, n + 1)
                        for bank, (t0, t1) in enumerate(BANKS):
                            last = nc.scalar.activation(hidden[:, t0 * P:t1 * P], p_hidden[:, bank, 0:(t1 - t0) * P], ACT.Relu,
                                                        bias=b1[:, 0:1])
                        last.then_inc(relued, 1)
                        act.wait_ge(pe_flow, n + 1)
                        nc.scalar.activation(flow[:, :, :], p_flow[:, 0:CHUNK * 2 * D].rearrange("p (t f) -> p t f", t=CHUNK),
                                             ACT.Relu).then_inc(flowed, 1)

                    def chunk(k, m, i):
                        j = k * CHUNKS + m
                        n = i * (2 * CHUNKS) + j
                        relus(n, s_hidden, s_relu, s_flow, s_flowed)
                        act.wait_ge(s_summed, n + 3)
                        act.wait_ge(s_sent, n + 1)
                        nc.scalar.activation(merged[j % 2][:, :, :], p_merged[:, 0:CHUNK * D].rearrange("p (t f) -> p t f", t=CHUNK),
                                             ACT.Copy).then_inc(s_merged, 1)

                    def fast():
                        act.sem_inc(s_merged, 1)
                        with act.Fori(0, PAIRS) as i:
                            for k in range(2):
                                for m in range(CHUNKS):
                                    chunk(k, m, i)
                        for m in range(CHUNKS):
                            chunk(0, m, PAIRS)

                    def general():
                        with act.Fori(0, NG * CHUNKS) as n:
                            relus(n, g_hidden, g_relu, g_flow, g_flowed)

                    both_paths(act, fast, general)

                @block.tensor
                def _(pe):
                    pe.wait_ge(s_w, (4 + 2 * (2 + CHUNK)) * DMA)
                    pe.wait_ge(s_const, 2)

                    def mlp(n, w1, hot_t_chunk, gathered, pe_hidden, relued, pe_flow):
                        for bank, (t0, t1) in enumerate(BANKS):
                            nc.tensor.matmul(p_hidden[:, bank, 0:(t1 - t0) * P], w1[:, :], hot_t_chunk(t0, t1), start=True, stop=False)
                            for t in range(t0, t1):
                                for x_, rows in enumerate(gathered):
                                    last = nc.tensor.matmul(p_hidden[:, bank, (t - t0) * P:(t - t0 + 1) * P], rows(t), identity[:, :],
                                                            start=False, stop=t == t1 - 1 and x_ == len(gathered) - 1)
                        last.then_inc(pe_hidden, 1)
                        nc.tensor.matmul(p_flow[:, 0:CHUNK * 2 * D], one_row[:, :], b2[:, :, :].rearrange("o t f -> o (t f)"),
                                         start=True, stop=False)
                        pe.wait_ge(relued, n + 1)
                        for t in range(CHUNK):
                            last = nc.tensor.matmul(p_flow[:, t * 2 * D:(t + 1) * 2 * D], hidden[:, t * P:(t + 1) * P], w2[:, :],
                                                    start=False, stop=t == CHUNK - 1)
                        last.then_inc(pe_flow, 1)

                    def chunk(k, m, i):
                        j = k * CHUNKS + m
                        n = i * (2 * CHUNKS) + j
                        first = m * CHUNK
                        pe.wait_ge(s_hot_t, n + 1)
                        mlp(n, w_e[k], lambda t0, t1: flat(hot_t[k][:, first + t0:first + t1, :]),
                            [lambda t: got[k][:, first + t, :]], s_hidden, s_relu, s_flow)
                        pe.wait_ge(s_flowed, n + 1)
                        pe.wait_ge(s_step, n * STEPS + 2)
                        pe.wait_ge(s_merged, n + 1)
                        if m == 0:
                            pe.wait_ge(s_used[k], i + 1)
                        for t in range(CHUNK):
                            nc.tensor.matmul(p_merged[:, t * D:(t + 1) * D], same[j % 2][:, t, :], flow[:, t, D:2 * D], start=True, stop=True)
                        for t in range(CHUNK):
                            last = nc.tensor.matmul(p_sum[k][:, 0:D], hot[j % 2][:, t, :], flow[:, t, 0:D],
                                                    start=m == 0 and t == 0, stop=m == CHUNKS - 1 and t == CHUNK - 1)
                        last.then_inc(s_summed, 1)

                    def group(k, i):
                        pe.wait_ge(s_got[k], i * (TILES * DMA) + TILES * DMA)
                        pe.wait_ge(s_in[k], i * (LOADS * DMA) + LOADS * DMA)
                        for m in range(CHUNKS):
                            chunk(k, m, i)

                    def fast():
                        pe.sem_inc(s_summed, 2)
                        with pe.Fori(0, PAIRS) as i:
                            group(0, i)
                            group(1, i)
                        group(0, PAIRS)

                    def general():
                        pe.wait_ge(s_hot_t, 2)
                        with pe.Fori(0, NG * CHUNKS) as n:
                            pe.wait_ge(g_in, n * (7 * DMA) + 7 * DMA)
                            pe.wait_ge(g_got, n * (2 * CHUNK * DMA) + 2 * CHUNK * DMA)
                            mlp(n, w_e[0], lambda t0, t1: flat(hot_t[0][:, t0:t1, :]),
                                [lambda t: got[0][:, t, :], lambda t: got[1][:, t, :]], g_hidden, g_relu, g_flow)
                            pe.wait_ge(g_flowed, n + 1)
                            pe.wait_ge(g_step, n * 12 + 12)
                            for d in range(2):
                                for t in range(CHUNK):
                                    at = (d * CHUNK + t) * D
                                    last = nc.tensor.matmul(p_merged[:, at:at + D], same[d][:, t, :], flow[:, t, d * D:(d + 1) * D],
                                                            start=True, stop=True)
                            last.then_inc(g_merged, 1)

                    both_paths(pe, fast, general)

        with ExitStack() as c:
            both = sb("both", [LANES, PER, 2 * D], c=c)
            part = [sb(f"part{n}", [LANES, PER, D], c=c) for n in range(CHUNK + 1)]
            b2 = sb("b2n", [LANES, D], c=c)
            p_in, v = sem("part_in"), sem("part_v")
            with nc.Block() as block:
                @block.sync
                def _(sp):
                    for n, table in enumerate((fwd_sum, *bwd_sum)):
                        sp.dma_start(part[n][:, :, :], table[0:n_nodes].rearrange("(p j) f -> p j f", p=LANES)).then_inc(p_in, DMA)
                    sp.dma_start(b2[:, :], a["L0_gnn_b2n"].rearrange("(o f) -> o f", o=1).to_broadcast([LANES, D])).then_inc(p_in, DMA)

                @block.vector
                def _(dve):
                    dve.wait_ge(p_in, (CHUNK + 2) * DMA)
                    step = Chain(dve, v)
                    step(nc.vector.tensor_copy(both[:, :, 0:D], part[0][:, :, :]))
                    for n in range(2, CHUNK):
                        step(nc.vector.tensor_tensor(part[1][:, :, :], part[1][:, :, :], part[n][:, :, :], ALU.add))
                    step(nc.vector.tensor_tensor(both[:, :, D:2 * D], part[1][:, :, :], part[CHUNK][:, :, :], ALU.add))
            taken = part[0]
            node_mlp("mlp0", both, 2 * D, a["L0_gnn_W1n"], a["L0_gnn_b1n"], a["L0_gnn_W2n"], ACT.Relu, taken)
            t = (sb("mean1", [LANES, PER], c=c), sb("var1", [LANES, PER], c=c), part[1], part[2])
            v, ready, rooted, stored = (sem(n) for n in ("n1_v", "n1_ready", "n1_root", "n1_stored"))
            with nc.Block() as block:
                @block.vector
                def _(dve):
                    step = Chain(dve, v)
                    step(nc.vector.tensor_tensor(taken[:, :, :], taken[:, :, :],
                                                 b2[:, :].unsqueeze(1).to_broadcast([LANES, PER, D]), ALU.add))
                    step(nc.vector.tensor_scalar(taken[:, :, :], taken[:, :, :], 0.0, None, ALU.max))
                    step(nc.vector.tensor_tensor(x[:, :, :], x[:, :, :], taken[:, :, :], ALU.add))
                    layernorm(step, rooted, ready, 1, t)
                    dve.sem_inc(ready, 1)

                @block.scalar
                def _(act):
                    root(act, ready, rooted, t[1][:, :], 1)

                @block.sync
                def _(sp):
                    sp.wait_ge(ready, 2)
                    sp.dma_start(feats[0][0:n_nodes].rearrange("(p j) f -> p j f", p=LANES), h[:, :, :]).then_inc(stored, DMA)
                    sp.wait_ge(stored, DMA)

        aggregate("l1", feats[0], sums[0], widths[0], a["edge_weight"])

        def node_step(tag, constants, kept, ops, roots, total, width=D):
            with ExitStack() as c:
                summed = sb(f"{tag}_summed", [LANES, PER, width], c=c)
                t = scratch(c, tag)
                extra = {n: sb(f"{tag}_{n}", list(shape), c=c) for n, (shape, _) in constants.items()}
                s_in, v, ready, rooted, stored = (sem(f"{tag}_{n}") for n in ("sums_in", "v", "ready", "root", "stored"))
                with nc.Block() as block:
                    @block.sync
                    def _(sp):
                        sp.dma_start(summed[:, :, :], total[0:n_nodes].rearrange("(p j) f -> p j f", p=LANES)).then_inc(s_in, DMA)
                        for n, (_, ap) in constants.items():
                            sp.dma_start(extra[n][:, :], ap).then_inc(s_in, DMA)
                        if kept is not None:
                            sp.wait_ge(ready, roots + 1)
                            sp.dma_start(kept[0], kept[1][:, :, :]).then_inc(stored, DMA)
                            sp.wait_ge(stored, DMA)

                    @block.vector
                    def _(dve):
                        dve.wait_ge(s_in, (1 + len(constants)) * DMA)
                        step = Chain(dve, v)
                        ops(dve, step, summed, t, extra, ready, rooted)
                        dve.sem_inc(ready, 1)

                    @block.scalar
                    def _(act):
                        for n in range(roots):
                            root(act, ready, rooted, (t[1], t[0])[n][:, :], n + 1)

        def node_rows(table):
            return table[0:n_nodes].rearrange("(p j) f -> p j f", p=LANES)

        def spread(ap):
            return ap.rearrange("(o f) -> o f", o=1).to_broadcast([LANES, ap.shape[0]])

        def after_l1(dve, step, summed, t, extra, ready, rooted):
            step(nc.vector.tensor_tensor(x[:, :, :], x[:, :, :], summed[:, :, :], ALU.add))
            layernorm(step, rooted, ready, 1, t)

        node_step("n2", {}, (node_rows(feats[1]), h), after_l1, 1, sums[0])

        aggregate("l2", feats[1], sums[1], widths[1], None)

        def after_l2(dve, step, summed, t, extra, ready, rooted):
            eps1 = extra["eps"]
            step(nc.vector.tensor_scalar(eps1[:, :], eps1[:, :], 1.0, None, ALU.add))
            step(nc.vector.scalar_tensor_tensor(out=h[:, :, :], in0=h[:, :, :], scalar=eps1[:, 0:1], in1=summed[:, :, 0:D],
                                                op0=ALU.mult, op1=ALU.add))
            step(nc.vector.tensor_tensor(x[:, :, :], x[:, :, :], h[:, :, :], ALU.add))
            layernorm(step, rooted, ready, 1, t)
            mean = t[0]
            step(nc.vector.tensor_scalar(mean[:, :], summed[:, :, D], 1.0, None, ALU.add))
            step(nc.vector.reciprocal(inv_deg[:, :], mean[:, :]))
            dve.sem_inc(ready, 1)
            dve.wait_ge(rooted, 2)
            step(nc.vector.reciprocal(inv_sqrt[:, :], mean[:, :]))
            step(nc.vector.tensor_tensor(t[2][:, :, :], h[:, :, :], over(inv_sqrt), ALU.mult))

        with ExitStack() as keep:
            scaled = sb("scaled", [LANES, PER, D], c=keep)

            def after_l2_store(dve, step, summed, t, extra, ready, rooted):
                after_l2(dve, step, summed, t, extra, ready, rooted)
                step(nc.vector.tensor_copy(scaled[:, :, :], t[2][:, :, :]))

            node_step("n3", {"eps": ((LANES, 1), spread(a["L2_gnn_eps"]))}, (node_rows(feats[2]), scaled), after_l2_store,
                      2, sums[1], widths[1])

            aggregate("l3a", feats[2], sums[2], widths[2], None)

            def after_l3a(dve, step, summed, t, extra, ready, rooted):
                step(nc.vector.tensor_tensor(summed[:, :, :], summed[:, :, :], over(inv_sqrt), ALU.mult))
                step(nc.vector.tensor_tensor(scaled[:, :, :], h[:, :, :], over(inv_deg), ALU.mult))
                step(nc.vector.tensor_tensor(scaled[:, :, :], scaled[:, :, :], summed[:, :, :], ALU.add))

            node_step("n4", {}, None, after_l3a, 0, sums[2])
            node_mlp("mlp3", scaled, D, a["L3_gnn_W1"], a["L3_gnn_b1"], a["L3_gnn_W2"], ACT.Identity, h)
            v, stored = sem("n5_v"), sem("n5_stored")
            with nc.Block() as block:
                @block.vector
                def _(dve):
                    nc.vector.tensor_tensor(scaled[:, :, :], h[:, :, :], over(inv_sqrt), ALU.mult).then_inc(v, 1)

                @block.sync
                def _(sp):
                    sp.wait_ge(v, 1)
                    sp.dma_start(node_rows(feats[3]), scaled[:, :, :]).then_inc(stored, DMA)
                    sp.wait_ge(stored, DMA)

            aggregate("l3b", feats[3], sums[3], widths[3], None)

            def after_l3b(dve, step, summed, t, extra, ready, rooted):
                step(nc.vector.tensor_tensor(summed[:, :, :], summed[:, :, :], over(inv_sqrt), ALU.mult))
                step(nc.vector.tensor_tensor(h[:, :, :], h[:, :, :], over(inv_deg), ALU.mult))
                step(nc.vector.tensor_tensor(h[:, :, :], h[:, :, :], summed[:, :, :], ALU.add))
                step(nc.vector.tensor_tensor(h[:, :, :], h[:, :, :], extra["b2"][:, :].unsqueeze(1).to_broadcast([LANES, PER, D]), ALU.add))
                step(nc.vector.tensor_scalar(h[:, :, :], h[:, :, :], 0.0, None, ALU.max))
                step(nc.vector.tensor_tensor(x[:, :, :], x[:, :, :], h[:, :, :], ALU.add))

            node_step("n6", {"b2": ((LANES, D), spread(a["L3_gnn_b2"]))}, (out.rearrange("(p j) f -> p j f", p=LANES), x), after_l3b,
                      0, sums[3])
    return nc



def kernel(**inputs):
    import concourse.bacc as bacc
    from concourse.bass_utils import run_bass_kernel_spmd

    n_nodes, n_edges = inputs["x"].shape[0], inputs["src"].shape[0]
    groups = n_edges // GROUP
    arrays = {name: np.ascontiguousarray(value) for name, value in inputs.items()}
    for name in ("src", "dst", "edge_weight"):
        arrays[name] = arrays[name].reshape(groups, P, TILES)
    arrays["edge_attr_16"] = np.ascontiguousarray(
        arrays["edge_attr_16"].reshape(groups, P, TILES, DE).transpose(0, 3, 2, 1)).reshape(groups, DE, GROUP)
    nc = bacc.Bacc("TRN2", target_bir_lowering=False, num_devices=1)
    aps = {name: nc.dram_tensor(f"in_{name}", value.shape, mybir.dt.from_np(value.dtype), kind="ExternalInput").ap()
           for name, value in arrays.items()}
    out = nc.dram_tensor("out", (n_nodes, D), F32, kind="ExternalOutput").ap()
    build(nc, aps, out, n_nodes, n_edges)
    result = run_bass_kernel_spmd(nc, [{f"in_{name}": value for name, value in arrays.items()}], core_ids=[0])
    return result.results[0]["out"]
```

```python
from contextlib import ExitStack

import numpy as np
import concourse.bass as bass
from concourse import mybir

F32 = mybir.dt.float32
BF16 = mybir.dt.bfloat16
I32 = mybir.dt.int32
ALU = mybir.AluOpType
ACT = mybir.ActivationFunctionType
AX = mybir.AxisListType.X

P = 128
TILES = 25
GROUP = P * TILES
CHUNK = 5
CHUNKS = TILES // CHUNK
COLS = CHUNK * P
BANK = 512
D = 32
DE = 16
H = 64
WINDOW = P - DE
LANES = 125
EPS = 1e-5
SPAN = 512
SPAN_CHUNKS = 5 * CHUNKS
PARTS = 3
REC = PARTS * D + 2
WORDS = REC // 2
SPLIT = PARTS * D + 1
DMA = 16


def build(nc, a, out, n_nodes, n_edges):
    PER = n_nodes // LANES
    NG = n_edges // GROUP
    PAIRS = (NG - 1) // 2
    assert PER * LANES == n_nodes and NG * GROUP == n_edges and NG % 2 == 1 and NG <= P
    ROWS = -(-(n_nodes + SPAN) // P) * P
    FILL = ROWS // P
    NC = NG * CHUNKS
    SPANS = max(NC // SPAN_CHUNKS, 1)
    BLOCKS = -(-n_nodes // P)
    assert BLOCKS % 2 == 0 and BLOCKS * CHUNK <= BANK
    even = (NC - (SPANS - 1) * SPAN_CHUNKS) * COLS * P / n_nodes
    DEEP = int(-(-(even + 6.5 * even ** 0.5) // P))
    CAPACITY = DEEP * P
    STRIDE = CAPACITY * SPANS
    RECORDS = BLOCKS * STRIDE
    assert CAPACITY <= 256 or n_nodes < 12500
    PIECES = max(d for d in range(1, 8) if BLOCKS % d == 0)
    PIECE = BLOCKS // PIECES

    def dram(name, shape, dt=F32):
        return nc.dram_tensor(name, shape, dt).ap()

    src_rows = dram("src_rows", [NG, TILES, P])
    src_cols = dram("src_cols", [NG, P, TILES])
    local_rows = dram("local_rows", [NG, TILES, P], BF16)
    local_cols = dram("local_cols", [NG, P, TILES])
    dst_rows = dram("dst_rows", [NG, TILES, P])
    dst_cols = dram("dst_cols", [NG, P, TILES])
    bases = dram("bases", [NG, 1], I32)
    spans = dram("spans", [NG, 1])
    pre_src = dram("pre_src", [n_nodes, P])
    pre_dst = dram("pre_dst", [n_nodes + P, P])
    bin_cols = dram("bin_cols", [NG, P, TILES])
    start_cols = dram("start_cols", [NG, P, TILES])
    place_cols = dram("place_cols", [NG, P, TILES, 2])
    chunk_ends = [dram(f"chunk_{n}", [NG, CHUNKS]) for n in ("low", "high")]
    chunk_base = dram("chunk_base", [NG, CHUNKS])
    records = dram("records", [RECORDS + P, WORDS])
    HALVES = [(0, SPANS // 2), (SPANS // 2, SPANS)] if SPANS > 1 else [(0, 1)]
    counts = [dram(f"counts{lo}", [hi - lo, P, BLOCKS, SPAN], BF16) for lo, hi in HALVES]
    local_table = dram("local_table", [BLOCKS, P, DEEP * SPANS * 2])
    worst_rank = dram("worst_rank", [P, CHUNK])
    feats = [dram(f"feats{n}", [BLOCKS * P, D]) for n in range(4)]
    widths = [D, D + 1, D, D]
    sums = [dram(f"sums{n}", [ROWS, w]) for n, w in enumerate(widths)]
    fwd_sum = dram("fwd_sum", [ROWS, D])
    fwd_general = dram("fwd_general", [ROWS, D])
    bwd_sum = dram("bwd_sum", [ROWS, D])

    ctx = ExitStack()
    with ctx:
        def sb(name, shape, dt=F32, c=ctx):
            return c.enter_context(nc.sbuf_tensor(name, shape, dt))

        def sem(name, c=ctx):
            return c.enter_context(nc.semaphore(name))

        def cleared(sems):
            with nc.Block() as block:
                @block.sync
                def _(sp):
                    for s in sems:
                        sp.sem_clear(s)

        x = sb("x", [LANES, PER, D])
        h = sb("h", [LANES, PER, D])
        identity = sb("identity", [P, P])
        column = sb("column", [P, P])
        row_id = sb("row_id", [P, 1])
        before = sb("before", [P, P])
        spare = sb("spare", [P, 1])
        spare_record = sb("spare_record", [P, 1])
        column_b = sb("column_b", [P, SPAN], BF16)
        column_s = sb("column_s", [P, P], BF16)
        gather_parts = sb("gather_parts", [SPLIT, D + 1])
        behind = sb("behind", [P, P], BF16)
        ones = sb("ones", [P, P], BF16)
        ones_f = sb("ones_f", [1, P])
        span_no = sb("span_no", [P, NC])
        keep = sb("keep", [1, NC])
        span_row = sb("span_row", [1, SPANS], I32)
        worst = sb("worst", [P, CHUNK])
        base_row = sb("base_row", [1, NG], I32)
        flag = sb("flag", [1, 1], I32)
        all_fit = sb("all_fit", [1, 1], I32)
        inv_deg = sb("inv_deg", [LANES, PER])
        inv_sqrt = sb("inv_sqrt", [LANES, PER])

        class Chain:

            def __init__(self, eng, s):
                self.eng, self.s, self.n = eng, s, 0

            def __call__(self, ins):
                self.n += 1
                ins.then_inc(self.s, 1)
                self.eng.wait_ge(self.s, self.n)

        empty = sb("empty", [P, 1, STRIDE // P * REC], BF16)
        emptied = sem("emptied")
        with ExitStack() as c:
            zero = sb("zero", [P, FILL * (D + 1)], c=c)
            ints = sb("ints", [P, SPAN], I32, c=c)
            column_f = sb("column_f", [P, SPAN], c=c)
            span_i = sb("span_i", [P, NC], I32, c=c)
            z_ready, filled, made, v = (sem(n) for n in ("z_ready", "filled", "made", "const_v"))
            IOTAS = 3 + (SPANS > 1)
            with nc.Block() as block:
                @block.vector
                def _(dve):
                    dve.memset(zero[:, :], 0.0).then_inc(z_ready, 1)
                    dve.memset(empty[:, :, :], -1.0).then_inc(z_ready, 1)
                    step = Chain(dve, v)
                    step(nc.vector.memset(ones[:, :], 1.0))
                    step(nc.vector.memset(ones_f[:, :], 1.0))
                    step(nc.vector.memset(worst[:, :], 0.0))
                    step(nc.vector.memset(keep[:, :], 1.0))
                    if SPANS > 1:
                        step(nc.vector.memset(keep[:, SPAN_CHUNKS - 1:SPAN_CHUNKS * (SPANS - 1):SPAN_CHUNKS], 0.0))
                    dve.wait_ge(made, IOTAS)
                    step(nc.vector.tensor_copy(column_f[:, :], ints[:, :]))
                    step(nc.vector.tensor_scalar(column_b[:, :], column_f[:, :], -SPAN / 2, None, ALU.add))
                    step(nc.vector.tensor_copy(span_no[:, :], span_i[:, :]))
                    step(nc.vector.tensor_copy(column[:, :], ints[:, 0:P]))
                    step(nc.vector.tensor_copy(column_s[:, :], ints[:, 0:P]))
                    step(nc.vector.tensor_copy(row_id[:, :], spare.ap().bitcast(I32)))
                    step(nc.vector.tensor_scalar(before[:, :], column[:, :], row_id[:, 0:1], None, ALU.is_lt))
                    step(nc.vector.tensor_scalar(identity[:, :], column[:, :], row_id[:, 0:1], None, ALU.is_equal))
                    step(nc.vector.memset(gather_parts[:, :], 0.0))
                    for n in range(PARTS):
                        rows = slice(n * D, (n + 1) * D)
                        step(nc.vector.tensor_copy(gather_parts[rows, 0:D], identity[rows, rows]))
                    step(nc.vector.memset(gather_parts[PARTS * D:SPLIT, D:D + 1], 1.0))
                    step(nc.vector.tensor_scalar(behind[:, :], column[:, :], row_id[:, 0:1], None, ALU.is_gt))
                    step(nc.vector.tensor_scalar(spare[:, :], row_id[:, :], float(n_nodes), None, ALU.add))
                    step(nc.vector.tensor_scalar(spare_record[:, :], row_id[:, :], float(RECORDS), None, ALU.add))

                @block.gpsimd
                def _(pool):
                    head = (SPANS - 1) * SPAN_CHUNKS
                    if head:
                        nc.gpsimd.iota(span_i[:, 0:head], pattern=[[1, SPANS - 1], [0, SPAN_CHUNKS]], base=0, channel_multiplier=0).then_inc(made, 1)
                    nc.gpsimd.iota(span_i[:, head:NC], pattern=[[0, NC - head]], base=SPANS - 1, channel_multiplier=0).then_inc(made, 1)
                    nc.gpsimd.iota(ints[:, :], pattern=[[1, SPAN]], base=0, channel_multiplier=0).then_inc(made, 1)
                    nc.gpsimd.iota(spare.ap().bitcast(I32), pattern=[[1, 1]], base=0, channel_multiplier=1).then_inc(made, 1)

                @block.sync
                def _(sp):
                    sp.wait_ge(z_ready, 2)
                    tables = [(t, D) for t in (fwd_sum, fwd_general, bwd_sum)] + list(zip(sums, widths))
                    for t, w in tables:
                        sp.dma_start(t.rearrange("(p r) c -> p (r c)", p=P), zero[:, 0:FILL * w]).then_inc(filled, DMA)
                    tails = [(pre_dst[n_nodes:n_nodes + P], P)] + [(t[n_nodes:BLOCKS * P], D) for t in feats] * (BLOCKS * P > n_nodes)
                    for t, w in tails:
                        sp.dma_start(t, zero[0:t.shape[0], 0:w]).then_inc(filled, DMA)
                    sp.wait_ge(filled, DMA * (len(tables) + len(tails)))
                    sp.dma_start(records[0:RECORDS].rearrange("(p b r) c -> p b (r c)", p=P, b=BLOCKS),
                                 empty.ap().bitcast(F32).to_broadcast([P, BLOCKS, STRIDE // P * WORDS])).then_inc(emptied, DMA)

        with ExitStack() as c:
            def big(name, shape=(NG, P, TILES), dt=F32):
                return sb(name, list(shape), dt, c=c)

            src_i, dst_i = (big(n, dt=I32) for n in ("src_i", "dst_i"))
            src_f, dst_f, loc_f, bin_f = (big(n) for n in ("src_f", "dst_f", "loc_f", "bin_f"))
            bin_i = src_i
            start_f = dst_i.ap().bitcast(F32)
            src_t, dst_t = (big(n, (NG, TILES, P)) for n in ("src_t", "dst_t"))
            loc_t = big("loc_t", (NG, TILES, P), BF16)
            place = sb("place", [NG, P, TILES, 2], c=c)
            low, high = (sb(n, [NG, 1], c=c) for n in ("low", "high"))
            low_i = sb("low_i", [NG, 1], I32, c=c)
            chunk_low, chunk_high, base_c = (sb(n, [NG, CHUNKS], c=c) for n in ("least", "greatest", "base_c"))
            low_row, high_row, base_f = (sb(n, [1, NC], c=c) for n in ("low_row", "high_row", "base_f"))
            span_low, span_high = (sb(n, [1, SPANS], c=c) for n in ("span_low", "span_high"))
            extent = sb("extent", [1, NG], c=c)
            widest, widest_span = (sb(n, [1, 1], c=c) for n in ("widest", "widest_span"))
            loaded, v, stored, back, spanned, based = (
                sem(n) for n in ("idx_loaded", "idx_v", "idx_stored", "idx_back", "idx_spanned", "idx_based"))
            HEAD = (SPANS - 1) * SPAN_CHUNKS
            with nc.Block() as block:
                @block.sync
                def _(sp):
                    sp.dma_start(dst_i[:, :, :], a["dst"]).then_inc(loaded, DMA)
                    sp.dma_start(src_i[:, :, :], a["src"]).then_inc(loaded, DMA)
                    sp.dma_start(x[:, :, :], a["x"].rearrange("(p j) f -> p j f", p=LANES)).then_inc(loaded, DMA)
                    sp.wait_ge(v, 4)
                    for table, tile in zip(chunk_ends, (chunk_low, chunk_high)):
                        sp.dma_start(table, tile[:, :]).then_inc(stored, DMA)
                    sp.wait_ge(stored, 2 * DMA)
                    for table, row in zip(chunk_ends, (low_row, high_row)):
                        sp.dma_start(row[:, :], table.rearrange("g c -> (g c)").rearrange("(o n) -> o n", o=1)).then_inc(back, DMA)
                    sp.wait_ge(spanned, 1)
                    sp.dma_start(chunk_base.rearrange("g c -> (g c)").rearrange("(o n) -> o n", o=1), base_f[:, :]).then_inc(based, DMA)
                    sp.wait_ge(based, DMA)
                    sp.dma_start(base_c[:, :], chunk_base).then_inc(based, DMA)
                    sp.wait_ge(spanned, 2)
                    pairs = [(src_cols, src_f), (src_rows, src_t), (dst_cols, dst_f), (dst_rows, dst_t),
                             (local_cols, loc_f), (local_rows, loc_t), (bin_cols, bin_f), (start_cols, start_f)]
                    for table, tile in pairs:
                        sp.dma_start(table, tile[:, :, :]).then_inc(stored, DMA)
                    sp.dma_start(place_cols.rearrange("g p t w -> g (p t w)"), place[:, :, :, :].rearrange("g p t w -> g (p t w)")).then_inc(stored, DMA)
                    sp.dma_start(bases, low_i[:, :]).then_inc(stored, DMA)
                    sp.dma_start(spans, high[:, :]).then_inc(stored, DMA)
                    sp.wait_ge(stored, DMA * (len(pairs) + 5))
                    sp.dma_start(base_row[:, :], bases.rearrange("g o -> o g")).then_inc(back, DMA)
                    sp.dma_start(extent[:, :], spans.rearrange("g o -> o g")).then_inc(back, DMA)
                    sp.wait_ge(back, 4 * DMA)

                @block.vector
                def _(dve):
                    step = Chain(dve, v)
                    dve.wait_ge(loaded, 3 * DMA)
                    step(nc.vector.tensor_copy(dst_f[:, :, :], dst_i[:, :, :]))
                    step(nc.vector.tensor_copy(dst_t[:, :, :], dst_f[:, :, :].rearrange("g p t -> g t p")))
                    by_chunk = dst_t[:, :, :].rearrange("g (c k) p -> g c (k p)", c=CHUNKS)
                    step(nc.vector.tensor_reduce(chunk_low[:, :], by_chunk, AX, ALU.min))
                    step(nc.vector.tensor_reduce(chunk_high[:, :], by_chunk, AX, ALU.max))
                    step(nc.vector.tensor_copy(src_f[:, :, :], src_i[:, :, :]))
                    step(nc.vector.tensor_copy(src_t[:, :, :], src_f[:, :, :].rearrange("g p t -> g t p")))
                    step(nc.vector.tensor_reduce(low[:, :], chunk_low[:, :], AX, ALU.min))
                    step(nc.vector.tensor_reduce(high[:, :], chunk_high[:, :], AX, ALU.max))
                    step(nc.vector.tensor_scalar(loc_f[:, :, :], dst_f[:, :, :], low[:, 0:1], None, ALU.subtract))
                    step(nc.vector.tensor_copy(loc_t[:, :, :], loc_f[:, :, :].rearrange("g p t -> g t p")))
                    step(nc.vector.tensor_copy(low_i[:, :], low[:, :]))
                    step(nc.vector.tensor_scalar(high[:, :], high[:, :], low[:, 0:1], None, ALU.subtract))
                    dve.wait_ge(back, 2 * DMA)
                    for row, out_, op in ((low_row, span_low, ALU.min), (high_row, span_high, ALU.max)):
                        if HEAD:
                            step(nc.vector.tensor_reduce(out_[:, 0:SPANS - 1], row[:, 0:HEAD].rearrange("o (s c) -> o s c", s=SPANS - 1), AX, op))
                        step(nc.vector.tensor_reduce(out_[:, SPANS - 1:SPANS], row[:, HEAD:NC], AX, op))
                    if HEAD:
                        step(nc.vector.tensor_copy(base_f[:, 0:HEAD].rearrange("o (s c) -> o s c", s=SPANS - 1),
                                                   span_low[:, 0:SPANS - 1].unsqueeze(2).to_broadcast([1, SPANS - 1, SPAN_CHUNKS])))
                    step(nc.vector.tensor_copy(base_f[:, HEAD:NC], span_low[:, SPANS - 1:SPANS].to_broadcast([1, NC - HEAD])))
                    dve.sem_inc(spanned, 1)
                    step(nc.vector.tensor_copy(span_row[:, :], span_low[:, :]))
                    step(nc.vector.tensor_tensor(span_high[:, :], span_high[:, :], span_low[:, :], ALU.subtract))
                    step(nc.vector.tensor_reduce(widest_span[:, :], span_high[:, :], AX, ALU.max))
                    step(nc.vector.tensor_scalar(widest_span[:, :], widest_span[:, :], float(SPAN), None, ALU.is_lt))
                    step(nc.vector.tensor_single_scalar(bin_i[:, :, :], src_i[:, :, :], P.bit_length() - 1, ALU.arith_shift_right))
                    step(nc.vector.tensor_copy(bin_f[:, :, :], bin_i[:, :, :]))
                    step(nc.vector.tensor_scalar(start_f[:, :, :], bin_f[:, :, :], float(STRIDE), None, ALU.mult))
                    step(nc.vector.scalar_tensor_tensor(out=place[:, :, :, 0], in0=bin_f[:, :, :], scalar=-float(P), in1=src_f[:, :, :],
                                                        op0=ALU.mult, op1=ALU.add))
                    dve.wait_ge(based, 2 * DMA)
                    for m in range(CHUNKS):
                        part = slice(m * CHUNK, (m + 1) * CHUNK)
                        step(nc.vector.tensor_scalar(place[:, :, part, 1], dst_f[:, :, part], base_c[:, m:m + 1], -SPAN / 2, ALU.subtract, ALU.add))
                    dve.sem_inc(spanned, 1)
                    dve.wait_ge(back, 4 * DMA)
                    step(nc.vector.tensor_reduce(widest[:, :], extent[:, :], AX, ALU.max))
                    step(nc.vector.tensor_scalar(widest[:, :], widest[:, :], float(WINDOW), None, ALU.is_lt))
                    step(nc.vector.tensor_tensor(widest[:, :], widest[:, :], widest_span[:, :], ALU.mult))
                    step(nc.vector.tensor_copy(flag[:, :], widest[:, :]))

        def over(ap):
            return ap[:, :].unsqueeze(2).to_broadcast([LANES, PER, D])

        def layernorm(step, act_done, dve_ready, n, t):
            mean, var, xc, sq = t
            step(nc.vector.tensor_reduce(mean[:, :], x[:, :, :], AX, ALU.add))
            step(nc.vector.tensor_scalar(mean[:, :], mean[:, :], 1.0 / D, None, ALU.mult))
            step(nc.vector.tensor_tensor(xc[:, :, :], x[:, :, :], over(mean), ALU.subtract))
            step(nc.vector.tensor_tensor(sq[:, :, :], xc[:, :, :], xc[:, :, :], ALU.mult))
            step(nc.vector.tensor_reduce(var[:, :], sq[:, :, :], AX, ALU.add))
            step(nc.vector.tensor_scalar(var[:, :], var[:, :], 1.0 / D, EPS, ALU.mult, ALU.add))
            step.eng.sem_inc(dve_ready, 1)
            step.eng.wait_ge(act_done, n)
            step(nc.vector.reciprocal(var[:, :], var[:, :]))
            step(nc.vector.tensor_tensor(xc[:, :, :], xc[:, :, :], over(var), ALU.mult))
            step(nc.vector.tensor_scalar(h[:, :, :], xc[:, :, :], 0.0, None, ALU.max))

        def root(act, dve_ready, act_done, ap, n):
            act.wait_ge(dve_ready, n)
            nc.scalar.activation(ap, ap, ACT.Sqrt).then_inc(act_done, 1)

        def scratch(c, tag):
            return (sb(f"mean{tag}", [LANES, PER], c=c), sb(f"var{tag}", [LANES, PER], c=c),
                    sb(f"xc{tag}", [LANES, PER, D], c=c), sb(f"sq{tag}", [LANES, PER, D], c=c))

        QUAD = 4
        TURNS = PER // QUAD
        assert TURNS * QUAD == PER

        with ExitStack() as c:
            t = scratch(c, "0")
            w_pre = sb("w_pre", [D, 2 * P], c=c)
            cols = sb("cols0", [LANES, QUAD, D], c=c)
            feat = sb("feat0", [D, QUAD * LANES], c=c)
            rows = sb("rows0", [LANES, QUAD, 2 * P], c=c)
            p_t = c.enter_context(nc.psum_tensor("p_t0", [D, BANK], F32))
            p_o = c.enter_context(nc.psum_tensor("p_o0", [LANES, QUAD, 2 * P], F32))
            names = ("n0_w", "n0_v", "n0_ready", "n0_root", "n0_cols", "n0_turned", "n0_feat", "n0_product", "n0_rows", "n0_stored")
            w_in, v, ready, rooted, s_cols, s_tr, s_feat, s_mm, s_out, s_st = (sem(n) for n in names)
            with nc.Block() as block:
                @block.sync
                def _(sp):
                    w1f, w1b = a["L0_gnn_W1f"], a["L0_gnn_W1b"]
                    for n, part in enumerate((w1f[D:2 * D], w1b[0:D], w1f[0:D], w1b[D:2 * D])):
                        sp.dma_start(w_pre[:, n * H:(n + 1) * H], part).then_inc(w_in, DMA)
                    with sp.Fori(0, TURNS) as i:
                        sp.wait_ge(s_out, i * 2 + 2)
                        for n, table in enumerate((pre_src, pre_dst)):
                            sp.dma_start(table[0:n_nodes].rearrange("(p j) f -> p j f", p=LANES)[:, bass.ds(i * QUAD, QUAD)],
                                         rows[:, :, n * P:(n + 1) * P]).then_inc(s_st, DMA)
                    sp.wait_ge(s_st, 2 * DMA * TURNS)

                @block.vector
                def _(dve):
                    step = Chain(dve, v)
                    layernorm(step, rooted, ready, 1, t)
                    with dve.Fori(0, TURNS) as i:
                        nc.vector.tensor_copy(cols[:, :, :], h[:, bass.ds(i * QUAD, QUAD), :]).then_inc(s_cols, 1)
                        dve.wait_ge(s_tr, i + 1)
                        nc.vector.tensor_copy(feat[:, :], p_t[:, 0:QUAD * LANES]).then_inc(s_feat, 1)
                        dve.wait_ge(s_mm, i + 1)
                        nc.vector.tensor_copy(rows[:, 0:2, :], p_o[:, 0:2, :]).then_inc(s_out, 1)
                        dve.wait_ge(s_st, i * (2 * DMA) + 2 * DMA)

                @block.scalar
                def _(act):
                    root(act, ready, rooted, t[1][:, :], 1)
                    with act.Fori(0, TURNS) as i:
                        act.wait_ge(s_mm, i + 1)
                        nc.scalar.activation(rows[:, 2:4, :], p_o[:, 2:4, :], ACT.Copy).then_inc(s_out, 1)
                        act.wait_ge(s_st, i * (2 * DMA) + 2 * DMA)

                @block.tensor
                def _(pe):
                    pe.wait_ge(w_in, 4 * DMA)
                    with pe.Fori(0, TURNS) as i:
                        pe.wait_ge(s_cols, i + 1)
                        for q in range(QUAD):
                            last = nc.tensor.transpose(p_t[:, q * LANES:(q + 1) * LANES], cols[:, q, :], identity[0:LANES, 0:LANES])
                        last.then_inc(s_tr, 1)
                        pe.wait_ge(s_feat, i + 1)
                        for q in range(QUAD):
                            last = nc.tensor.matmul(p_o[:, q, :], feat[:, q * LANES:(q + 1) * LANES], w_pre[:, :],
                                                    start=True, stop=True)
                        last.then_inc(s_mm, 1)

        def node_mlp(tag, given, k, w1, b1, w2, fn, taken):
            with ExitStack() as c:
                w1_s = sb(f"w1_{tag}", [k, H], c=c)
                w2_s = sb(f"w2_{tag}", [H, D], c=c)
                b1_s = sb(f"b1_{tag}", [H, 1], c=c)
                cols = sb(f"cols_{tag}", [LANES, QUAD, k], c=c)
                feat = sb(f"feat_{tag}", [k, QUAD * LANES], c=c)
                hid = sb(f"hid_{tag}", [H, QUAD * LANES], c=c)
                p_t = c.enter_context(nc.psum_tensor(f"p_t_{tag}", [k, BANK], F32))
                p_h = c.enter_context(nc.psum_tensor(f"p_h_{tag}", [H, BANK], F32))
                p_o = c.enter_context(nc.psum_tensor(f"p_o_{tag}", [LANES, BANK], F32))
                names = ("weights", "cols", "turned", "feat", "hidden", "activated", "product", "taken", "turn")
                w_in, s_cols, s_tr, s_feat, s_hid, s_act, s_mm, s_out, s_turn = (sem(f"{tag}_{n}") for n in names)
                with nc.Block() as block:
                    @block.sync
                    def _(sp):
                        sp.dma_start(w1_s[:, :], w1).then_inc(w_in, DMA)
                        sp.dma_start(w2_s[:, :], w2).then_inc(w_in, DMA)
                        sp.dma_start(b1_s[:, :], b1.rearrange("(h o) -> h o", o=1)).then_inc(w_in, DMA)

                    @block.vector
                    def _(dve):
                        with dve.Fori(0, TURNS) as i:
                            nc.vector.tensor_copy(cols[:, :, :], given[:, bass.ds(i * QUAD, QUAD), :]).then_inc(s_cols, 1)
                            dve.wait_ge(s_tr, i + 1)
                            nc.vector.tensor_copy(feat[:, :], p_t[:, 0:QUAD * LANES]).then_inc(s_feat, 1)
                            dve.wait_ge(s_mm, i + 1)
                            nc.vector.tensor_copy(taken[:, bass.ds(i * QUAD, QUAD), :],
                                                  p_o[:, 0:QUAD * D].rearrange("p (q f) -> p q f", q=QUAD)).then_inc(s_out, 1)

                    @block.scalar
                    def _(act):
                        act.wait_ge(w_in, 3 * DMA)
                        with act.Fori(0, TURNS) as i:
                            act.wait_ge(s_hid, i + 1)
                            nc.scalar.activation(hid[:, :], p_h[:, 0:QUAD * LANES], fn, bias=b1_s[:, 0:1]).then_inc(s_act, 1)

                    @block.tensor
                    def _(pe):
                        pe.wait_ge(w_in, 3 * DMA)
                        with pe.Fori(0, TURNS) as i:
                            pe.wait_ge(s_cols, i + 1)
                            pe.sem_inc(s_turn, 1)
                            for q in range(QUAD):
                                last = nc.tensor.transpose(p_t[:, q * LANES:(q + 1) * LANES], cols[:, q, :], identity[0:LANES, 0:LANES])
                            last.then_inc(s_tr, 1)
                            pe.wait_ge(s_feat, i + 1)
                            pe.sem_inc(s_turn, 1)
                            nc.tensor.matmul(p_h[:, 0:QUAD * LANES], w1_s[:, :], feat[:, :], start=True, stop=True).then_inc(s_hid, 1)
                            pe.wait_ge(s_act, i + 1)
                            for q in range(QUAD):
                                last = nc.tensor.matmul(p_o[:, q * D:(q + 1) * D], hid[:, q * LANES:(q + 1) * LANES], w2_s[:, :],
                                                        start=True, stop=True)
                            last.then_inc(s_mm, 1)

        def window_rows(sp, table, base):
            return table[bass.ds(base, WINDOW)]

        def fetch_base(eng, g):
            at = base_row[0:1, g:g + 1] if isinstance(g, int) else base_row[0:1, bass.ds(g, 1)]
            return eng.value_load(at, min_val=0, max_val=n_nodes - 1)

        def at_group(table, g):
            return table[g] if isinstance(g, int) else table[bass.ds(g, 1)].rearrange("o p t -> (o p) t")

        def row_group(table, g, first=0, count=TILES):
            flat = table.rearrange("g t p -> g (t p)")
            one = flat[g:g + 1] if isinstance(g, int) else flat[bass.ds(g, 1)]
            return one[:, first * P:(first + count) * P].to_broadcast([P, count * P])

        def both_paths(eng, which, fast, general):
            fits = eng.value_load(which[0:1, 0:1], min_val=0, max_val=1)
            with eng.If(fits > 0):
                fast()
            with eng.Else():
                general()

        def merge_steps(dve, s, count, cols, row, same, earlier, twin, away, to_row, rest=6):
            def add(ins, n):
                ins.then_inc(s, 1)
                dve.wait_ge(s, count + n)
            shape = [P, CHUNK, P]
            add(nc.vector.tensor_tensor(same[:, :, :], row[:, :, :], cols.unsqueeze(2).to_broadcast(shape), ALU.is_equal), 1)
            add(nc.vector.tensor_tensor(earlier[:, :, :], same[:, :, :], before[:, :].unsqueeze(1).to_broadcast(shape), ALU.mult), 2)
            add(nc.vector.tensor_reduce(twin[:, :], earlier[:, :, :], AX, ALU.add), 3)
            add(nc.vector.tensor_scalar(away[:, :], cols, -1.0, spare[:, 0:1], ALU.mult, ALU.add), 4)
            add(nc.vector.scalar_tensor_tensor(out=away[:, :], in0=twin[:, :], scalar=0.0, in1=away[:, :], op0=ALU.is_gt, op1=ALU.mult), 5)
            add(nc.vector.tensor_tensor(to_row[:, :], away[:, :], cols, ALU.add), 6)

        def general_sum(c, tag, table, total, width, weights):
            src_i = sb(f"{tag}_g_src", [P, CHUNK], I32, c=c)
            cols = sb(f"{tag}_g_cols", [P, CHUNK], c=c)
            wgt = sb(f"{tag}_g_wgt", [P, CHUNK], c=c)
            got = sb(f"{tag}_g_got", [P, CHUNK, D + 1], c=c)
            same_row = sb(f"{tag}_g_same_row", [P, CHUNK, P], c=c)
            same = sb(f"{tag}_g_same", [P, CHUNK, P], c=c)
            earlier = sb(f"{tag}_g_earlier", [P, CHUNK, P], c=c)
            twin = sb(f"{tag}_g_twin", [P, CHUNK], c=c)
            away = sb(f"{tag}_g_away", [P, CHUNK], c=c)
            to_row = sb(f"{tag}_g_to_row", [P, CHUNK], I32, c=c)
            merged = sb(f"{tag}_g_merged", [P, CHUNK, width], c=c)
            p_merged = c.enter_context(nc.psum_tensor(f"{tag}_g_p", [P, BANK], F32))
            g_got, g_added = sem(f"{tag}_g_got"), sem(f"{tag}_g_added")
            g_in, g_step, g_merged, g_copied, g_free, g_turn = stage = [
                sem(f"{tag}_g_{n}", c) for n in ("in", "step", "merged", "copied", "free", "turn")]
            loads = 4 if weights is not None else 3
            steps = 8 if weights is not None else 7

            def sync(sp):
                with sp.Fori(0, NG) as g:
                    for m in range(CHUNKS):
                        part = slice(m * CHUNK, (m + 1) * CHUNK)
                        sp.wait_ge(g_free, g * CHUNKS + (m + 1))
                        sp.dma_start(src_i[:, :], at_group(a["src"], g)[:, part]).then_inc(g_in, DMA)
                        sp.dma_start(cols[:, :], at_group(dst_cols, g)[:, part]).then_inc(g_in, DMA)
                        sp.dma_start(flat(same_row[:, :, :]), row_group(dst_rows, g, m * CHUNK, CHUNK)).then_inc(g_in, DMA)
                        if weights is not None:
                            sp.dma_start(wgt[:, :], at_group(weights, g)[:, part]).then_inc(g_in, DMA)

            def gpsimd(pool):
                pool.sem_inc(g_free, 1)
                with pool.Fori(0, NG) as g:
                    for m in range(CHUNKS):
                        n = g * CHUNKS + m
                        pool.wait_ge(g_in, n * (loads * DMA) + loads * DMA)
                        pool.sem_inc(g_turn, 1)
                        for t in range(CHUNK):
                            nc.gpsimd.indirect_dma_start(
                                out=got[:, t, 0:D], out_offset=None, in_=table,
                                in_offset=bass.IndirectOffsetOnAxis(ap=src_i[:, t:t + 1], axis=0)).then_inc(g_got, DMA)
                        pool.wait_ge(g_copied, n + 1)
                        pool.sem_inc(g_turn, 1)
                        for t in range(CHUNK):
                            nc.gpsimd.indirect_dma_start(
                                out=total, out_offset=bass.IndirectOffsetOnAxis(ap=to_row[:, t:t + 1], axis=0),
                                in_=merged[:, t, :], in_offset=None, compute_op=ALU.add).then_inc(g_added, DMA)
                            pool.wait_ge(g_added, n * (CHUNK * DMA) + (t + 1) * DMA)
                            pool.sem_inc(g_turn, 1)
                        pool.sem_inc(g_free, 1)

            def vector(dve):
                with dve.Fori(0, NG) as g:
                    for m in range(CHUNKS):
                        n = g * CHUNKS + m
                        dve.wait_ge(g_in, n * (loads * DMA) + loads * DMA)
                        nc.vector.memset(got[:, :, D:D + 1], 1.0).then_inc(g_step, 1)
                        merge_steps(dve, g_step, n * steps + 1, cols[:, :], same_row, same, earlier, twin, away, to_row)
                        if weights is not None:
                            dve.wait_ge(g_got, n * (CHUNK * DMA) + CHUNK * DMA)
                            nc.vector.tensor_tensor(got[:, :, 0:D], got[:, :, 0:D],
                                                    wgt[:, :].unsqueeze(2).to_broadcast([P, CHUNK, D]), ALU.mult).then_inc(g_step, 1)
                        dve.wait_ge(g_merged, n + 1)
                        nc.vector.tensor_copy(merged[:, :, :], p_merged[:, 0:CHUNK * width].rearrange(
                            "p (t w) -> p t w", t=CHUNK)).then_inc(g_copied, 1)

            def tensor(pe):
                with pe.Fori(0, NC) as n:
                    pe.wait_ge(g_got, n * (CHUNK * DMA) + CHUNK * DMA)
                    pe.wait_ge(g_step, n * steps + steps)
                    for t in range(CHUNK):
                        last = nc.tensor.matmul(p_merged[:, t * width:(t + 1) * width], same[:, t, :],
                                                got[:, t, 0:width], start=True, stop=True)
                    last.then_inc(g_merged, 1)

            def scalar(act):
                act.sem_inc(g_turn, 1)

            return sync, gpsimd, vector, tensor, scalar, stage

        def weighted_sum(tag, table, total, weights):
            with ExitStack() as c:
                LOADS = 3
                src_i = [sb(f"{tag}_src{k}", [P, TILES], I32, c=c) for k in range(2)]
                local = [sb(f"{tag}_local{k}", [P, TILES], c=c) for k in range(2)]
                wgt = [sb(f"{tag}_wgt{k}", [P, TILES], c=c) for k in range(2)]
                got = [sb(f"{tag}_got{k}", [P, TILES, D], c=c) for k in range(2)]
                hot = [sb(f"{tag}_hot{k}", [P, TILES, WINDOW], c=c) for k in range(2)]
                old = [sb(f"{tag}_old{k}", [WINDOW, D], c=c) for k in range(2)]
                new = [sb(f"{tag}_new{k}", [WINDOW, D], c=c) for k in range(2)]
                p_sum = [c.enter_context(nc.psum_tensor(f"{tag}_p{k}", [WINDOW, BANK], F32)) for k in range(2)]
                s_got = [sem(f"{tag}_got{k}") for k in range(2)]
                s_in, s_hot, s_summed, s_used, s_old = ([sem(f"{tag}_{n}{k}", c) for k in range(2)]
                                                       for n in ("in", "hot", "summed", "used", "old"))
                s_stored, s_turn = sem(f"{tag}_stored", c), sem(f"{tag}_turn", c)
                BIN = DEEP * SPANS
                RING = 5 if SPANS % 5 == 0 else 2
                place = [sb(f"{tag}_place{k}", [P, DEEP, SPANS, 2], c=c) for k in range(2)]
                place_b = [sb(f"{tag}_place_b{k}", [P, DEEP, SPANS, 2], BF16, c=c) for k in range(2)]
                from_hot = [sb(f"{tag}_from_hot{k}", [P, DEEP, SPANS, P], BF16, c=c) for k in range(2)]
                to_hot = [sb(f"{tag}_to_hot{r}", [P, DEEP, SPAN], BF16, c=c) for r in range(RING)]
                counted = [sb(f"{tag}_counted{k}", [P, SPANS, SPAN], BF16, c=c) for k in range(2)]
                p_count = [c.enter_context(nc.psum_tensor(f"{tag}_p_count{r}", [P, BANK], F32)) for r in range(RING)]
                s_place, s_kept = ([sem(f"{tag}_{n}{k}", c) for k in range(2)] for n in ("place", "kept"))
                s_from, s_to, s_count, s_copied = (sem(f"{tag}_{n}", c) for n in ("from", "to", "count", "copied"))
                g_sync, g_gpsimd, g_vector, g_tensor, g_scalar, g_stage = general_sum(c, tag, table, total, D, weights)
                half = BLOCKS // 2
                assert half <= PAIRS or n_nodes < 12500
                KEPT = len(HALVES) * DMA
                BOTH = min(half, PAIRS)

                with nc.Block() as block:
                    @block.sync
                    def _(sp):
                        def load(k, g, i):
                            sp.wait_ge(s_summed[k], i + 1)
                            sp.dma_start(src_i[k][:, :], at_group(a["src"], g)).then_inc(s_in[k], DMA)
                            sp.dma_start(local[k][:, :], at_group(local_cols, g)).then_inc(s_in[k], DMA)
                            sp.dma_start(wgt[k][:, :], at_group(weights, g)).then_inc(s_in[k], DMA)

                        def add_window(k, g, i):
                            base = fetch_base(sp, g)
                            rows = window_rows(sp, total, base)
                            sp.dma_start(old[k][:, :], rows).then_inc(s_old[k], DMA)
                            sp.wait_ge(s_used[k], i + 2)
                            sp.dma_start(rows, new[k][:, :]).then_inc(s_stored, DMA)
                            sp.wait_ge(s_stored, (g + 1) * DMA)
                            sp.sem_inc(s_turn, 1)

                        def load_block(k, b, turn):
                            sp.wait_ge(s_to, (turn + 1) * SPANS)
                            table = local_table[b] if isinstance(b, int) else local_table[bass.ds(b % BLOCKS, 1)].rearrange("o p n -> (o p) n")
                            sp.dma_start(place[k][:, :, :, :].rearrange("p d s w -> p (d s w)"), table).then_inc(s_place[k], DMA)

                        def fast():
                            load(0, 0, 0)
                            load_block(0, 0, 0)
                            with sp.Fori(0, BOTH) as i:
                                for k in range(2):
                                    load(1 - k, i * 2 + (k + 1), i + k)
                                    load_block(1 - k, i * 2 + (k + 1), i * 2 + (k + 1))
                                    add_window(k, i * 2 + k, i)
                            if BOTH < half:
                                with sp.Fori(BOTH, half) as i:
                                    for k in range(2):
                                        load_block(1 - k, i * 2 + (k + 1), i * 2 + (k + 1))
                            if BOTH < PAIRS:
                                with sp.Fori(BOTH, PAIRS) as i:
                                    for k in range(2):
                                        load(1 - k, i * 2 + (k + 1), i + k)
                                        add_window(k, i * 2 + k, i)
                            add_window(0, NG - 1, PAIRS)
                            sp.wait_ge(s_place[0], (half + 1) * DMA)

                        both_paths(sp, all_fit, fast, lambda: g_sync(sp))

                    @block.gpsimd
                    def _(pool):
                        def gather(k, i):
                            pool.wait_ge(s_in[k], i * (LOADS * DMA) + LOADS * DMA)
                            pool.sem_inc(s_turn, 1)
                            for t in range(TILES):
                                nc.gpsimd.indirect_dma_start(
                                    out=got[k][:, t, :], out_offset=None, in_=table,
                                    in_offset=bass.IndirectOffsetOnAxis(ap=src_i[k][:, t:t + 1], axis=0)).then_inc(s_got[k], DMA)

                        def fast():
                            with pool.Fori(0, PAIRS) as i:
                                gather(0, i)
                                gather(1, i)
                            gather(0, PAIRS)

                        both_paths(pool, all_fit, fast, lambda: g_gpsimd(pool))

                    @block.vector
                    def _(dve):
                        def one_hot(k, i):
                            dve.wait_ge(s_in[k], i * (LOADS * DMA) + LOADS * DMA)
                            nc.vector.tensor_tensor(
                                hot[k][:, :, :], column[:, 0:WINDOW].unsqueeze(1).to_broadcast([P, TILES, WINDOW]),
                                local[k][:, :].unsqueeze(2).to_broadcast([P, TILES, WINDOW]), ALU.is_equal).then_inc(s_hot[k], 1)

                        def weigh(k, i):
                            dve.wait_ge(s_got[k], i * (TILES * DMA) + TILES * DMA)
                            nc.vector.tensor_tensor(got[k][:, :, :], got[k][:, :, :],
                                                    wgt[k][:, :].unsqueeze(2).to_broadcast([P, TILES, D]), ALU.mult).then_inc(s_hot[k], 1)

                        def add_old(k, i):
                            dve.wait_ge(s_summed[k], i + 2)
                            dve.wait_ge(s_old[k], i * DMA + DMA)
                            nc.vector.tensor_tensor(new[k][:, :], p_sum[k][:, 0:D], old[k][:, :], ALU.add).then_inc(s_used[k], 1)

                        def one_hot_block(k, b, turn):
                            dve.wait_ge(s_place[k], turn * DMA + DMA)
                            dve.wait_ge(s_count, b * SPANS + RING)
                            nc.vector.tensor_copy(place_b[k][:, :, :, :], place[k][:, :, :, :]).then_inc(s_from, 1)
                            dve.wait_ge(s_from, b * 2 + 1)
                            nc.vector.tensor_tensor(
                                from_hot[k][:, :, :, :].rearrange("p d s e -> p (d s) e"), column_s[:, :].unsqueeze(1).to_broadcast([P, BIN, P]),
                                place_b[k][:, :, :, 0:1].rearrange("p d s o -> p (d s) o").to_broadcast([P, BIN, P]), ALU.is_equal).then_inc(s_from, 1)
                            for s in range(SPANS):
                                dve.wait_ge(s_count, b * SPANS + (s + 1))
                                for d in range(DEEP):
                                    last = nc.vector.tensor_scalar(to_hot[(k * SPANS + s) % RING][:, d, :], column_b[:, :],
                                                                   place[k][:, d, s, 1:2], None, ALU.is_equal)
                                last.then_inc(s_to, 1)

                        def fast():
                            dve.sem_inc(s_to, 2 * SPANS)
                            for k in range(2):
                                dve.sem_inc(s_used[k], 1)
                            one_hot(0, 0)
                            with dve.Fori(0, BOTH) as i:
                                for k in range(2):
                                    weigh(k, i)
                                    one_hot(1 - k, i + k)
                                    one_hot_block(k, i * 2 + k, i)
                                    add_old(k, i)
                            if BOTH < half:
                                with dve.Fori(BOTH, half) as i:
                                    for k in range(2):
                                        one_hot_block(k, i * 2 + k, i)
                            if BOTH < PAIRS:
                                with dve.Fori(BOTH, PAIRS) as i:
                                    for k in range(2):
                                        weigh(k, i)
                                        one_hot(1 - k, i + k)
                                        add_old(k, i)
                            weigh(0, PAIRS)
                            add_old(0, PAIRS)

                        both_paths(dve, all_fit, fast, lambda: g_vector(dve))

                    @block.scalar
                    def _(act):
                        def copy_block(k, b, turn):
                            act.wait_ge(s_kept[k], turn * KEPT + KEPT)
                            for s in range(SPANS):
                                act.wait_ge(s_count, b * SPANS + (s + 1 + RING))
                                nc.scalar.activation(counted[k][:, s, :], p_count[(k * SPANS + s) % RING][:, :], ACT.Copy).then_inc(s_copied, 1)
                            act.wait_ge(s_copied, b * SPANS + (SPANS + RING))
                            for table, (lo, hi) in zip(counts, HALVES):
                                act.dma_start(table[:, :, bass.ds(b, 1), :].rearrange("s p o n -> p (s o) n"), counted[k][:, lo:hi, :]).then_inc(s_kept[k], DMA)

                        def fast():
                            act.sem_inc(s_copied, RING)
                            for k in range(2):
                                act.sem_inc(s_kept[k], KEPT)
                            with act.Fori(0, half) as i:
                                for k in range(2):
                                    copy_block(k, i * 2 + k, i)
                            for k in range(2):
                                act.wait_ge(s_kept[k], (half + 1) * KEPT)

                        both_paths(act, all_fit, fast, lambda: g_scalar(act))

                    @block.tensor
                    def _(pe):
                        def sum_group(k, i):
                            pe.wait_ge(s_got[k], i * (TILES * DMA) + TILES * DMA)
                            pe.wait_ge(s_hot[k], i * 2 + 2)
                            pe.wait_ge(s_used[k], i + 1)
                            for t in range(TILES):
                                last = nc.tensor.matmul(p_sum[k][:, 0:D], hot[k][:, t, :], got[k][:, t, :],
                                                        start=t == 0, stop=t == TILES - 1)
                            last.then_inc(s_summed[k], 1)

                        def count_block(k, b):
                            pe.wait_ge(s_from, b * 2 + 2)
                            for s in range(SPANS):
                                r = (k * SPANS + s) % RING
                                pe.wait_ge(s_to, b * SPANS + (s + 1 + 2 * SPANS))
                                pe.wait_ge(s_copied, b * SPANS + (s + 1))
                                for d in range(DEEP):
                                    last = nc.tensor.matmul(p_count[r][:, :], from_hot[k][:, d, s, :], to_hot[r][:, d, :],
                                                            start=d == 0, stop=d == DEEP - 1)
                                last.then_inc(s_count, 1)

                        def fast():
                            pe.sem_inc(s_count, RING)
                            for k in range(2):
                                pe.sem_inc(s_summed[k], 1)
                            with pe.Fori(0, BOTH) as i:
                                for k in range(2):
                                    sum_group(k, i)
                                    count_block(k, i * 2 + k)
                            if BOTH < half:
                                with pe.Fori(BOTH, half) as i:
                                    for k in range(2):
                                        count_block(k, i * 2 + k)
                            if BOTH < PAIRS:
                                with pe.Fori(BOTH, PAIRS) as i:
                                    for k in range(2):
                                        sum_group(k, i)
                            sum_group(0, PAIRS)

                        both_paths(pe, all_fit, fast, lambda: g_tensor(pe))
                cleared([*s_in, *s_hot, *s_summed, *s_used, *s_old, s_stored, s_turn, *s_place, *s_kept, s_from, s_to,
                         s_count, s_copied, *g_stage])

        def counted_sum(tag, table, total, width):
            with ExitStack() as c:
                feat = sb(f"{tag}_feat", [P, BLOCKS, D], c=c)
                parts = sb(f"{tag}_parts", [P, BLOCKS, SPLIT], BF16, c=c)
                piece = [sb(f"{tag}_piece{q}", [P, PIECE, SPAN], BF16, c=c) for q in range(PIECES)]
                wide = sb(f"{tag}_wide", [SPLIT, SPAN], c=c)
                QUARTERS = SPAN // P
                old = sb(f"{tag}_old", [P, QUARTERS, width], c=c)
                new = sb(f"{tag}_new", [P, QUARTERS, width], c=c)
                p_wide = c.enter_context(nc.psum_tensor(f"{tag}_p_wide", [SPLIT, SPAN], F32))
                p_node = c.enter_context(nc.psum_tensor(f"{tag}_p_node", [P, BANK], F32))
                s_piece = [sem(f"{tag}_piece{q}", c) for q in range(PIECES)]
                s_feat, s_parts, s_used, s_copied, s_node, s_old, s_new, s_stored, s_turn = stage = [
                    sem(f"{tag}_{n}", c) for n in ("feat", "parts", "used", "copied", "node", "old", "new", "stored", "turn")]
                g_sync, g_gpsimd, g_vector, g_tensor, g_scalar, g_stage = general_sum(c, tag, table[0:n_nodes], total, width, None)

                with nc.Block() as block:
                    @block.sync
                    def _(sp):
                        def fast():
                            sp.dma_start(feat[:, :, :], table.rearrange("(b p) f -> p b f", p=P)).then_inc(s_feat, DMA)
                            for span_table, (lo, hi) in zip(counts, HALVES):
                                with sp.Fori(lo, hi) as s:
                                    for q in range(PIECES):
                                        sp.wait_ge(s_used, s * PIECES + (q + 1))
                                        sp.dma_start(piece[q][:, :, :], span_table[bass.ds(s - lo, 1), :, q * PIECE:(q + 1) * PIECE, :].rearrange(
                                            "o p b n -> (o p) b n")).then_inc(s_piece[q], DMA)

                        both_paths(sp, all_fit, fast, lambda: g_sync(sp))

                    @block.gpsimd
                    def _(pool):
                        both_paths(pool, all_fit, lambda: pool.sem_inc(s_turn, 1), lambda: g_gpsimd(pool))

                    @block.vector
                    def _(dve):
                        def fast():
                            step = Chain(dve, s_parts)
                            dve.wait_ge(s_feat, DMA)
                            for n in range(PARTS):
                                part = parts[:, :, n * D:(n + 1) * D]
                                step(nc.vector.tensor_copy(part, feat[:, :, :]))
                                if n < PARTS - 1:
                                    step(nc.vector.tensor_tensor(feat[:, :, :], feat[:, :, :], part, ALU.subtract))
                            step(nc.vector.memset(parts[:, :, PARTS * D:SPLIT], 1.0))
                            with dve.Fori(0, SPANS) as s:
                                dve.wait_ge(s_node, s + 1)
                                dve.wait_ge(s_old, s * DMA + DMA)
                                nc.vector.tensor_tensor(new[:, :, :], p_node[:, 0:QUARTERS * width].rearrange("p (q w) -> p q w", q=QUARTERS),
                                                        old[:, :, :], ALU.add).then_inc(s_new, 1)

                        both_paths(dve, all_fit, fast, lambda: g_vector(dve))

                    @block.scalar
                    def _(act):
                        def fast():
                            with act.Fori(0, SPANS) as s:
                                base = act.value_load(span_row[0:1, bass.ds(s, 1)], min_val=0, max_val=n_nodes - 1)
                                rows = total[bass.ds(base, SPAN)].rearrange("(q p) w -> p q w", p=P)
                                act.dma_start(old[:, :, :], rows).then_inc(s_old, DMA)
                                act.wait_ge(s_used, s * PIECES + 2 * PIECES)
                                nc.scalar.activation(wide[:, :], p_wide[:, :], ACT.Copy).then_inc(s_copied, 1)
                                act.wait_ge(s_new, s + 1)
                                act.dma_start(rows, new[:, :, :]).then_inc(s_stored, DMA)
                                act.wait_ge(s_stored, s * DMA + DMA)
                                act.sem_inc(s_turn, 1)

                        both_paths(act, all_fit, fast, lambda: g_scalar(act))

                    @block.tensor
                    def _(pe):
                        def fast():
                            pe.sem_inc(s_used, PIECES)
                            pe.wait_ge(s_parts, 2 * PARTS)
                            with pe.Fori(0, SPANS) as s:
                                for q in range(PIECES):
                                    pe.wait_ge(s_piece[q], s * DMA + DMA)
                                    for b in range(PIECE):
                                        last = nc.tensor.matmul(p_wide[:, :], parts[:, q * PIECE + b, :], piece[q][:, b, :],
                                                                start=q == 0 and b == 0, stop=q == PIECES - 1 and b == PIECE - 1)
                                    last.then_inc(s_used, 1)
                                pe.wait_ge(s_copied, s + 1)
                                for q in range(QUARTERS):
                                    last = nc.tensor.matmul(p_node[:, q * width:(q + 1) * width], wide[:, q * P:(q + 1) * P],
                                                            gather_parts[:, 0:width], start=True, stop=True)
                                last.then_inc(s_node, 1)

                        both_paths(pe, all_fit, fast, lambda: g_tensor(pe))
                cleared([*s_piece, *stage, *g_stage])

        BANKS = [(0, 3), (3, CHUNK)]

        def flat(ap):
            return ap.rearrange("p t e -> p (t e)")

        def when_fast(eng, fast):
            fits = eng.value_load(flag[0:1, 0:1], min_val=0, max_val=1)
            with eng.If(fits > 0):
                fast()

        def edge_mlp(pe, n, w1, hot_t_chunk, gathered, p_hidden, p_flow, hidden, w2, b2, s_hidden, s_relu, s_flow):
            for bank, (t0, t1) in enumerate(BANKS):
                nc.tensor.matmul(p_hidden[:, bank, 0:(t1 - t0) * P], w1[:, :], hot_t_chunk(t0, t1), start=True, stop=False)
                for t in range(t0, t1):
                    for r, rows in enumerate(gathered):
                        last = nc.tensor.matmul(p_hidden[:, bank, (t - t0) * P:(t - t0 + 1) * P], rows(t), identity[:, :],
                                                start=False, stop=t == t1 - 1 and r == len(gathered) - 1)
            last.then_inc(s_hidden, 1)
            nc.tensor.matmul(p_flow[:, 0:CHUNK * 2 * D], ones_f[0:1, :], b2[:, :, :].rearrange("o t f -> o (t f)"),
                             start=True, stop=False)
            pe.wait_ge(s_relu, n + 1)
            for t in range(CHUNK):
                last = nc.tensor.matmul(p_flow[:, t * 2 * D:(t + 1) * 2 * D], hidden[:, t * P:(t + 1) * P], w2[:, :],
                                        start=False, stop=t == CHUNK - 1)
            last.then_inc(s_flow, 1)

        with ExitStack() as c:
            SLOTS = CHUNKS
            w_e = [sb(f"e_w1{k}", [P, P], c=c) for k in range(2)]
            hot_t = [sb(f"e_hot_t{k}", [P, TILES, P], c=c) for k in range(2)]
            local_row = [sb(f"e_local_row{k}", [P, TILES, P], BF16, c=c) for k in range(2)]
            src_i = [sb(f"e_src_i{k}", [P, TILES], I32, c=c) for k in range(2)]
            bins = [sb(f"e_bins{k}", [P, TILES], c=c) for k in range(2)]
            starts = [sb(f"e_starts{k}", [P, TILES], c=c) for k in range(2)]
            places = [sb(f"e_places{k}", [P, TILES, 2], c=c) for k in range(2)]
            local = [sb(f"e_local{k}", [P, TILES], c=c) for k in range(2)]
            got = [sb(f"e_got{k}", [P, TILES, P], c=c) for k in range(2)]
            hot = [sb(f"e_hot{k}", [P, CHUNK, WINDOW], c=c) for k in range(2)]
            own = [sb(f"e_own{k}", [P, CHUNK, BLOCKS], BF16, c=c) for k in range(2)]
            ranked = sb("e_ranked", [P, CHUNK, BLOCKS], c=c)
            rank = sb("e_rank", [P, CHUNK], c=c)
            slot = sb("e_slot", [P, CHUNK], c=c)
            away = sb("e_away", [P, CHUNK], c=c)
            carry = sb("e_carry", [1, BLOCKS], BF16, c=c)
            to_row = [sb(f"e_to_row{k}", [P, CHUNK], I32, c=c) for k in range(SLOTS)]
            hidden = sb("e_hidden", [P, COLS], c=c)
            flow = sb("e_flow", [P, CHUNK, D], c=c)
            rec = [sb(f"e_rec{k}", [P, CHUNK, REC], BF16, c=c) for k in range(SLOTS)]
            bwd = [sb(f"e_bwd{k}", [P, CHUNK, D], c=c) for k in range(2)]
            b1 = sb("e_b1", [P, 1], c=c)
            w2 = sb("e_w2", [P, 2 * D], c=c)
            b2 = sb("e_b2", [1, CHUNK, 2 * D], c=c)
            old = [sb(f"e_old{k}", [WINDOW, D], c=c) for k in range(2)]
            new = [sb(f"e_new{k}", [WINDOW, D], c=c) for k in range(2)]
            p_hidden = c.enter_context(nc.psum_tensor("e_p_hidden", [P, 2, BANK], F32))
            p_flow = c.enter_context(nc.psum_tensor("e_p_flow", [P, BANK], F32))
            p_rank = c.enter_context(nc.psum_tensor("e_p_rank", [P, BANK], F32))
            p_carry = c.enter_context(nc.psum_tensor("e_p_carry", [1, BANK], F32))
            p_sum = [c.enter_context(nc.psum_tensor(f"e_p_sum{k}", [WINDOW, BANK], F32)) for k in range(2)]

            s_in, s_got, s_used, s_old = ([sem(f"e_{n}{k}", ctx if n == "got" else c) for k in range(2)]
                                           for n in ("in", "got", "used", "old"))
            s_recs = [sem(f"e_recs{q}") for q in range(2)]
            (s_w, s_const, s_hot_t, s_step, s_hidden, s_relu, s_flow, s_flowed, s_summed, s_ranked, s_carried, s_sent,
             s_stored, s_turn, s_worst, s_split) = (sem(f"e_{n}", c) for n in (
                 "weights", "const", "hot_t", "step", "hidden", "relu", "flow", "flowed", "summed", "ranked", "carried",
                 "sent", "stored", "turn", "worst", "split"))
            LOADS = 8
            STEPS = 11

            worst_row = sb("e_worst_row", [1, P * CHUNK], c=c)
            top, held = sb("e_top", [1, 1], c=c), sb("e_held", [1, 1], c=c)
            s_fits, s_turn_v, s_worst_in = (sem(f"e_{n}", c) for n in ("fits", "worst_step", "worst_in"))
            WEIGHTS = 4 + 2 * (2 + CHUNK)

            with nc.Block() as block:
                @block.sync
                def _(sp):
                    for k in range(2):
                        for n, w1 in enumerate((a["L0_gnn_W1f"], a["L0_gnn_W1b"])):
                            sp.dma_start(w_e[k][WINDOW:P, n * H:(n + 1) * H], w1[2 * D:2 * D + DE]).then_inc(s_w, DMA)
                    sp.wait_ge(s_const, 1)
                    for n, (w, b, bb) in enumerate((("W2f", "b1f", "b2f"), ("W2b", "b1b", "b2b"))):
                        sp.dma_start(w2[n * H:(n + 1) * H, n * D:(n + 1) * D], a[f"L0_gnn_{w}"]).then_inc(s_w, DMA)
                        sp.dma_start(b1[n * H:(n + 1) * H, :], a[f"L0_gnn_{b}"].rearrange("(h o) -> h o", o=1)).then_inc(s_w, DMA)
                        for t in range(CHUNK):
                            sp.dma_start(b2[0:1, t, n * D:(n + 1) * D], a[f"L0_gnn_{bb}"].rearrange("(o h) -> o h", o=1)).then_inc(s_w, DMA)
                    sp.wait_ge(s_w, WEIGHTS * DMA)

                    def attributes(g):
                        return a["edge_attr_16"][g] if isinstance(g, int) else a["edge_attr_16"][bass.ds(g, 1)].rearrange("o f n -> (o f) n")

                    def load(k, g, i):
                        base = fetch_base(sp, g)
                        sp.wait_ge(s_used[k], i + 1)
                        sp.dma_start(src_i[k][:, :], at_group(a["src"], g)).then_inc(s_in[k], DMA)
                        sp.dma_start(bins[k][:, :], at_group(bin_cols, g)).then_inc(s_in[k], DMA)
                        sp.dma_start(starts[k][:, :], at_group(start_cols, g)).then_inc(s_in[k], DMA)
                        sp.dma_start(places[k][:, :, :].rearrange("p t w -> p (t w)"),
                                     at_group(place_cols.rearrange("g p t w -> g p (t w)"), g)).then_inc(s_in[k], DMA)
                        sp.dma_start(local[k][:, :], at_group(local_cols, g)).then_inc(s_in[k], DMA)
                        sp.dma_start(flat(local_row[k][:, :, :]), row_group(local_rows, g)).then_inc(s_in[k], DMA)
                        sp.dma_start(flat(hot_t[k][WINDOW:P, :, :]), attributes(g)).then_inc(s_in[k], DMA)
                        sp.dma_start(w_e[k][0:WINDOW, :], window_rows(sp, pre_dst, base)).then_inc(s_in[k], DMA)

                    def add_window(k, g, i):
                        base = fetch_base(sp, g)
                        rows = window_rows(sp, fwd_sum, base)
                        sp.dma_start(old[k][:, :], rows).then_inc(s_old[k], DMA)
                        sp.wait_ge(s_used[k], i + 2)
                        sp.dma_start(rows, new[k][:, :]).then_inc(s_stored, DMA)
                        sp.wait_ge(s_stored, (g + 1) * DMA)
                        sp.sem_inc(s_turn, 1)

                    def fast():
                        load(0, 0, 0)
                        with sp.Fori(0, PAIRS) as i:
                            load(1, i * 2 + 1, i)
                            add_window(0, i * 2, i)
                            load(0, i * 2 + 2, i + 1)
                            add_window(1, i * 2 + 1, i)
                        add_window(0, NG - 1, PAIRS)

                    when_fast(sp, fast)
                    sp.wait_ge(s_worst, 1)
                    sp.dma_start(worst_rank, worst[:, :]).then_inc(s_worst_in, DMA)
                    sp.wait_ge(s_worst_in, DMA)
                    sp.dma_start(worst_row[:, :], worst_rank.rearrange("p t -> (p t)").rearrange("(o n) -> o n", o=1)).then_inc(s_worst_in, DMA)

                @block.gpsimd
                def _(pool):
                    def gather(k, t):
                        nc.gpsimd.indirect_dma_start(
                            out=got[k][:, t, :], out_offset=None, in_=pre_src,
                            in_offset=bass.IndirectOffsetOnAxis(ap=src_i[k][:, t:t + 1], axis=0)).then_inc(s_got[k], DMA)

                    def group(k, i, following):
                        if following is not None:
                            pool.wait_ge(s_in[1 - k], following * (LOADS * DMA) + LOADS * DMA)
                            pool.sem_inc(s_turn, 1)
                        for m in range(CHUNKS):
                            if following is not None:
                                for t in range(m * CHUNK, (m + 1) * CHUNK):
                                    gather(1 - k, t)
                            j = k * CHUNKS + m
                            n = i * (2 * CHUNKS) + j
                            pool.wait_ge(s_step, n * STEPS + STEPS)
                            pool.wait_ge(s_split, n * 3 + 6)
                            if not isinstance(n, int) or n:
                                pool.wait_ge(s_recs[(j + 1) % 2], (i * CHUNKS + (j + 1) // 2) * (CHUNK * DMA))
                            pool.sem_inc(s_turn, 1)
                            for t in range(CHUNK):
                                nc.gpsimd.indirect_dma_start(
                                    out=records, out_offset=bass.IndirectOffsetOnAxis(ap=to_row[j % SLOTS][:, t:t + 1], axis=0),
                                    in_=rec[j % SLOTS].ap().bitcast(F32)[:, t, :], in_offset=None).then_inc(s_recs[j % 2], DMA)
                            pool.sem_inc(s_sent, 1)

                    def fast():
                        pool.sem_inc(s_sent, SLOTS - 1)
                        pool.wait_ge(emptied, DMA)
                        pool.wait_ge(s_in[0], LOADS * DMA)
                        for t in range(TILES):
                            gather(0, t)
                        group(0, 0, 0)
                        group(1, 0, 1)
                        with pool.Fori(1, PAIRS) as i:
                            group(0, i, i)
                            group(1, i, i + 1)
                        group(0, PAIRS, None)
                        for q in range(2):
                            pool.wait_ge(s_recs[q], ((NC + 1 - q) // 2) * (CHUNK * DMA))

                    when_fast(pool, fast)

                @block.vector
                def _(dve):
                    nc.vector.memset(w2[:, :], 0.0).then_inc(s_const, 1)
                    nc.vector.memset(carry[:, :], 0.0).then_inc(s_const, 1)
                    nc.vector.memset(bwd[1][:, :, :], 0.0).then_inc(s_const, 1)
                    nc.vector.memset(rec[SLOTS - 1][:, :, :], 0.0).then_inc(s_const, 1)

                    def split(j, n):
                        flows, parts = bwd[(j - 1) % 2], rec[(j - 1) % SLOTS]
                        dve.wait_ge(s_flowed, n + 1)
                        nc.vector.tensor_tensor(flows[:, :, :], flows[:, :, :], parts[:, :, 0:D], ALU.subtract).then_inc(s_split, 1)
                        dve.wait_ge(s_split, n * 3 + 1)
                        nc.vector.tensor_copy(parts[:, :, D:2 * D], flows[:, :, :]).then_inc(s_split, 1)
                        dve.wait_ge(s_split, n * 3 + 2)
                        nc.vector.tensor_tensor(parts[:, :, 2 * D:3 * D], flows[:, :, :], parts[:, :, D:2 * D], ALU.subtract).then_inc(s_split, 1)

                    def chunk(k, m, i):
                        j = k * CHUNKS + m
                        n = i * (2 * CHUNKS) + j
                        q = j % 2
                        part = slice(m * CHUNK, (m + 1) * CHUNK)
                        count = [0]

                        def add(ins):
                            count[0] += 1
                            ins.then_inc(s_step, 1)
                            dve.wait_ge(s_step, n * STEPS + count[0])

                        dve.wait_ge(s_summed, n + 1)
                        nc.vector.tensor_tensor(own[q][:, :, :], column[:, 0:BLOCKS].unsqueeze(1).to_broadcast([P, CHUNK, BLOCKS]),
                                                bins[k][:, part].unsqueeze(2).to_broadcast([P, CHUNK, BLOCKS]), ALU.is_equal).then_inc(s_step, 1)
                        nc.vector.tensor_scalar(hot_t[k][0:WINDOW, part, :], local_row[k][0:WINDOW, part, :],
                                                row_id[0:WINDOW, 0:1], None, ALU.is_equal).then_inc(s_step, 1)
                        nc.vector.tensor_tensor(hot[q][:, :, :], column[:, 0:WINDOW].unsqueeze(1).to_broadcast([P, CHUNK, WINDOW]),
                                                local[k][:, part].unsqueeze(2).to_broadcast([P, CHUNK, WINDOW]), ALU.is_equal).then_inc(s_step, 1)
                        dve.wait_ge(s_sent, n + 1)
                        nc.vector.tensor_copy(rec[j % SLOTS][:, :, PARTS * D:REC], places[k][:, part, :]).then_inc(s_step, 1)
                        count[0] = 4
                        split(j, n)
                        dve.wait_ge(s_ranked, n + 1)
                        dve.wait_ge(s_step, n * STEPS + 4)
                        shape = [P, CHUNK, BLOCKS]
                        add(nc.vector.tensor_tensor(ranked[:, :, :], p_rank[:, 0:CHUNK * BLOCKS].rearrange("p (t b) -> p t b", t=CHUNK),
                                                    own[q][:, :, :], ALU.mult))
                        add(nc.vector.tensor_reduce(rank[:, :], ranked[:, :, :], AX, ALU.add))
                        add(nc.vector.scalar_tensor_tensor(out=slot[:, :], in0=rank[:, :], scalar=float(SPANS), in1=starts[k][:, part],
                                                           op0=ALU.mult, op1=ALU.add))
                        at = span_no[:, n:n + 1] if isinstance(n, int) else span_no[:, bass.ds(n, 1)]
                        add(nc.vector.tensor_scalar(slot[:, :], slot[:, :], at, None, ALU.add))
                        add(nc.vector.tensor_scalar(away[:, :], slot[:, :], -1.0, spare_record[:, 0:1], ALU.mult, ALU.add))
                        add(nc.vector.scalar_tensor_tensor(out=away[:, :], in0=rank[:, :], scalar=float(CAPACITY), in1=away[:, :],
                                                           op0=ALU.is_ge, op1=ALU.mult))
                        nc.vector.tensor_tensor(worst[:, :], worst[:, :], rank[:, :], ALU.max).then_inc(s_turn_v, 1)
                        add(nc.vector.tensor_tensor(to_row[j % SLOTS][:, :], slot[:, :], away[:, :], ALU.add))

                    def add_old(k, i):
                        dve.wait_ge(s_summed, (i * 2 + (k + 1)) * CHUNKS + 2)
                        dve.wait_ge(s_old[k], i * DMA + DMA)
                        nc.vector.tensor_tensor(new[k][:, :], p_sum[k][:, 0:D], old[k][:, :], ALU.add).then_inc(s_used[k], 1)

                    def fast():
                        for k in range(2):
                            dve.sem_inc(s_used[k], 1)
                        with dve.Fori(0, PAIRS) as i:
                            for k in range(2):
                                dve.wait_ge(s_in[k], i * (LOADS * DMA) + LOADS * DMA)
                                for m in range(CHUNKS):
                                    chunk(k, m, i)
                                add_old(k, i)
                        dve.wait_ge(s_in[0], (PAIRS + 1) * LOADS * DMA)
                        for m in range(CHUNKS):
                            chunk(0, m, PAIRS)
                        split(CHUNKS, NC)
                        add_old(0, PAIRS)

                    when_fast(dve, fast)
                    dve.sem_inc(s_worst, 1)
                    step = Chain(dve, s_fits)
                    dve.wait_ge(s_worst_in, 2 * DMA)
                    step(nc.vector.tensor_reduce(top[:, :], worst_row[:, :], AX, ALU.max))
                    step(nc.vector.tensor_scalar(top[:, :], top[:, :], float(CAPACITY), None, ALU.is_lt))
                    step(nc.vector.tensor_copy(held[:, :], flag[:, :]))
                    step(nc.vector.tensor_tensor(held[:, :], held[:, :], top[:, :], ALU.mult))
                    step(nc.vector.tensor_copy(all_fit[:, :], held[:, :]))

                @block.scalar
                def _(act):
                    act.wait_ge(s_w, WEIGHTS * DMA)

                    def chunk(k, m, i):
                        j = k * CHUNKS + m
                        n = i * (2 * CHUNKS) + j
                        act.wait_ge(s_ranked, n + 1)
                        at = keep[0:1, n:n + 1] if isinstance(n, int) else keep[0:1, bass.ds(n, 1)]
                        nc.scalar.activation(carry[:, :], p_carry[:, 0:BLOCKS], ACT.Copy, scale=at).then_inc(s_carried, 1)
                        act.wait_ge(s_hidden, n + 1)
                        for bank, (t0, t1) in enumerate(BANKS):
                            last = nc.scalar.activation(hidden[:, t0 * P:t1 * P], p_hidden[:, bank, 0:(t1 - t0) * P], ACT.Relu,
                                                        bias=b1[:, 0:1])
                        last.then_inc(s_relu, 1)
                        act.wait_ge(s_flow, n + 1)
                        flows = p_flow[:, 0:CHUNK * 2 * D].rearrange("p (t f) -> p t f", t=CHUNK)
                        nc.scalar.activation(flow[:, :, :], flows[:, :, 0:D], ACT.Relu)
                        nc.scalar.activation(bwd[j % 2][:, :, :], flows[:, :, D:2 * D], ACT.Relu)
                        act.wait_ge(s_sent, n + 1)
                        nc.scalar.activation(rec[j % SLOTS][:, :, 0:D], flows[:, :, D:2 * D], ACT.Relu).then_inc(s_flowed, 1)

                    def fast():
                        act.wait_ge(s_const, 4)
                        act.sem_inc(s_flowed, 1)
                        with act.Fori(0, PAIRS) as i:
                            for k in range(2):
                                for m in range(CHUNKS):
                                    chunk(k, m, i)
                        for m in range(CHUNKS):
                            chunk(0, m, PAIRS)

                    when_fast(act, fast)

                @block.tensor
                def _(pe):
                    pe.wait_ge(s_w, WEIGHTS * DMA)
                    pe.wait_ge(s_const, 2)

                    def chunk(k, m, i):
                        j = k * CHUNKS + m
                        n = i * (2 * CHUNKS) + j
                        q = j % 2
                        pe.wait_ge(s_step, n * STEPS + 1)
                        pe.wait_ge(s_carried, n + 1)
                        counted = p_rank[:, 0:CHUNK * BLOCKS].rearrange("p (t b) -> p t b", t=CHUNK)
                        nc.tensor.matmul(counted, ones[0:1, :], carry[0:1, :].unsqueeze(1).to_broadcast([1, CHUNK, BLOCKS]), start=True, stop=False)
                        for t in range(CHUNK):
                            nc.tensor.matmul(counted[:, t, :], behind[:, :], own[q][:, t, :], start=False, stop=False)
                        for t in range(CHUNK - 1):
                            nc.tensor.matmul(counted[:, t + 1:CHUNK, :], ones[:, :],
                                             own[q][:, t:t + 1, :].to_broadcast([P, CHUNK - 1 - t, BLOCKS]), start=False, stop=t == CHUNK - 2)
                        nc.tensor.matmul(p_carry[:, 0:BLOCKS], ones[0:1, 0:1], carry[0:1, :], start=True, stop=False)
                        for t in range(CHUNK):
                            last = nc.tensor.matmul(p_carry[:, 0:BLOCKS], ones[:, 0:1], own[q][:, t, :], start=False, stop=t == CHUNK - 1)
                        last.then_inc(s_ranked, 1)

                        first = m * CHUNK
                        pe.wait_ge(s_step, n * STEPS + 2)
                        edge_mlp(pe, n, w_e[k], lambda t0, t1: flat(hot_t[k][:, first + t0:first + t1, :]),
                                 [lambda t: got[k][:, first + t, :]], p_hidden, p_flow, hidden, w2, b2, s_hidden, s_relu, s_flow)
                        pe.wait_ge(s_flowed, n + 2)
                        pe.wait_ge(s_step, n * STEPS + 3)
                        if m == 0:
                            pe.wait_ge(s_used[k], i + 1)
                        for t in range(CHUNK):
                            last = nc.tensor.matmul(p_sum[k][:, 0:D], hot[q][:, t, :], flow[:, t, :],
                                                    start=m == 0 and t == 0, stop=m == CHUNKS - 1 and t == CHUNK - 1)
                        last.then_inc(s_summed, 1)

                    def group(k, i):
                        pe.wait_ge(s_got[k], i * (TILES * DMA) + TILES * DMA)
                        pe.wait_ge(s_in[k], i * (LOADS * DMA) + LOADS * DMA)
                        for m in range(CHUNKS):
                            chunk(k, m, i)

                    def fast():
                        pe.sem_inc(s_summed, 2)
                        pe.sem_inc(s_carried, 1)
                        with pe.Fori(0, PAIRS) as i:
                            group(0, i)
                            group(1, i)
                        group(0, PAIRS)

                    when_fast(pe, fast)
            cleared([*s_in, *s_used, *s_old, s_w, s_const, s_hot_t, s_step, s_hidden, s_relu, s_flow, s_flowed, s_summed,
                     s_ranked, s_carried, s_sent, s_stored, s_turn, s_worst, s_split, s_fits, s_turn_v, s_worst_in])

        with ExitStack() as c:
            BIN = DEEP * SPANS
            rec = [sb(f"s_rec{k}", [P, DEEP, SPANS, REC], BF16, c=c) for k in range(2)]
            hot = [sb(f"s_hot{k}", [P, DEEP, SPANS, P], BF16, c=c) for k in range(2)]
            local = [sb(f"s_local{k}", [P, DEEP, SPANS, 2], c=c) for k in range(2)]
            wide = sb("s_wide", [PARTS * D, P], c=c)
            total = [sb(f"s_total{k}", [P, D], c=c) for k in range(2)]
            p_wide = [c.enter_context(nc.psum_tensor(f"s_p_wide{k}", [PARTS * D, BANK], F32)) for k in range(2)]
            p_total = c.enter_context(nc.psum_tensor("s_p_total", [P, BANK], F32))
            w_e = sb("g_w1", [P, P], c=c)
            hot_t = sb("g_hot_t", [P, CHUNK, P], c=c)
            g_rows = [sb(f"g_row{n}", [P, CHUNK, P], c=c) for n in range(2)]
            g_ints = [sb(f"g_int{n}", [P, CHUNK], I32, c=c) for n in range(2)]
            g_cols = [sb(f"g_col{n}", [P, CHUNK], c=c) for n in range(2)]
            got = [sb(f"g_got{n}", [P, CHUNK, P], c=c) for n in range(2)]
            same = [sb(f"g_same{n}", [P, CHUNK, P], c=c) for n in range(2)]
            earlier = sb("g_earlier", [P, CHUNK, P], c=c)
            twin, away = sb("g_twin", [P, CHUNK], c=c), sb("g_away", [P, CHUNK], c=c)
            to_row = [sb(f"g_to_row{n}", [P, CHUNK], I32, c=c) for n in range(2)]
            hidden = sb("g_hidden", [P, COLS], c=c)
            flow = sb("g_flow", [P, CHUNK, 2 * D], c=c)
            merged = [sb(f"g_merged{n}", [P, CHUNK, D], c=c) for n in range(2)]
            b1, w2, b2 = sb("g_b1", [P, 1], c=c), sb("g_w2", [P, 2 * D], c=c), sb("g_b2", [1, CHUNK, 2 * D], c=c)
            p_hidden = c.enter_context(nc.psum_tensor("g_p_hidden", [P, 2, BANK], F32))
            p_flow = c.enter_context(nc.psum_tensor("g_p_flow", [P, BANK], F32))
            p_merged = c.enter_context(nc.psum_tensor("g_p_merged", [P, BANK], F32))
            s_in = [sem(f"s_in{k}", c) for k in range(2)]
            g_got, g_added = ([sem(f"g_{n}{d}") for d in range(2)] for n in ("got", "added"))
            s_hot, s_total, s_taken, s_local, s_wide, s_copied = (
                sem(f"s_{n}", c) for n in ("hot", "total", "taken", "local", "wide", "copied"))
            s_stored = [sem(f"s_stored{k}", c) for k in range(2)]
            g_w, g_step, g_relu, g_flow, g_flowed, g_copied, g_free, g_turn = (
                sem(f"g_{n}", c) for n in ("weights", "step", "relu", "flow", "flowed", "copied", "free", "turn"))
            g_in, g_zeroed, g_merged, g_hidden = s_in[0], s_hot, s_total, s_taken
            g_loads = 7
            half = BLOCKS // 2
            WEIGHTS = 2 + 2 * (2 + CHUNK)

            with nc.Block() as block:
                @block.sync
                def _(sp):
                    def block_records(b):
                        return records[bass.ds(b * STRIDE, STRIDE)].rearrange("(d p s) c -> p d (s c)", d=DEEP, p=P)

                    def fast():
                        def slot(k):
                            return rec[k].ap().bitcast(F32).rearrange("p d s c -> p d (s c)")

                        for k in range(2):
                            sp.dma_start(slot(k), records[k * STRIDE:(k + 1) * STRIDE].rearrange("(d p s) c -> p d (s c)", d=DEEP, p=P)).then_inc(s_in[k], DMA)
                        with sp.Fori(0, half) as i:
                            for k in range(2):
                                sp.wait_ge(s_local, i * 2 + (k + 1))
                                sp.wait_ge(s_wide, i * 2 + (k + 1))
                                following = (i * 2 + (k + 2)) % BLOCKS
                                sp.dma_start(slot(k), block_records(following)).then_inc(s_in[k], DMA)
                                sp.wait_ge(s_taken, i * 2 + (k + 1))
                                sp.dma_start(bwd_sum[bass.ds((i * 2 + k) * P, P)], total[k][:, :]).then_inc(s_stored[k], DMA)
                                sp.dma_start(local_table[bass.ds(i * 2 + k, 1)].rearrange("o p n -> (o p) n"),
                                             local[k][:, :, :, :].rearrange("p d s w -> p (d s w)")).then_inc(s_stored[k], DMA)
                        for k in range(2):
                            sp.wait_ge(s_stored[k], (BLOCKS + 2) * DMA)
                        for k in range(2):
                            sp.wait_ge(s_in[k], (half + 1) * DMA)

                    def general():
                        for n, w1 in enumerate((a["L0_gnn_W1f"], a["L0_gnn_W1b"])):
                            sp.dma_start(w_e[WINDOW:P, n * H:(n + 1) * H], w1[2 * D:2 * D + DE]).then_inc(g_w, DMA)
                        sp.wait_ge(g_zeroed, 3)
                        for n, (w, b, bb) in enumerate((("W2f", "b1f", "b2f"), ("W2b", "b1b", "b2b"))):
                            sp.dma_start(w2[n * H:(n + 1) * H, n * D:(n + 1) * D], a[f"L0_gnn_{w}"]).then_inc(g_w, DMA)
                            sp.dma_start(b1[n * H:(n + 1) * H, :], a[f"L0_gnn_{b}"].rearrange("(h o) -> h o", o=1)).then_inc(g_w, DMA)
                            for t in range(CHUNK):
                                sp.dma_start(b2[0:1, t, n * D:(n + 1) * D], a[f"L0_gnn_{bb}"].rearrange("(o h) -> o h", o=1)).then_inc(g_w, DMA)
                        with sp.Fori(0, NG) as g:
                            features = a["edge_attr_16"][bass.ds(g, 1)].rearrange("o f n -> (o f) n")
                            for m in range(CHUNKS):
                                part = slice(m * CHUNK, (m + 1) * CHUNK)
                                sp.wait_ge(g_free, g * CHUNKS + (m + 1))
                                for n, (ints, cols, rows) in enumerate(((a["src"], src_cols, src_rows), (a["dst"], dst_cols, dst_rows))):
                                    sp.dma_start(g_ints[n][:, :], at_group(ints, g)[:, part]).then_inc(g_in, DMA)
                                    sp.dma_start(g_cols[n][:, :], at_group(cols, g)[:, part]).then_inc(g_in, DMA)
                                    sp.dma_start(flat(g_rows[n][:, :, :]), row_group(rows, g, m * CHUNK, CHUNK)).then_inc(g_in, DMA)
                                sp.dma_start(flat(hot_t[WINDOW:P, :, :]), features[:, m * COLS:(m + 1) * COLS]).then_inc(g_in, DMA)

                    both_paths(sp, all_fit, fast, general)

                @block.gpsimd
                def _(pool):
                    def fast():
                        pool.sem_inc(g_turn, 1)

                    def general():
                        pool.sem_inc(g_free, 1)
                        with pool.Fori(0, NG) as g:
                            for m in range(CHUNKS):
                                n = g * CHUNKS + m
                                pool.wait_ge(g_in, n * (g_loads * DMA) + g_loads * DMA)
                                pool.sem_inc(g_turn, 1)
                                for t in range(CHUNK):
                                    for d, table in enumerate((pre_src, pre_dst[0:n_nodes])):
                                        nc.gpsimd.indirect_dma_start(
                                            out=got[d][:, t, :], out_offset=None, in_=table,
                                            in_offset=bass.IndirectOffsetOnAxis(ap=g_ints[d][:, t:t + 1], axis=0)).then_inc(g_got[d], DMA)
                                pool.wait_ge(g_copied, n * 2 + 2)
                                pool.sem_inc(g_turn, 1)
                                for t in range(CHUNK):
                                    for d, table in enumerate((bwd_sum, fwd_general)):
                                        nc.gpsimd.indirect_dma_start(
                                            out=table, out_offset=bass.IndirectOffsetOnAxis(ap=to_row[d][:, t:t + 1], axis=0),
                                            in_=merged[d][:, t, :], in_offset=None, compute_op=ALU.add).then_inc(g_added[d], DMA)
                                    for d in range(2):
                                        pool.wait_ge(g_added[d], n * (CHUNK * DMA) + (t + 1) * DMA)
                                    pool.sem_inc(g_turn, 1)
                                pool.sem_inc(g_free, 1)

                    both_paths(pool, all_fit, fast, general)

                @block.vector
                def _(dve):
                    def fast():
                        with dve.Fori(0, half) as i:
                            for k in range(2):
                                dve.wait_ge(s_in[k], i * DMA + DMA)
                                nc.vector.tensor_tensor(
                                    hot[k][:, :, :, :].rearrange("p d s e -> p (d s) e"), column_s[:, :].unsqueeze(1).to_broadcast([P, BIN, P]),
                                    rec[k][:, :, :, PARTS * D:PARTS * D + 1].rearrange("p d s o -> p (d s) o").to_broadcast([P, BIN, P]),
                                    ALU.is_equal).then_inc(s_hot, 1)

                    def general():
                        nc.vector.memset(hot_t[0:WINDOW, :, :], 0.0).then_inc(g_zeroed, 1)
                        nc.vector.memset(w_e[0:WINDOW, :], 0.0).then_inc(g_zeroed, 1)
                        nc.vector.memset(w2[:, :], 0.0).then_inc(g_zeroed, 1)
                        with dve.Fori(0, NG) as g:
                            for m in range(CHUNKS):
                                n = g * CHUNKS + m
                                dve.wait_ge(g_in, n * (g_loads * DMA) + g_loads * DMA)
                                for d in range(2):
                                    merge_steps(dve, g_step, n * 12 + 6 * d, g_cols[d][:, :], g_rows[d], same[d], earlier, twin, away, to_row[d])
                                dve.wait_ge(g_merged, n + 1)
                                for d in range(2):
                                    nc.vector.tensor_copy(merged[d][:, :, :], p_merged[:, d * CHUNK * D:(d + 1) * CHUNK * D].rearrange(
                                        "p (t f) -> p t f", t=CHUNK)).then_inc(g_copied, 1)

                    both_paths(dve, all_fit, fast, general)

                @block.scalar
                def _(act):
                    def fast():
                        for k in range(2):
                            act.sem_inc(s_stored[k], 2 * DMA)
                        with act.Fori(0, half) as i:
                            for k in range(2):
                                act.wait_ge(s_in[k], i * DMA + DMA)
                                act.wait_ge(s_stored[k], i * (2 * DMA) + 2 * DMA)
                                nc.scalar.activation(local[k][:, :, :, :], rec[k][:, :, :, PARTS * D:REC], ACT.Copy).then_inc(s_local, 1)
                                act.wait_ge(s_wide, i * 2 + (k + 1))
                                nc.scalar.activation(wide[:, :], p_wide[k][:, 0:P], ACT.Copy).then_inc(s_copied, 1)
                                act.wait_ge(s_total, i * 2 + (k + 1))
                                nc.scalar.activation(total[k][:, :], p_total[:, 0:D], ACT.Copy).then_inc(s_taken, 1)

                    def general():
                        act.wait_ge(g_w, WEIGHTS * DMA)
                        with act.Fori(0, NC) as n:
                            act.wait_ge(g_hidden, n + 1)
                            for bank, (t0, t1) in enumerate(BANKS):
                                last = nc.scalar.activation(hidden[:, t0 * P:t1 * P], p_hidden[:, bank, 0:(t1 - t0) * P], ACT.Relu,
                                                            bias=b1[:, 0:1])
                            last.then_inc(g_relu, 1)
                            act.wait_ge(g_flow, n + 1)
                            nc.scalar.activation(flow[:, :, :], p_flow[:, 0:CHUNK * 2 * D].rearrange("p (t f) -> p t f", t=CHUNK),
                                                 ACT.Relu).then_inc(g_flowed, 1)

                    both_paths(act, all_fit, fast, general)

                @block.tensor
                def _(pe):
                    def fast():
                        with pe.Fori(0, half) as i:
                            for k in range(2):
                                pe.wait_ge(s_in[k], i * DMA + DMA)
                                pe.wait_ge(s_hot, i * 2 + (k + 1))
                                for t in range(BIN):
                                    d, s = divmod(t, SPANS)
                                    last = nc.tensor.matmul(p_wide[k][:, 0:P], rec[k][:, d, s, 0:PARTS * D], hot[k][:, d, s, :],
                                                            start=t == 0, stop=t == BIN - 1)
                                last.then_inc(s_wide, 1)
                                pe.wait_ge(s_copied, i * 2 + (k + 1))
                                nc.tensor.matmul(p_total[:, 0:D], wide[:, :], gather_parts[0:PARTS * D, 0:D], start=True, stop=True).then_inc(s_total, 1)

                    def general():
                        pe.wait_ge(g_w, WEIGHTS * DMA)
                        pe.wait_ge(g_zeroed, 3)
                        with pe.Fori(0, NC) as n:
                            pe.wait_ge(g_in, n * (g_loads * DMA) + g_loads * DMA)
                            for d in range(2):
                                pe.wait_ge(g_got[d], n * (CHUNK * DMA) + CHUNK * DMA)
                            edge_mlp(pe, n, w_e, lambda t0, t1: flat(hot_t[:, t0:t1, :]),
                                     [lambda t: got[0][:, t, :], lambda t: got[1][:, t, :]], p_hidden, p_flow, hidden, w2, b2,
                                     g_hidden, g_relu, g_flow)
                            pe.wait_ge(g_flowed, n + 1)
                            pe.wait_ge(g_step, n * 12 + 12)
                            for d in range(2):
                                for t in range(CHUNK):
                                    at = (d * CHUNK + t) * D
                                    last = nc.tensor.matmul(p_merged[:, at:at + D], same[d][:, t, :], flow[:, t, (1 - d) * D:(2 - d) * D],
                                                            start=True, stop=True)
                            last.then_inc(g_merged, 1)

                    both_paths(pe, all_fit, fast, general)
            cleared([*s_in, s_hot, s_total, s_taken, *s_stored, s_local, s_wide, s_copied, g_w, g_step, g_relu, g_flow, g_flowed, g_copied, g_free, g_turn])


        with ExitStack() as c:
            both = sb("both", [LANES, PER, 2 * D], c=c)
            part = [sb(f"part{n}", [LANES, PER, D], c=c) for n in range(3)]
            b2 = sb("b2n", [LANES, D], c=c)
            p_in, v = sem("part_in"), sem("part_v")
            with nc.Block() as block:
                @block.sync
                def _(sp):
                    def load(n, table):
                        sp.dma_start(part[n][:, :, :], table[0:n_nodes].rearrange("(p j) f -> p j f", p=LANES)).then_inc(p_in, DMA)

                    both_paths(sp, all_fit, lambda: load(0, fwd_sum), lambda: load(0, fwd_general))
                    load(1, bwd_sum)
                    sp.dma_start(b2[:, :], a["L0_gnn_b2n"].rearrange("(o f) -> o f", o=1).to_broadcast([LANES, D])).then_inc(p_in, DMA)

                @block.vector
                def _(dve):
                    dve.wait_ge(p_in, 3 * DMA)
                    step = Chain(dve, v)
                    step(nc.vector.tensor_copy(both[:, :, 0:D], part[0][:, :, :]))
                    step(nc.vector.tensor_copy(both[:, :, D:2 * D], part[1][:, :, :]))
            taken = part[0]
            node_mlp("mlp0", both, 2 * D, a["L0_gnn_W1n"], a["L0_gnn_b1n"], a["L0_gnn_W2n"], ACT.Relu, taken)
            t = (sb("mean1", [LANES, PER], c=c), sb("var1", [LANES, PER], c=c), part[1], part[2])
            v, ready, rooted, stored = (sem(n) for n in ("n1_v", "n1_ready", "n1_root", "n1_stored"))
            with nc.Block() as block:
                @block.vector
                def _(dve):
                    step = Chain(dve, v)
                    step(nc.vector.tensor_tensor(taken[:, :, :], taken[:, :, :],
                                                 b2[:, :].unsqueeze(1).to_broadcast([LANES, PER, D]), ALU.add))
                    step(nc.vector.tensor_scalar(taken[:, :, :], taken[:, :, :], 0.0, None, ALU.max))
                    step(nc.vector.tensor_tensor(x[:, :, :], x[:, :, :], taken[:, :, :], ALU.add))
                    layernorm(step, rooted, ready, 1, t)
                    dve.sem_inc(ready, 1)

                @block.scalar
                def _(act):
                    root(act, ready, rooted, t[1][:, :], 1)

                @block.sync
                def _(sp):
                    sp.wait_ge(ready, 2)
                    sp.dma_start(feats[0][0:n_nodes].rearrange("(p j) f -> p j f", p=LANES), h[:, :, :]).then_inc(stored, DMA)
                    sp.wait_ge(stored, DMA)

        weighted_sum("l1", feats[0][0:n_nodes], sums[0], a["edge_weight"])

        def node_step(tag, constants, kept, ops, roots, total, width=D):
            with ExitStack() as c:
                summed = sb(f"{tag}_summed", [LANES, PER, width], c=c)
                t = scratch(c, tag)
                extra = {n: sb(f"{tag}_{n}", list(shape), c=c) for n, (shape, _) in constants.items()}
                s_in, v, ready, rooted, stored = (sem(f"{tag}_{n}") for n in ("sums_in", "v", "ready", "root", "stored"))
                with nc.Block() as block:
                    @block.sync
                    def _(sp):
                        sp.dma_start(summed[:, :, :], total[0:n_nodes].rearrange("(p j) f -> p j f", p=LANES)).then_inc(s_in, DMA)
                        for n, (_, ap) in constants.items():
                            sp.dma_start(extra[n][:, :], ap).then_inc(s_in, DMA)
                        if kept is not None:
                            sp.wait_ge(ready, roots + 1)
                            sp.dma_start(kept[0], kept[1][:, :, :]).then_inc(stored, DMA)
                            sp.wait_ge(stored, DMA)

                    @block.vector
                    def _(dve):
                        dve.wait_ge(s_in, (1 + len(constants)) * DMA)
                        step = Chain(dve, v)
                        ops(dve, step, summed, t, extra, ready, rooted)
                        dve.sem_inc(ready, 1)

                    @block.scalar
                    def _(act):
                        for n in range(roots):
                            root(act, ready, rooted, (t[1], t[0])[n][:, :], n + 1)

        def node_rows(table):
            return table[0:n_nodes].rearrange("(p j) f -> p j f", p=LANES)

        def spread(ap):
            return ap.rearrange("(o f) -> o f", o=1).to_broadcast([LANES, ap.shape[0]])

        def after_l1(dve, step, summed, t, extra, ready, rooted):
            step(nc.vector.tensor_tensor(x[:, :, :], x[:, :, :], summed[:, :, :], ALU.add))
            layernorm(step, rooted, ready, 1, t)

        node_step("n2", {}, (node_rows(feats[1]), h), after_l1, 1, sums[0])

        counted_sum("l2", feats[1], sums[1], widths[1])

        def after_l2(dve, step, summed, t, extra, ready, rooted):
            eps1 = extra["eps"]
            step(nc.vector.tensor_scalar(eps1[:, :], eps1[:, :], 1.0, None, ALU.add))
            step(nc.vector.scalar_tensor_tensor(out=h[:, :, :], in0=h[:, :, :], scalar=eps1[:, 0:1], in1=summed[:, :, 0:D],
                                                op0=ALU.mult, op1=ALU.add))
            step(nc.vector.tensor_tensor(x[:, :, :], x[:, :, :], h[:, :, :], ALU.add))
            layernorm(step, rooted, ready, 1, t)
            mean = t[0]
            step(nc.vector.tensor_scalar(mean[:, :], summed[:, :, D], 1.0, None, ALU.add))
            step(nc.vector.reciprocal(inv_deg[:, :], mean[:, :]))
            dve.sem_inc(ready, 1)
            dve.wait_ge(rooted, 2)
            step(nc.vector.reciprocal(inv_sqrt[:, :], mean[:, :]))
            step(nc.vector.tensor_tensor(t[2][:, :, :], h[:, :, :], over(inv_sqrt), ALU.mult))

        with ExitStack() as keep:
            scaled = sb("scaled", [LANES, PER, D], c=keep)

            def after_l2_store(dve, step, summed, t, extra, ready, rooted):
                after_l2(dve, step, summed, t, extra, ready, rooted)
                step(nc.vector.tensor_copy(scaled[:, :, :], t[2][:, :, :]))

            node_step("n3", {"eps": ((LANES, 1), spread(a["L2_gnn_eps"]))}, (node_rows(feats[2]), scaled), after_l2_store,
                      2, sums[1], widths[1])

            counted_sum("l3a", feats[2], sums[2], widths[2])

            def after_l3a(dve, step, summed, t, extra, ready, rooted):
                step(nc.vector.tensor_tensor(summed[:, :, :], summed[:, :, :], over(inv_sqrt), ALU.mult))
                step(nc.vector.tensor_tensor(scaled[:, :, :], h[:, :, :], over(inv_deg), ALU.mult))
                step(nc.vector.tensor_tensor(scaled[:, :, :], scaled[:, :, :], summed[:, :, :], ALU.add))

            node_step("n4", {}, None, after_l3a, 0, sums[2])
            node_mlp("mlp3", scaled, D, a["L3_gnn_W1"], a["L3_gnn_b1"], a["L3_gnn_W2"], ACT.Identity, h)
            v, stored = sem("n5_v"), sem("n5_stored")
            with nc.Block() as block:
                @block.vector
                def _(dve):
                    nc.vector.tensor_tensor(scaled[:, :, :], h[:, :, :], over(inv_sqrt), ALU.mult).then_inc(v, 1)

                @block.sync
                def _(sp):
                    sp.wait_ge(v, 1)
                    sp.dma_start(node_rows(feats[3]), scaled[:, :, :]).then_inc(stored, DMA)
                    sp.wait_ge(stored, DMA)

            counted_sum("l3b", feats[3], sums[3], widths[3])

            def after_l3b(dve, step, summed, t, extra, ready, rooted):
                step(nc.vector.tensor_tensor(summed[:, :, :], summed[:, :, :], over(inv_sqrt), ALU.mult))
                step(nc.vector.tensor_tensor(h[:, :, :], h[:, :, :], over(inv_deg), ALU.mult))
                step(nc.vector.tensor_tensor(h[:, :, :], h[:, :, :], summed[:, :, :], ALU.add))
                step(nc.vector.tensor_tensor(h[:, :, :], h[:, :, :], extra["b2"][:, :].unsqueeze(1).to_broadcast([LANES, PER, D]), ALU.add))
                step(nc.vector.tensor_scalar(h[:, :, :], h[:, :, :], 0.0, None, ALU.max))
                step(nc.vector.tensor_tensor(x[:, :, :], x[:, :, :], h[:, :, :], ALU.add))

            node_step("n6", {"b2": ((LANES, D), spread(a["L3_gnn_b2"]))}, (out.rearrange("(p j) f -> p j f", p=LANES), x), after_l3b,
                      0, sums[3])
    return nc



def kernel(**inputs):
    import concourse.bacc as bacc
    from concourse.bass_utils import run_bass_kernel_spmd

    n_nodes, n_edges = inputs["x"].shape[0], inputs["src"].shape[0]
    groups = n_edges // GROUP
    arrays = {name: np.ascontiguousarray(value) for name, value in inputs.items()}
    for name in ("src", "dst", "edge_weight"):
        arrays[name] = arrays[name].reshape(groups, P, TILES)
    arrays["edge_attr_16"] = np.ascontiguousarray(
        arrays["edge_attr_16"].reshape(groups, P, TILES, DE).transpose(0, 3, 2, 1)).reshape(groups, DE, GROUP)
    nc = bacc.Bacc("TRN2", target_bir_lowering=False, num_devices=1)
    aps = {name: nc.dram_tensor(f"in_{name}", value.shape, mybir.dt.from_np(value.dtype), kind="ExternalInput").ap()
           for name, value in arrays.items()}
    out = nc.dram_tensor("out", (n_nodes, D), F32, kind="ExternalOutput").ap()
    build(nc, aps, out, n_nodes, n_edges)
    result = run_bass_kernel_spmd(nc, [{f"in_{name}": value for name, value in arrays.items()}], core_ids=[0])
    return result.results[0]["out"]
```

```python
from contextlib import ExitStack

import numpy as np
import concourse.bass as bass
from concourse import mybir

F32 = mybir.dt.float32
BF16 = mybir.dt.bfloat16
FP8 = mybir.dt.float8e4
I32 = mybir.dt.int32
ALU = mybir.AluOpType
ACT = mybir.ActivationFunctionType
AX = mybir.AxisListType.X

P = 128
TILES = 25
GROUP = P * TILES
CHUNK = 5
CHUNKS = TILES // CHUNK
COLS = CHUNK * P
BANK = 512
D = 32
DE = 16
H = 64
WINDOW = P - DE
LANES = 125
EPS = 1e-5
SPAN = 512
SPAN_CHUNKS = 5 * CHUNKS
MOST = 16
PARTS = 3
REC = PARTS * D + 2
WORDS = REC // 2
SPLIT = PARTS * D + 1
DMA = 16


def build(nc, a, out, n_nodes, n_edges):
    PER = n_nodes // LANES
    NG = n_edges // GROUP
    PAIRS = (NG - 1) // 2
    assert PER * LANES == n_nodes and NG * GROUP == n_edges and NG % 2 == 1 and NG <= P
    ROWS = -(-(n_nodes + SPAN) // P) * P
    FILL = ROWS // P
    NC = NG * CHUNKS
    SPANS = max(NC // SPAN_CHUNKS, 1)
    assert SPANS % 2 == 1
    BLOCKS = -(-n_nodes // P)
    assert BLOCKS % 2 == 0 and BLOCKS * CHUNK <= BANK
    even = (NC - (SPANS - 1) * SPAN_CHUNKS) * COLS * P / n_nodes
    DEEP = min(int(-(-(even + 6.5 * even ** 0.5) // P)), 2)
    CAPACITY = DEEP * P
    STRIDE = CAPACITY * SPANS
    RECORDS = BLOCKS * STRIDE
    PIECES = max(d for d in range(1, 8) if BLOCKS % d == 0)
    PIECE = BLOCKS // PIECES

    def dram(name, shape, dt=F32):
        return nc.dram_tensor(name, shape, dt).ap()

    src_rows = dram("src_rows", [NG, TILES, P])
    src_cols = dram("src_cols", [NG, P, TILES])
    local_rows = dram("local_rows", [NG, TILES, P], BF16)
    local_cols = dram("local_cols", [NG, P, TILES])
    dst_rows = dram("dst_rows", [NG, TILES, P])
    dst_cols = dram("dst_cols", [NG, P, TILES])
    bases = dram("bases", [NG, 1], I32)
    spans = dram("spans", [NG, 1])
    pre_src = dram("pre_src", [n_nodes, P])
    pre_dst = dram("pre_dst", [n_nodes + P, P])
    bin_cols = dram("bin_cols", [NG, P, TILES])
    start_cols = dram("start_cols", [NG, P, TILES])
    place_cols = dram("place_cols", [NG, P, TILES, 2])
    chunk_ends = [dram(f"chunk_{n}", [NG, CHUNKS]) for n in ("low", "high")]
    chunk_base = dram("chunk_base", [NG, CHUNKS])
    records = dram("records", [RECORDS + COLS, WORDS])
    HALVES = [(0, SPANS // 2), (SPANS // 2, SPANS)] if SPANS > 1 else [(0, 1)]
    counts = [dram(f"counts{lo}", [hi - lo, P, BLOCKS, SPAN // 4]) for lo, hi in HALVES]
    local_table = dram("local_table", [BLOCKS, P, DEEP * SPANS * 2])
    row_edges = dram("row_edges", [P, 1])
    worst_rank = dram("worst_rank", [P, CHUNK])
    feats = [dram(f"feats{n}", [BLOCKS * P, D]) for n in range(4)]
    widths = [D, D + 1, D, D]
    sums = [dram(f"sums{n}", [ROWS, w]) for n, w in enumerate(widths)]
    fwd_sum = dram("fwd_sum", [ROWS, D])
    fwd_general = dram("fwd_general", [ROWS, D])
    bwd_sum = dram("bwd_sum", [ROWS, D])

    ctx = ExitStack()
    with ctx:
        def sb(name, shape, dt=F32, c=ctx):
            return c.enter_context(nc.sbuf_tensor(name, shape, dt))

        def sem(name, c=ctx):
            return c.enter_context(nc.semaphore(name))

        def cleared(sems):
            with nc.Block() as block:
                @block.sync
                def _(sp):
                    for s in sems:
                        sp.sem_clear(s)

        x = sb("x", [LANES, PER, D])
        h = sb("h", [LANES, PER, D])
        identity = sb("identity", [P, P])
        column = sb("column", [P, P])
        row_id = sb("row_id", [P, 1])
        before = sb("before", [P, P])
        spare = sb("spare", [P, 1])
        spare_record = sb("spare_record", [P, CHUNK])
        column_b = sb("column_b", [P, SPAN], BF16)
        column_s = sb("column_s", [P, P, DEEP * SPANS], BF16)
        gather_parts = sb("gather_parts", [SPLIT, D + 1])
        behind = sb("behind", [P, P], BF16)
        ones = sb("ones", [P, P], BF16)
        ones_f = sb("ones_f", [1, P])
        span_no = sb("span_no", [P, NC])
        keep = sb("keep", [1, NC])
        span_row = sb("span_row", [1, SPANS], I32)
        worst = sb("worst", [P, CHUNK])
        base_row = sb("base_row", [1, NG], I32)
        flag = sb("flag", [1, 1], I32)
        all_fit = sb("all_fit", [1, 1], I32)
        dense = sb("dense", [1, 1], I32)
        inv_deg = sb("inv_deg", [LANES, PER])
        inv_sqrt = sb("inv_sqrt", [LANES, PER])

        class Chain:

            def __init__(self, eng, s):
                self.eng, self.s, self.n = eng, s, 0

            def __call__(self, ins):
                self.n += 1
                ins.then_inc(self.s, 1)
                self.eng.wait_ge(self.s, self.n)

        QUAD = 4
        TURNS = PER // QUAD
        assert TURNS * QUAD == PER
        EARLY = next(n for n in (5, 1) if TURNS % n == 0)
        EARLY_RECORDS = RECORDS // 4
        SHARE = (RECORDS - EARLY_RECORDS) // P // TURNS
        assert EARLY_RECORDS * 4 == RECORDS and EARLY_RECORDS + SHARE * P * TURNS == RECORDS
        EMPTY = max(n for n in range(1, 51) if SHARE % n == 0 and EARLY_RECORDS % (EARLY * P * n) == 0)

        def emptying(first, count):
            return (records[bass.ds(first, count)].rearrange("(p n r) c -> p n (r c)", p=P, r=EMPTY),
                    empty.ap().bitcast(F32).to_broadcast([P, count // (P * EMPTY), EMPTY * WORDS]))

        empty = sb("empty", [P, 1, EMPTY * REC], BF16)
        emptied = sem("emptied")
        with ExitStack() as c:
            zero = sb("zero", [P, FILL * (D + 1)], c=c)
            ints = sb("ints", [P, SPAN], I32, c=c)
            column_f = sb("column_f", [P, SPAN], c=c)
            span_i = sb("span_i", [P, NC], I32, c=c)
            z_ready, filled, made, v = (sem(n) for n in ("z_ready", "filled", "made", "const_v"))
            IOTAS = 3 + (SPANS > 1)
            with nc.Block() as block:
                @block.vector
                def _(dve):
                    dve.memset(zero[:, :], 0.0).then_inc(z_ready, 1)
                    dve.memset(empty[:, :, :], -1.0).then_inc(z_ready, 1)
                    step = Chain(dve, v)
                    step(nc.vector.memset(ones[:, :], 1.0))
                    step(nc.vector.memset(ones_f[:, :], 1.0))
                    step(nc.vector.memset(worst[:, :], 0.0))
                    step(nc.vector.memset(keep[:, :], 1.0))
                    if SPANS > 1:
                        step(nc.vector.memset(keep[:, SPAN_CHUNKS - 1:SPAN_CHUNKS * (SPANS - 1):SPAN_CHUNKS], 0.0))
                    dve.wait_ge(made, IOTAS)
                    step(nc.vector.tensor_copy(column_f[:, :], ints[:, :]))
                    step(nc.vector.tensor_scalar(column_b[:, :], column_f[:, :], -SPAN / 2, None, ALU.add))
                    step(nc.vector.tensor_copy(span_no[:, :], span_i[:, :]))
                    step(nc.vector.tensor_copy(column[:, :], ints[:, 0:P]))
                    step(nc.vector.tensor_copy(column_s[:, :, :], column[:, :].unsqueeze(2).to_broadcast([P, P, DEEP * SPANS])))
                    step(nc.vector.tensor_copy(row_id[:, :], spare.ap().bitcast(I32)))
                    step(nc.vector.tensor_scalar(before[:, :], column[:, :], row_id[:, 0:1], None, ALU.is_lt))
                    step(nc.vector.tensor_scalar(identity[:, :], column[:, :], row_id[:, 0:1], None, ALU.is_equal))
                    step(nc.vector.memset(gather_parts[:, :], 0.0))
                    for n in range(PARTS):
                        rows = slice(n * D, (n + 1) * D)
                        step(nc.vector.tensor_copy(gather_parts[rows, 0:D], identity[rows, rows]))
                    step(nc.vector.memset(gather_parts[PARTS * D:SPLIT, D:D + 1], 1.0))
                    step(nc.vector.tensor_scalar(behind[:, :], column[:, :], row_id[:, 0:1], None, ALU.is_gt))
                    step(nc.vector.tensor_scalar(spare[:, :], row_id[:, :], float(n_nodes), None, ALU.add))
                    for t in range(CHUNK):
                        step(nc.vector.tensor_scalar(spare_record[:, t:t + 1], row_id[:, :], float(RECORDS + t * P), None, ALU.add))

                @block.gpsimd
                def _(pool):
                    head = (SPANS - 1) * SPAN_CHUNKS
                    if head:
                        nc.gpsimd.iota(span_i[:, 0:head], pattern=[[1, SPANS - 1], [0, SPAN_CHUNKS]], base=0, channel_multiplier=0).then_inc(made, 1)
                    nc.gpsimd.iota(span_i[:, head:NC], pattern=[[0, NC - head]], base=SPANS - 1, channel_multiplier=0).then_inc(made, 1)
                    nc.gpsimd.iota(ints[:, :], pattern=[[1, SPAN]], base=0, channel_multiplier=0).then_inc(made, 1)
                    nc.gpsimd.iota(spare.ap().bitcast(I32), pattern=[[1, 1]], base=0, channel_multiplier=1).then_inc(made, 1)

                @block.sync
                def _(sp):
                    sp.wait_ge(z_ready, 2)
                    tables = [(t, D) for t in (fwd_sum, fwd_general, bwd_sum)] + list(zip(sums, widths))
                    for t, w in tables:
                        sp.dma_start(t.rearrange("(p r) c -> p (r c)", p=P), zero[:, 0:FILL * w]).then_inc(filled, DMA)
                    tails = [(pre_dst[n_nodes:n_nodes + P], P)] + [(t[n_nodes:BLOCKS * P], D) for t in feats] * (BLOCKS * P > n_nodes)
                    for t, w in tails:
                        sp.dma_start(t, zero[0:t.shape[0], 0:w]).then_inc(filled, DMA)
                    sp.wait_ge(filled, DMA * (len(tables) + len(tails)))

        with ExitStack() as c:
            def big(name, shape=(NG, P, TILES), dt=F32):
                return sb(name, list(shape), dt, c=c)

            src_i, dst_i = (big(n, dt=I32) for n in ("src_i", "dst_i"))
            src_f, dst_f, loc_f, bin_f = (big(n) for n in ("src_f", "dst_f", "loc_f", "bin_f"))
            bin_i = src_i
            start_f = dst_i.ap().bitcast(F32)
            src_t, dst_t = (big(n, (NG, TILES, P)) for n in ("src_t", "dst_t"))
            loc_t = big("loc_t", (NG, TILES, P), BF16)
            place = sb("place", [NG, P, TILES, 2], c=c)
            low, high = (sb(n, [NG, 1], c=c) for n in ("low", "high"))
            low_i = sb("low_i", [NG, 1], I32, c=c)
            chunk_low, chunk_high, base_c = (sb(n, [NG, CHUNKS], c=c) for n in ("least", "greatest", "base_c"))
            low_row, high_row, base_f = (sb(n, [1, NC], c=c) for n in ("low_row", "high_row", "base_f"))
            span_low, span_high = (sb(n, [1, SPANS], c=c) for n in ("span_low", "span_high"))
            extent = sb("extent", [1, NG], c=c)
            widest, widest_span = (sb(n, [1, 1], c=c) for n in ("widest", "widest_span"))
            loaded, v, stored, back, spanned, based = (
                sem(n) for n in ("idx_loaded", "idx_v", "idx_stored", "idx_back", "idx_spanned", "idx_based"))
            HEAD = (SPANS - 1) * SPAN_CHUNKS
            with nc.Block() as block:
                @block.sync
                def _(sp):
                    sp.dma_start(dst_i[:, :, :], a["dst"]).then_inc(loaded, DMA)
                    sp.dma_start(src_i[:, :, :], a["src"]).then_inc(loaded, DMA)
                    sp.dma_start(x[:, :, :], a["x"].rearrange("(p j) f -> p j f", p=LANES)).then_inc(loaded, DMA)
                    sp.wait_ge(v, 4)
                    for table, tile in zip(chunk_ends, (chunk_low, chunk_high)):
                        sp.dma_start(table, tile[:, :]).then_inc(stored, DMA)
                    sp.wait_ge(stored, 2 * DMA)
                    for table, row in zip(chunk_ends, (low_row, high_row)):
                        sp.dma_start(row[:, :], table.rearrange("g c -> (g c)").rearrange("(o n) -> o n", o=1)).then_inc(back, DMA)
                    sp.wait_ge(spanned, 1)
                    sp.dma_start(chunk_base.rearrange("g c -> (g c)").rearrange("(o n) -> o n", o=1), base_f[:, :]).then_inc(based, DMA)
                    sp.wait_ge(based, DMA)
                    sp.dma_start(base_c[:, :], chunk_base).then_inc(based, DMA)
                    sp.wait_ge(spanned, 2)
                    pairs = [(src_cols, src_f), (src_rows, src_t), (dst_cols, dst_f), (dst_rows, dst_t),
                             (local_cols, loc_f), (local_rows, loc_t), (bin_cols, bin_f), (start_cols, start_f)]
                    for table, tile in pairs:
                        sp.dma_start(table, tile[:, :, :]).then_inc(stored, DMA)
                    sp.dma_start(place_cols.rearrange("g p t w -> g (p t w)"), place[:, :, :, :].rearrange("g p t w -> g (p t w)")).then_inc(stored, DMA)
                    sp.dma_start(bases, low_i[:, :]).then_inc(stored, DMA)
                    sp.dma_start(spans, high[:, :]).then_inc(stored, DMA)
                    sp.wait_ge(stored, DMA * (len(pairs) + 5))
                    sp.dma_start(base_row[:, :], bases.rearrange("g o -> o g")).then_inc(back, DMA)
                    sp.dma_start(extent[:, :], spans.rearrange("g o -> o g")).then_inc(back, DMA)
                    sp.wait_ge(back, 4 * DMA)

                @block.scalar
                def _(act):
                    act.wait_ge(loaded, 3 * DMA)
                    for n in range(EARLY):
                        act.dma_start(*emptying(n * (EARLY_RECORDS // EARLY), EARLY_RECORDS // EARLY)).then_inc(emptied, DMA)

                @block.vector
                def _(dve):
                    step = Chain(dve, v)
                    dve.wait_ge(loaded, 3 * DMA)
                    step(nc.vector.tensor_copy(dst_f[:, :, :], dst_i[:, :, :]))
                    step(nc.vector.tensor_copy(dst_t[:, :, :], dst_f[:, :, :].rearrange("g p t -> g t p")))
                    by_chunk = dst_t[:, :, :].rearrange("g (c k) p -> g c (k p)", c=CHUNKS)
                    step(nc.vector.tensor_reduce(chunk_low[:, :], by_chunk, AX, ALU.min))
                    step(nc.vector.tensor_reduce(chunk_high[:, :], by_chunk, AX, ALU.max))
                    step(nc.vector.tensor_copy(src_f[:, :, :], src_i[:, :, :]))
                    step(nc.vector.tensor_copy(src_t[:, :, :], src_f[:, :, :].rearrange("g p t -> g t p")))
                    step(nc.vector.tensor_reduce(low[:, :], chunk_low[:, :], AX, ALU.min))
                    step(nc.vector.tensor_reduce(high[:, :], chunk_high[:, :], AX, ALU.max))
                    step(nc.vector.tensor_scalar(loc_f[:, :, :], dst_f[:, :, :], low[:, 0:1], None, ALU.subtract))
                    step(nc.vector.tensor_copy(loc_t[:, :, :], loc_f[:, :, :].rearrange("g p t -> g t p")))
                    step(nc.vector.tensor_copy(low_i[:, :], low[:, :]))
                    step(nc.vector.tensor_scalar(high[:, :], high[:, :], low[:, 0:1], None, ALU.subtract))
                    dve.wait_ge(back, 2 * DMA)
                    for row, out_, op in ((low_row, span_low, ALU.min), (high_row, span_high, ALU.max)):
                        if HEAD:
                            step(nc.vector.tensor_reduce(out_[:, 0:SPANS - 1], row[:, 0:HEAD].rearrange("o (s c) -> o s c", s=SPANS - 1), AX, op))
                        step(nc.vector.tensor_reduce(out_[:, SPANS - 1:SPANS], row[:, HEAD:NC], AX, op))
                    if HEAD:
                        step(nc.vector.tensor_copy(base_f[:, 0:HEAD].rearrange("o (s c) -> o s c", s=SPANS - 1),
                                                   span_low[:, 0:SPANS - 1].unsqueeze(2).to_broadcast([1, SPANS - 1, SPAN_CHUNKS])))
                    step(nc.vector.tensor_copy(base_f[:, HEAD:NC], span_low[:, SPANS - 1:SPANS].to_broadcast([1, NC - HEAD])))
                    dve.sem_inc(spanned, 1)
                    step(nc.vector.tensor_copy(span_row[:, :], span_low[:, :]))
                    step(nc.vector.tensor_tensor(span_high[:, :], span_high[:, :], span_low[:, :], ALU.subtract))
                    step(nc.vector.tensor_reduce(widest_span[:, :], span_high[:, :], AX, ALU.max))
                    step(nc.vector.tensor_scalar(widest_span[:, :], widest_span[:, :], float(SPAN), None, ALU.is_lt))
                    step(nc.vector.tensor_single_scalar(bin_i[:, :, :], src_i[:, :, :], P.bit_length() - 1, ALU.arith_shift_right))
                    step(nc.vector.tensor_copy(bin_f[:, :, :], bin_i[:, :, :]))
                    step(nc.vector.tensor_scalar(start_f[:, :, :], bin_f[:, :, :], float(STRIDE), None, ALU.mult))
                    step(nc.vector.scalar_tensor_tensor(out=place[:, :, :, 0], in0=bin_f[:, :, :], scalar=-float(P), in1=src_f[:, :, :],
                                                        op0=ALU.mult, op1=ALU.add))
                    dve.wait_ge(based, 2 * DMA)
                    for m in range(CHUNKS):
                        part = slice(m * CHUNK, (m + 1) * CHUNK)
                        step(nc.vector.tensor_scalar(place[:, :, part, 1], dst_f[:, :, part], base_c[:, m:m + 1], -SPAN / 2, ALU.subtract, ALU.add))
                    dve.sem_inc(spanned, 1)
                    dve.wait_ge(back, 4 * DMA)
                    step(nc.vector.tensor_reduce(widest[:, :], extent[:, :], AX, ALU.max))
                    step(nc.vector.tensor_scalar(widest[:, :], widest[:, :], float(WINDOW), None, ALU.is_lt))
                    step(nc.vector.tensor_tensor(widest[:, :], widest[:, :], widest_span[:, :], ALU.mult))
                    step(nc.vector.tensor_copy(flag[:, :], widest[:, :]))

        def over(ap):
            return ap[:, :].unsqueeze(2).to_broadcast([LANES, PER, D])

        def layernorm(step, act_done, dve_ready, n, t):
            mean, var, xc, sq = t
            step(nc.vector.tensor_reduce(mean[:, :], x[:, :, :], AX, ALU.add))
            step(nc.vector.tensor_scalar(mean[:, :], mean[:, :], 1.0 / D, None, ALU.mult))
            step(nc.vector.tensor_tensor(xc[:, :, :], x[:, :, :], over(mean), ALU.subtract))
            step(nc.vector.tensor_tensor(sq[:, :, :], xc[:, :, :], xc[:, :, :], ALU.mult))
            step(nc.vector.tensor_reduce(var[:, :], sq[:, :, :], AX, ALU.add))
            step(nc.vector.tensor_scalar(var[:, :], var[:, :], 1.0 / D, EPS, ALU.mult, ALU.add))
            step.eng.sem_inc(dve_ready, 1)
            step.eng.wait_ge(act_done, n)
            step(nc.vector.reciprocal(var[:, :], var[:, :]))
            step(nc.vector.tensor_tensor(xc[:, :, :], xc[:, :, :], over(var), ALU.mult))
            step(nc.vector.tensor_scalar(h[:, :, :], xc[:, :, :], 0.0, None, ALU.max))

        def root(act, dve_ready, act_done, ap, n):
            act.wait_ge(dve_ready, n)
            nc.scalar.activation(ap, ap, ACT.Sqrt).then_inc(act_done, 1)

        def scratch(c, tag):
            return (sb(f"mean{tag}", [LANES, PER], c=c), sb(f"var{tag}", [LANES, PER], c=c),
                    sb(f"xc{tag}", [LANES, PER, D], c=c), sb(f"sq{tag}", [LANES, PER, D], c=c))

        with ExitStack() as c:
            t = scratch(c, "0")
            w_pre = sb("w_pre", [D, 2 * P], c=c)
            cols = sb("cols0", [LANES, QUAD, D], c=c)
            feat = sb("feat0", [D, QUAD * LANES], c=c)
            rows = [sb(f"rows0{q}", [LANES, QUAD, 2 * P], c=c) for q in range(2)]
            p_t = c.enter_context(nc.psum_tensor("p_t0", [D, BANK], F32))
            p_o = c.enter_context(nc.psum_tensor("p_o0", [LANES, QUAD, 2 * P], F32))
            names = ("n0_w", "n0_v", "n0_ready", "n0_root", "n0_cols", "n0_turned", "n0_feat", "n0_product", "n0_rows", "n0_turn")
            s_st = [sem(f"n0_stored{q}") for q in range(2)]
            UNITS = next(n for n in (5, 1) if TURNS % n == 0)
            w_in, v, ready, rooted, s_cols, s_tr, s_feat, s_mm, s_out, s_turn = (sem(n) for n in names)
            USES = [(UNITS + 1) // 2, UNITS // 2]

            def wait_slot(eng, i, u):
                eng.wait_ge(s_st[u % 2], i * (USES[u % 2] * 2 * DMA) + (u // 2 + 1) * 2 * DMA)

            with nc.Block() as block:
                @block.sync
                def _(sp):
                    w1f, w1b = a["L0_gnn_W1f"], a["L0_gnn_W1b"]
                    for n, part in enumerate((w1f[D:2 * D], w1b[0:D], w1f[0:D], w1b[D:2 * D])):
                        sp.dma_start(w_pre[:, n * H:(n + 1) * H], part).then_inc(w_in, DMA)
                    with sp.Fori(0, TURNS // UNITS) as i:
                        for u in range(UNITS):
                            sp.wait_ge(s_out, i * (2 * UNITS) + (2 * u + 4))
                            sp.sem_inc(s_turn, 1)
                            for n, table in enumerate((pre_src, pre_dst)):
                                sp.dma_start(table[0:n_nodes].rearrange("(p j) f -> p j f", p=LANES)[:, bass.ds(i * (UNITS * QUAD) + u * QUAD, QUAD)],
                                             rows[u % 2][:, :, n * P:(n + 1) * P]).then_inc(s_st[u % 2], DMA)
                    for q in range(2):
                        sp.wait_ge(s_st[q], (1 + TURNS // UNITS * USES[q]) * 2 * DMA)

                @block.vector
                def _(dve):
                    for q in range(2):
                        dve.sem_inc(s_st[q], 2 * DMA)
                    step = Chain(dve, v)
                    layernorm(step, rooted, ready, 1, t)
                    with dve.Fori(0, TURNS // UNITS) as i:
                        for u in range(UNITS):
                            nc.vector.tensor_copy(cols[:, :, :], h[:, bass.ds(i * (UNITS * QUAD) + u * QUAD, QUAD), :]).then_inc(s_cols, 1)
                            dve.wait_ge(s_tr, i * UNITS + (u + 1))
                            nc.vector.tensor_copy(feat[:, :], p_t[:, 0:QUAD * LANES]).then_inc(s_feat, 1)
                            dve.wait_ge(s_mm, i * UNITS + (u + 1))
                            wait_slot(dve, i, u)
                            nc.vector.tensor_copy(rows[u % 2][:, 0:2, :], p_o[:, 0:2, :]).then_inc(s_out, 1)

                @block.scalar
                def _(act):
                    root(act, ready, rooted, t[1][:, :], 1)
                    with act.Fori(0, TURNS // UNITS) as i:
                        for u in range(UNITS):
                            act.dma_start(*emptying((i * UNITS + u) * (SHARE * P) + EARLY_RECORDS, SHARE * P)).then_inc(emptied, DMA)
                            act.wait_ge(s_mm, i * UNITS + (u + 1))
                            wait_slot(act, i, u)
                            nc.scalar.activation(rows[u % 2][:, 2:4, :], p_o[:, 2:4, :], ACT.Copy).then_inc(s_out, 1)

                @block.tensor
                def _(pe):
                    pe.wait_ge(w_in, 4 * DMA)
                    pe.sem_inc(s_out, 2)
                    with pe.Fori(0, TURNS) as i:
                        pe.wait_ge(s_cols, i + 1)
                        for q in range(QUAD):
                            last = nc.tensor.transpose(p_t[:, q * LANES:(q + 1) * LANES], cols[:, q, :], identity[0:LANES, 0:LANES])
                        last.then_inc(s_tr, 1)
                        pe.wait_ge(s_feat, i + 1)
                        pe.wait_ge(s_out, i * 2 + 2)
                        for q in range(QUAD):
                            last = nc.tensor.matmul(p_o[:, q, :], feat[:, q * LANES:(q + 1) * LANES], w_pre[:, :],
                                                    start=True, stop=True)
                        last.then_inc(s_mm, 1)

        def node_mlp(tag, given, k, w1, b1, w2, fn, taken):
            UNITS = next(n for n in (5, 1) if TURNS % n == 0)
            with ExitStack() as c:
                w1_s = sb(f"w1_{tag}", [k, H], c=c)
                w2_s = sb(f"w2_{tag}", [H, D], c=c)
                b1_s = sb(f"b1_{tag}", [H, 1], c=c)
                cols = [sb(f"cols_{tag}{q}", [LANES, QUAD, k], c=c) for q in range(2)]
                feat = [sb(f"feat_{tag}{q}", [k, QUAD * LANES], c=c) for q in range(2)]
                hid = [sb(f"hid_{tag}{q}", [H, QUAD * LANES], c=c) for q in range(2)]
                p_t = [c.enter_context(nc.psum_tensor(f"p_t_{tag}{q}", [k, BANK], F32)) for q in range(2)]
                p_h = [c.enter_context(nc.psum_tensor(f"p_h_{tag}{q}", [H, BANK], F32)) for q in range(2)]
                p_o = [c.enter_context(nc.psum_tensor(f"p_o_{tag}{q}", [LANES, BANK], F32)) for q in range(2)]
                names = ("weights", "cols", "turned", "feat", "hidden", "activated", "product", "taken", "turn")
                w_in, s_cols, s_tr, s_feat, s_hid, s_act, s_mm, s_out, s_turn = (sem(f"{tag}_{n}") for n in names)

                def staggered(steps):
                    for u in range(UNITS + len(steps) - 1):
                        for n, step in enumerate(steps):
                            if 0 <= u - n < UNITS:
                                step(u - n)

                with nc.Block() as block:
                    @block.sync
                    def _(sp):
                        sp.dma_start(w1_s[:, :], w1).then_inc(w_in, DMA)
                        sp.dma_start(w2_s[:, :], w2).then_inc(w_in, DMA)
                        sp.dma_start(b1_s[:, :], b1.rearrange("(h o) -> h o", o=1)).then_inc(w_in, DMA)

                    @block.vector
                    def _(dve):
                        with dve.Fori(0, TURNS // UNITS) as i:
                            def copy_cols(u):
                                nc.vector.tensor_copy(cols[u % 2][:, :, :], given[:, bass.ds(i * (UNITS * QUAD) + u * QUAD, QUAD), :]).then_inc(s_cols, 1)

                            def copy_features(u):
                                dve.wait_ge(s_tr, i * UNITS + (u + 1))
                                nc.vector.tensor_copy(feat[u % 2][:, :], p_t[u % 2][:, 0:QUAD * LANES]).then_inc(s_feat, 1)

                            def copy_result(u):
                                dve.wait_ge(s_mm, i * UNITS + (u + 1))
                                nc.vector.tensor_copy(taken[:, bass.ds(i * (UNITS * QUAD) + u * QUAD, QUAD), :],
                                                      p_o[u % 2][:, 0:QUAD * D].rearrange("p (q f) -> p q f", q=QUAD)).then_inc(s_out, 1)

                            staggered((copy_cols, copy_features, copy_result))

                    @block.scalar
                    def _(act):
                        act.wait_ge(w_in, 3 * DMA)
                        with act.Fori(0, TURNS // UNITS) as i:
                            for u in range(UNITS):
                                act.wait_ge(s_hid, i * UNITS + (u + 1))
                                nc.scalar.activation(hid[u % 2][:, :], p_h[u % 2][:, 0:QUAD * LANES], fn, bias=b1_s[:, 0:1]).then_inc(s_act, 1)

                    @block.tensor
                    def _(pe):
                        pe.wait_ge(w_in, 3 * DMA)
                        pe.sem_inc(s_out, 2)
                        with pe.Fori(0, TURNS // UNITS) as i:
                            def turn_cols(u):
                                pe.wait_ge(s_cols, i * UNITS + (u + 1))
                                pe.sem_inc(s_turn, 1)
                                for q in range(QUAD):
                                    last = nc.tensor.transpose(p_t[u % 2][:, q * LANES:(q + 1) * LANES], cols[u % 2][:, q, :], identity[0:LANES, 0:LANES])
                                last.then_inc(s_tr, 1)

                            def first_product(u):
                                pe.wait_ge(s_feat, i * UNITS + (u + 1))
                                pe.sem_inc(s_turn, 1)
                                nc.tensor.matmul(p_h[u % 2][:, 0:QUAD * LANES], w1_s[:, :], feat[u % 2][:, :], start=True, stop=True).then_inc(s_hid, 1)

                            def second_product(u):
                                pe.wait_ge(s_act, i * UNITS + (u + 1))
                                pe.wait_ge(s_out, i * UNITS + (u + 1))
                                pe.sem_inc(s_turn, 1)
                                for q in range(QUAD):
                                    last = nc.tensor.matmul(p_o[u % 2][:, q * D:(q + 1) * D], hid[u % 2][:, q * LANES:(q + 1) * LANES], w2_s[:, :],
                                                            start=True, stop=True)
                                last.then_inc(s_mm, 1)

                            staggered((turn_cols, first_product, second_product))

        def window_rows(sp, table, base):
            return table[bass.ds(base, WINDOW)]

        def fetch_base(eng, g):
            at = base_row[0:1, g:g + 1] if isinstance(g, int) else base_row[0:1, bass.ds(g, 1)]
            return eng.value_load(at, min_val=0, max_val=n_nodes - 1)

        def at_group(table, g):
            return table[g] if isinstance(g, int) else table[bass.ds(g, 1)].rearrange("o p t -> (o p) t")

        def row_group(table, g, first=0, count=TILES):
            flat = table.rearrange("g t p -> g (t p)")
            one = flat[g:g + 1] if isinstance(g, int) else flat[bass.ds(g, 1)]
            return one[:, first * P:(first + count) * P].to_broadcast([P, count * P])

        def both_paths(eng, which, fast, general):
            fits = eng.value_load(which[0:1, 0:1], min_val=0, max_val=1)
            with eng.If(fits > 0):
                fast()
            with eng.Else():
                general()

        def merge_steps(dve, s, count, cols, row, same, earlier, twin, away, to_row, rest=6):
            def add(ins, n):
                ins.then_inc(s, 1)
                dve.wait_ge(s, count + n)
            shape = [P, CHUNK, P]
            add(nc.vector.tensor_tensor(same[:, :, :], row[:, :, :], cols.unsqueeze(2).to_broadcast(shape), ALU.is_equal), 1)
            add(nc.vector.tensor_tensor(earlier[:, :, :], same[:, :, :], before[:, :].unsqueeze(1).to_broadcast(shape), ALU.mult), 2)
            add(nc.vector.tensor_reduce(twin[:, :], earlier[:, :, :], AX, ALU.add), 3)
            add(nc.vector.tensor_scalar(away[:, :], cols, -1.0, spare[:, 0:1], ALU.mult, ALU.add), 4)
            add(nc.vector.scalar_tensor_tensor(out=away[:, :], in0=twin[:, :], scalar=0.0, in1=away[:, :], op0=ALU.is_gt, op1=ALU.mult), 5)
            add(nc.vector.tensor_tensor(to_row[:, :], away[:, :], cols, ALU.add), 6)

        def general_sum(c, tag, table, total, width, weights):
            src_i = sb(f"{tag}_g_src", [P, CHUNK], I32, c=c)
            cols = sb(f"{tag}_g_cols", [P, CHUNK], c=c)
            wgt = sb(f"{tag}_g_wgt", [P, CHUNK], c=c)
            got = sb(f"{tag}_g_got", [P, CHUNK, D + 1], c=c)
            same_row = sb(f"{tag}_g_same_row", [P, CHUNK, P], c=c)
            same = sb(f"{tag}_g_same", [P, CHUNK, P], c=c)
            earlier = sb(f"{tag}_g_earlier", [P, CHUNK, P], c=c)
            twin = sb(f"{tag}_g_twin", [P, CHUNK], c=c)
            away = sb(f"{tag}_g_away", [P, CHUNK], c=c)
            to_row = sb(f"{tag}_g_to_row", [P, CHUNK], I32, c=c)
            merged = sb(f"{tag}_g_merged", [P, CHUNK, width], c=c)
            p_merged = c.enter_context(nc.psum_tensor(f"{tag}_g_p", [P, BANK], F32))
            g_got, g_added = sem(f"{tag}_g_got"), sem(f"{tag}_g_added")
            g_in, g_step, g_merged, g_copied, g_free, g_turn = stage = [
                sem(f"{tag}_g_{n}", c) for n in ("in", "step", "merged", "copied", "free", "turn")]
            loads = 4 if weights is not None else 3
            steps = 8 if weights is not None else 7

            def sync(sp):
                with sp.Fori(0, NG) as g:
                    for m in range(CHUNKS):
                        part = slice(m * CHUNK, (m + 1) * CHUNK)
                        sp.wait_ge(g_free, g * CHUNKS + (m + 1))
                        sp.dma_start(src_i[:, :], at_group(a["src"], g)[:, part]).then_inc(g_in, DMA)
                        sp.dma_start(cols[:, :], at_group(dst_cols, g)[:, part]).then_inc(g_in, DMA)
                        sp.dma_start(flat(same_row[:, :, :]), row_group(dst_rows, g, m * CHUNK, CHUNK)).then_inc(g_in, DMA)
                        if weights is not None:
                            sp.dma_start(wgt[:, :], at_group(weights, g)[:, part]).then_inc(g_in, DMA)

            def gpsimd(pool):
                pool.sem_inc(g_free, 1)
                with pool.Fori(0, NG) as g:
                    for m in range(CHUNKS):
                        n = g * CHUNKS + m
                        pool.wait_ge(g_in, n * (loads * DMA) + loads * DMA)
                        pool.sem_inc(g_turn, 1)
                        for t in range(CHUNK):
                            nc.gpsimd.indirect_dma_start(
                                out=got[:, t, 0:D], out_offset=None, in_=table,
                                in_offset=bass.IndirectOffsetOnAxis(ap=src_i[:, t:t + 1], axis=0)).then_inc(g_got, DMA)
                        pool.wait_ge(g_copied, n + 1)
                        pool.sem_inc(g_turn, 1)
                        for t in range(CHUNK):
                            nc.gpsimd.indirect_dma_start(
                                out=total, out_offset=bass.IndirectOffsetOnAxis(ap=to_row[:, t:t + 1], axis=0),
                                in_=merged[:, t, :], in_offset=None, compute_op=ALU.add).then_inc(g_added, DMA)
                            pool.wait_ge(g_added, n * (CHUNK * DMA) + (t + 1) * DMA)
                            pool.sem_inc(g_turn, 1)
                        pool.sem_inc(g_free, 1)

            def vector(dve):
                with dve.Fori(0, NG) as g:
                    for m in range(CHUNKS):
                        n = g * CHUNKS + m
                        dve.wait_ge(g_in, n * (loads * DMA) + loads * DMA)
                        nc.vector.memset(got[:, :, D:D + 1], 1.0).then_inc(g_step, 1)
                        merge_steps(dve, g_step, n * steps + 1, cols[:, :], same_row, same, earlier, twin, away, to_row)
                        if weights is not None:
                            dve.wait_ge(g_got, n * (CHUNK * DMA) + CHUNK * DMA)
                            nc.vector.tensor_tensor(got[:, :, 0:D], got[:, :, 0:D],
                                                    wgt[:, :].unsqueeze(2).to_broadcast([P, CHUNK, D]), ALU.mult).then_inc(g_step, 1)
                        dve.wait_ge(g_merged, n + 1)
                        nc.vector.tensor_copy(merged[:, :, :], p_merged[:, 0:CHUNK * width].rearrange(
                            "p (t w) -> p t w", t=CHUNK)).then_inc(g_copied, 1)

            def tensor(pe):
                with pe.Fori(0, NC) as n:
                    pe.wait_ge(g_got, n * (CHUNK * DMA) + CHUNK * DMA)
                    pe.wait_ge(g_step, n * steps + steps)
                    for t in range(CHUNK):
                        last = nc.tensor.matmul(p_merged[:, t * width:(t + 1) * width], same[:, t, :],
                                                got[:, t, 0:width], start=True, stop=True)
                    last.then_inc(g_merged, 1)

            def scalar(act):
                act.sem_inc(g_turn, 1)

            return sync, gpsimd, vector, tensor, scalar, stage

        def weighted_sum(tag, table, total, weights):
            with ExitStack() as c:
                LOADS = 3
                src_i = [sb(f"{tag}_src{k}", [P, TILES], I32, c=c) for k in range(2)]
                local = [sb(f"{tag}_local{k}", [P, TILES], c=c) for k in range(2)]
                wgt = [sb(f"{tag}_wgt{k}", [P, TILES], c=c) for k in range(2)]
                got = [sb(f"{tag}_got{k}", [P, TILES, D], c=c) for k in range(2)]
                msg = [sb(f"{tag}_msg{k}", [P, TILES, D], c=c) for k in range(2)]
                hot = [sb(f"{tag}_hot{k}", [P, TILES, WINDOW], c=c) for k in range(2)]
                old = [sb(f"{tag}_old{k}", [WINDOW, D], c=c) for k in range(2)]
                new = [sb(f"{tag}_new{k}", [WINDOW, D], c=c) for k in range(2)]
                p_sum = [c.enter_context(nc.psum_tensor(f"{tag}_p{k}", [WINDOW, BANK], F32)) for k in range(2)]
                s_got = [sem(f"{tag}_got{k}") for k in range(2)]
                s_in, s_hot, s_weighed, s_summed, s_used, s_old = ([sem(f"{tag}_{n}{k}", c) for k in range(2)]
                                                                  for n in ("in", "hot", "weighed", "summed", "used", "old"))
                s_stored, s_turn = sem(f"{tag}_stored", c), sem(f"{tag}_turn", c)
                BIN = DEEP * SPANS
                RING = 5 if SPANS % 5 == 0 else 2
                place = [sb(f"{tag}_place{k}", [P, DEEP, SPANS, 2], c=c) for k in range(2)]
                source = [sb(f"{tag}_source{k}", [P, DEEP * SPANS], BF16, c=c) for k in range(2)]
                from_hot = [sb(f"{tag}_from_hot{k}", [P, P, DEEP * SPANS], BF16, c=c) for k in range(2)]
                to_hot = [sb(f"{tag}_to_hot{r}", [P, DEEP, SPAN], BF16, c=c) for r in range(RING)]
                counted = [sb(f"{tag}_counted{k}", [P, SPANS, SPAN], FP8, c=c) for k in range(2)]
                edges = [sb(f"{tag}_edges{k}", [P, SPANS], c=c) for k in range(2)]
                most_edges = sb(f"{tag}_most_edges", [P, SPANS], c=c)
                most, row_most, held = sb(f"{tag}_most", [P, 1], c=c), sb(f"{tag}_row_most", [1, P], c=c), sb(f"{tag}_held", [1, 1], c=c)
                s_most, s_row_most, s_noted = (sem(f"{tag}_{n}", c) for n in ("s_most", "s_row_most", "noted"))
                p_count = [c.enter_context(nc.psum_tensor(f"{tag}_p_count{r}", [P, BANK], F32)) for r in range(RING)]
                s_place, s_kept = ([sem(f"{tag}_{n}{k}", c) for k in range(2)] for n in ("place", "kept"))
                s_from, s_to, s_count, s_copied = (sem(f"{tag}_{n}", c) for n in ("from", "to", "count", "copied"))
                g_sync, g_gpsimd, g_vector, g_tensor, g_scalar, g_stage = general_sum(c, tag, table, total, D, weights)
                half = BLOCKS // 2
                KEPT = len(HALVES) * DMA
                BOTH = min(half, PAIRS)

                with nc.Block() as block:
                    @block.sync
                    def _(sp):
                        def load(k, g, i):
                            sp.wait_ge(s_weighed[k], i + 1)
                            sp.dma_start(src_i[k][:, :], at_group(a["src"], g)).then_inc(s_in[k], DMA)
                            sp.dma_start(local[k][:, :], at_group(local_cols, g)).then_inc(s_in[k], DMA)
                            sp.dma_start(wgt[k][:, :], at_group(weights, g)).then_inc(s_in[k], DMA)

                        def add_window(k, g, i):
                            base = fetch_base(sp, g)
                            rows = window_rows(sp, total, base)
                            sp.dma_start(old[k][:, :], rows).then_inc(s_old[k], DMA)
                            sp.wait_ge(s_used[k], i + 2)
                            sp.dma_start(rows, new[k][:, :]).then_inc(s_stored, DMA)
                            sp.wait_ge(s_stored, (g + 1) * DMA)
                            sp.sem_inc(s_turn, 1)

                        def load_block(k, b, turn):
                            sp.wait_ge(s_to, (turn + 1) * SPANS)
                            table = local_table[b] if isinstance(b, int) else local_table[bass.ds(b % BLOCKS, 1)].rearrange("o p n -> (o p) n")
                            sp.dma_start(place[k][:, :, :, :].rearrange("p d s w -> p (d s w)"), table).then_inc(s_place[k], DMA)

                        def fast():
                            for k in range(2):
                                load(k, k, 0)
                            load_block(0, 0, 0)

                            def group_turn(k, i):
                                load(k, (i * 2 + (k + 2)) % NG, i + 1)
                                add_window(k, i * 2 + k, i)

                            with sp.Fori(0, BOTH) as i:
                                for k in range(2):
                                    load_block(1 - k, i * 2 + (k + 1), i * 2 + (k + 1))
                                    group_turn(k, i)
                            if BOTH < half:
                                with sp.Fori(BOTH, half) as i:
                                    for k in range(2):
                                        load_block(1 - k, i * 2 + (k + 1), i * 2 + (k + 1))
                            if BOTH < PAIRS:
                                with sp.Fori(BOTH, PAIRS) as i:
                                    for k in range(2):
                                        group_turn(k, i)
                            add_window(0, NG - 1, PAIRS)
                            sp.wait_ge(s_in[1], (PAIRS + 1) * LOADS * DMA)
                            sp.wait_ge(s_place[0], (half + 1) * DMA)
                            sp.wait_ge(s_most, 1)
                            sp.dma_start(row_edges, most[:, :]).then_inc(s_row_most, DMA)
                            sp.wait_ge(s_row_most, DMA)
                            sp.dma_start(row_most[:, :], row_edges.rearrange("p o -> o p")).then_inc(s_row_most, DMA)

                        both_paths(sp, all_fit, fast, lambda: g_sync(sp))

                    @block.gpsimd
                    def _(pool):
                        def gather(k, i):
                            pool.wait_ge(s_in[k], i * (LOADS * DMA) + LOADS * DMA)
                            pool.sem_inc(s_turn, 1)
                            for t in range(TILES):
                                nc.gpsimd.indirect_dma_start(
                                    out=got[k][:, t, :], out_offset=None, in_=table,
                                    in_offset=bass.IndirectOffsetOnAxis(ap=src_i[k][:, t:t + 1], axis=0)).then_inc(s_got[k], DMA)

                        def fast():
                            with pool.Fori(0, PAIRS) as i:
                                gather(0, i)
                                gather(1, i)
                            gather(0, PAIRS)

                        both_paths(pool, all_fit, fast, lambda: g_gpsimd(pool))

                    @block.vector
                    def _(dve):
                        def one_hot(k, i):
                            dve.wait_ge(s_in[k], i * (LOADS * DMA) + LOADS * DMA)
                            dve.wait_ge(s_summed[k], i + 1)
                            nc.vector.tensor_tensor(
                                hot[k][:, :, :], column[:, 0:WINDOW].unsqueeze(1).to_broadcast([P, TILES, WINDOW]),
                                local[k][:, :].unsqueeze(2).to_broadcast([P, TILES, WINDOW]), ALU.is_equal).then_inc(s_hot[k], 1)

                        def weigh(k, i):
                            dve.wait_ge(s_got[k], i * (TILES * DMA) + TILES * DMA)
                            nc.vector.tensor_tensor(msg[k][:, :, :], got[k][:, :, :],
                                                    wgt[k][:, :].unsqueeze(2).to_broadcast([P, TILES, D]), ALU.mult).then_inc(s_weighed[k], 1)

                        def add_old(k, i):
                            dve.wait_ge(s_summed[k], i + 2)
                            dve.wait_ge(s_old[k], i * DMA + DMA)
                            nc.vector.tensor_tensor(new[k][:, :], p_sum[k][:, 0:D], old[k][:, :], ALU.add).then_inc(s_used[k], 1)

                        def note_edges(k, b):
                            dve.wait_ge(s_copied, b * SPANS + (SPANS + RING))
                            dve.wait_ge(s_noted, b + 3)
                            nc.vector.tensor_tensor(most_edges[:, :], most_edges[:, :], edges[k][:, :], ALU.max).then_inc(s_noted, 1)

                        def one_hot_block(k, b, turn):
                            dve.wait_ge(s_place[k], turn * DMA + DMA)
                            dve.wait_ge(s_count, b * SPANS + RING)
                            nc.vector.tensor_copy(source[k][:, :], place[k][:, :, :, 0].rearrange("p d s -> p (d s)")).then_inc(s_from, 1)
                            note_edges(k, b)
                            dve.wait_ge(s_from, b * 2 + 1)
                            nc.vector.tensor_tensor(from_hot[k][:, :, :], column_s[:, :, :], source[k][:, :].unsqueeze(1).to_broadcast([P, P, BIN]),
                                                    ALU.is_equal).then_inc(s_from, 1)
                            for s in range(SPANS):
                                dve.wait_ge(s_count, b * SPANS + (s + 1))
                                for d in range(DEEP):
                                    last = nc.vector.tensor_scalar(to_hot[(k * SPANS + s) % RING][:, d, :], column_b[:, :],
                                                                   place[k][:, d, s, 1:2], None, ALU.is_equal)
                                last.then_inc(s_to, 1)

                        def fast():
                            dve.sem_inc(s_to, 2 * SPANS)
                            for k in range(2):
                                dve.sem_inc(s_weighed[k], 1)
                            nc.vector.memset(most_edges[:, :], 0.0).then_inc(s_noted, 1)
                            for k in range(2):
                                nc.vector.memset(edges[k][:, :], 0.0).then_inc(s_noted, 1)
                            for k in range(2):
                                dve.sem_inc(s_used[k], 1)
                            one_hot(0, 0)
                            with dve.Fori(0, BOTH) as i:
                                for k in range(2):
                                    weigh(k, i)
                                    one_hot(1 - k, i + k)
                                    one_hot_block(k, i * 2 + k, i)
                                    add_old(k, i)
                            if BOTH < half:
                                with dve.Fori(BOTH, half) as i:
                                    for k in range(2):
                                        one_hot_block(k, i * 2 + k, i)
                            if BOTH < PAIRS:
                                with dve.Fori(BOTH, PAIRS) as i:
                                    for k in range(2):
                                        weigh(k, i)
                                        one_hot(1 - k, i + k)
                                        add_old(k, i)
                            weigh(0, PAIRS)
                            add_old(0, PAIRS)
                            for k in range(2):
                                note_edges(k, BLOCKS + k)
                            dve.wait_ge(s_noted, BLOCKS + 5)
                            step = Chain(dve, s_most)
                            step(nc.vector.tensor_reduce(most[:, :], most_edges[:, :], AX, ALU.max))
                            dve.wait_ge(s_row_most, 2 * DMA)
                            step(nc.vector.tensor_reduce(held[:, :], row_most[:, :], AX, ALU.max))
                            step(nc.vector.tensor_scalar(held[:, :], held[:, :], float(MOST), None, ALU.is_le))
                            step(nc.vector.tensor_copy(dense[:, :], held[:, :]))

                        def general():
                            nc.vector.tensor_copy(dense[:, :], all_fit[:, :])
                            g_vector(dve)

                        both_paths(dve, all_fit, fast, general)

                    @block.scalar
                    def _(act):
                        def copy_block(k, b, turn):
                            act.wait_ge(s_kept[k], turn * KEPT + KEPT)
                            for s in range(SPANS):
                                act.wait_ge(s_count, b * SPANS + (s + 1 + RING))
                                act.sem_inc(s_turn, 1)
                                nc.scalar.activation(counted[k][:, s, :], p_count[(k * SPANS + s) % RING][:, :], ACT.Copy,
                                                     accum_out=edges[k][:, s:s + 1], saturate=True).then_inc(s_copied, 1)
                            act.wait_ge(s_copied, b * SPANS + (3 * SPANS + RING))
                            for table, (lo, hi) in zip(counts, HALVES):
                                act.dma_start(table[:, :, bass.ds(b, 1), :].rearrange("s p o n -> p (s o) n"), counted[k].ap().bitcast(F32)[:, lo:hi, :]).then_inc(s_kept[k], DMA)

                        def fast():
                            act.sem_inc(s_copied, 2 * SPANS + RING)
                            for k in range(2):
                                act.sem_inc(s_kept[k], KEPT)
                            with act.Fori(0, half) as i:
                                for k in range(2):
                                    copy_block(k, i * 2 + k, i)
                            for k in range(2):
                                act.wait_ge(s_kept[k], (half + 1) * KEPT)

                        both_paths(act, all_fit, fast, lambda: g_scalar(act))

                    @block.tensor
                    def _(pe):
                        def sum_group(k, i):
                            pe.wait_ge(s_weighed[k], i + 2)
                            pe.wait_ge(s_hot[k], i + 1)
                            pe.wait_ge(s_used[k], i + 1)
                            for t in range(TILES):
                                last = nc.tensor.matmul(p_sum[k][:, 0:D], hot[k][:, t, :], msg[k][:, t, :],
                                                        start=t == 0, stop=t == TILES - 1)
                            last.then_inc(s_summed[k], 1)

                        def count_block(k, b):
                            pe.wait_ge(s_from, b * 2 + 2)
                            for s in range(SPANS):
                                r = (k * SPANS + s) % RING
                                pe.wait_ge(s_to, b * SPANS + (s + 1 + 2 * SPANS))
                                pe.wait_ge(s_copied, b * SPANS + (s + 1 + 2 * SPANS))
                                for d in range(DEEP):
                                    last = nc.tensor.matmul(p_count[r][:, :], from_hot[k][:, :, d * SPANS + s], to_hot[r][:, d, :],
                                                            start=d == 0, stop=d == DEEP - 1)
                                last.then_inc(s_count, 1)

                        def fast():
                            pe.sem_inc(s_count, RING)
                            for k in range(2):
                                pe.sem_inc(s_summed[k], 1)
                            with pe.Fori(0, BOTH) as i:
                                for k in range(2):
                                    sum_group(k, i)
                                    count_block(k, i * 2 + k)
                            if BOTH < half:
                                with pe.Fori(BOTH, half) as i:
                                    for k in range(2):
                                        count_block(k, i * 2 + k)
                            if BOTH < PAIRS:
                                with pe.Fori(BOTH, PAIRS) as i:
                                    for k in range(2):
                                        sum_group(k, i)
                            sum_group(0, PAIRS)

                        both_paths(pe, all_fit, fast, lambda: g_tensor(pe))
                cleared([*s_in, *s_hot, *s_weighed, *s_summed, *s_used, *s_old, s_stored, s_turn, *s_place, *s_kept, s_from, s_to,
                         s_count, s_copied, s_most, s_row_most, s_noted, *g_stage])

        def counted_sum(tag, table, total, width):
            with ExitStack() as c:
                feat = sb(f"{tag}_feat", [P, BLOCKS, D], c=c)
                parts = sb(f"{tag}_parts", [P, BLOCKS, SPLIT], BF16, c=c)
                piece = [sb(f"{tag}_piece{q}", [P, PIECE, SPAN], FP8, c=c) for q in range(PIECES)]
                wide = sb(f"{tag}_wide", [SPLIT, SPAN], c=c)
                QUARTERS = SPAN // P
                old = sb(f"{tag}_old", [P, QUARTERS, width], c=c)
                new = sb(f"{tag}_new", [P, QUARTERS, width], c=c)
                p_wide = [c.enter_context(nc.psum_tensor(f"{tag}_p_wide{k}", [SPLIT, SPAN], F32)) for k in range(2)]
                p_node = c.enter_context(nc.psum_tensor(f"{tag}_p_node", [P, BANK], F32))
                s_piece = [sem(f"{tag}_piece{q}", c) for q in range(PIECES)]
                s_feat, s_parts, s_used, s_copied, s_node, s_old, s_new, s_stored, s_turn = stage = [
                    sem(f"{tag}_{n}", c) for n in ("feat", "parts", "used", "copied", "node", "old", "new", "stored", "turn")]
                g_sync, g_gpsimd, g_vector, g_tensor, g_scalar, g_stage = general_sum(c, tag, table[0:n_nodes], total, width, None)

                with nc.Block() as block:
                    @block.sync
                    def _(sp):
                        def fast():
                            sp.dma_start(feat[:, :, :], table.rearrange("(b p) f -> p b f", p=P)).then_inc(s_feat, DMA)
                            for span_table, (lo, hi) in zip(counts, HALVES):
                                with sp.Fori(lo, hi) as s:
                                    for q in range(PIECES):
                                        sp.wait_ge(s_used, s * PIECES + (q + 1))
                                        sp.dma_start(piece[q].ap().bitcast(F32), span_table[bass.ds(s - lo, 1), :, q * PIECE:(q + 1) * PIECE, :].rearrange(
                                            "o p b n -> (o p) b n")).then_inc(s_piece[q], DMA)

                        both_paths(sp, dense, fast, lambda: g_sync(sp))

                    @block.gpsimd
                    def _(pool):
                        both_paths(pool, dense, lambda: pool.sem_inc(s_turn, 1), lambda: g_gpsimd(pool))

                    @block.vector
                    def _(dve):
                        def fast():
                            step = Chain(dve, s_parts)
                            dve.wait_ge(s_feat, DMA)
                            step(nc.vector.memset(parts[:, :, PARTS * D:SPLIT], 1.0))
                            for blocks in (slice(0, PIECE), slice(PIECE, BLOCKS)):
                                for n in range(PARTS):
                                    part = parts[:, blocks, n * D:(n + 1) * D]
                                    step(nc.vector.tensor_copy(part, feat[:, blocks, :]))
                                    if n < PARTS - 1:
                                        step(nc.vector.tensor_tensor(feat[:, blocks, :], feat[:, blocks, :], part, ALU.subtract))
                            with dve.Fori(0, SPANS) as s:
                                dve.wait_ge(s_node, s + 1)
                                dve.wait_ge(s_old, s * DMA + DMA)
                                nc.vector.tensor_tensor(new[:, :, :], p_node[:, 0:QUARTERS * width].rearrange("p (q w) -> p q w", q=QUARTERS),
                                                        old[:, :, :], ALU.add).then_inc(s_new, 1)

                        both_paths(dve, dense, fast, lambda: g_vector(dve))

                    @block.scalar
                    def _(act):
                        def fast():
                            def span(k, s):
                                at = span_row[0:1, s:s + 1] if isinstance(s, int) else span_row[0:1, bass.ds(s, 1)]
                                base = act.value_load(at, min_val=0, max_val=n_nodes - 1)
                                rows = total[bass.ds(base, SPAN)].rearrange("(q p) w -> p q w", p=P)
                                act.dma_start(old[:, :, :], rows).then_inc(s_old, DMA)
                                act.wait_ge(s_used, s * PIECES + 2 * PIECES)
                                nc.scalar.activation(wide[:, :], p_wide[k][:, :], ACT.Copy).then_inc(s_copied, 1)
                                act.wait_ge(s_new, s + 1)
                                act.dma_start(rows, new[:, :, :]).then_inc(s_stored, DMA)
                                act.wait_ge(s_stored, s * DMA + DMA)
                                act.sem_inc(s_turn, 1)

                            span(0, 0)
                            with act.Fori(0, SPANS // 2) as i:
                                for k in range(2):
                                    span(1 - k, i * 2 + (k + 1))

                        both_paths(act, dense, fast, lambda: g_scalar(act))

                    @block.tensor
                    def _(pe):
                        def fast():
                            pe.sem_inc(s_used, PIECES)

                            def take_piece(k, s, q):
                                pe.wait_ge(s_piece[q], s * DMA + DMA)
                                pe.sem_inc(s_turn, 1)
                                for b in range(PIECE):
                                    last = nc.tensor.matmul(p_wide[k][:, :], parts[:, q * PIECE + b, :], piece[q][:, b, :],
                                                            start=q == 0 and b == 0, stop=q == PIECES - 1 and b == PIECE - 1)
                                last.then_inc(s_used, 1)

                            def finish(n):
                                pe.wait_ge(s_copied, n)
                                for q in range(QUARTERS):
                                    last = nc.tensor.matmul(p_node[:, q * width:(q + 1) * width], wide[:, q * P:(q + 1) * P],
                                                            gather_parts[:, 0:width], start=True, stop=True)
                                last.then_inc(s_node, 1)

                            for q in range(PIECES):
                                if q < 2:
                                    pe.wait_ge(s_parts, 1 + (q + 1) * (2 * PARTS - 1))
                                take_piece(0, 0, q)
                            with pe.Fori(0, SPANS // 2) as i:
                                for k in range(2):
                                    for q in range(PIECES):
                                        take_piece(1 - k, i * 2 + (k + 1), q)
                                        if q == 0:
                                            finish(i * 2 + (k + 1))
                            finish(SPANS)

                        both_paths(pe, dense, fast, lambda: g_tensor(pe))
                cleared([*s_piece, *stage, *g_stage])

        BANKS = [(0, 3), (3, CHUNK)]

        def flat(ap):
            return ap.rearrange("p t e -> p (t e)")

        def when_fast(eng, fast):
            fits = eng.value_load(flag[0:1, 0:1], min_val=0, max_val=1)
            with eng.If(fits > 0):
                fast()

        def edge_mlp(pe, n, w1, hot_t_chunk, gathered, p_hidden, p_flow, hidden, w2, b2, s_hidden, s_relu, s_flow):
            for bank, (t0, t1) in enumerate(BANKS):
                nc.tensor.matmul(p_hidden[:, bank, 0:(t1 - t0) * P], w1[:, :], hot_t_chunk(t0, t1), start=True, stop=False)
                for t in range(t0, t1):
                    for r, rows in enumerate(gathered):
                        last = nc.tensor.matmul(p_hidden[:, bank, (t - t0) * P:(t - t0 + 1) * P], rows(t), identity[:, :],
                                                start=False, stop=t == t1 - 1 and r == len(gathered) - 1)
            last.then_inc(s_hidden, 1)
            nc.tensor.matmul(p_flow[:, 0:CHUNK * 2 * D], ones_f[0:1, :], b2[:, :, :].rearrange("o t f -> o (t f)"),
                             start=True, stop=False)
            pe.wait_ge(s_relu, n + 1)
            for t in range(CHUNK):
                last = nc.tensor.matmul(p_flow[:, t * 2 * D:(t + 1) * 2 * D], hidden[:, t * P:(t + 1) * P], w2[:, :],
                                        start=False, stop=t == CHUNK - 1)
            last.then_inc(s_flow, 1)

        with ExitStack() as c:
            SLOTS = CHUNKS
            w_e = [sb(f"e_w1{k}", [P, P], c=c) for k in range(2)]
            hot_t = [sb(f"e_hot_t{k}", [P, TILES, P], c=c) for k in range(2)]
            local_row = [sb(f"e_local_row{k}", [P, TILES, P], BF16, c=c) for k in range(2)]
            src_i = [sb(f"e_src_i{k}", [P, TILES], I32, c=c) for k in range(2)]
            bins = [sb(f"e_bins{k}", [P, TILES], c=c) for k in range(2)]
            starts = [sb(f"e_starts{k}", [P, TILES], c=c) for k in range(2)]
            places = [sb(f"e_places{k}", [P, TILES, 2], c=c) for k in range(2)]
            local = [sb(f"e_local{k}", [P, TILES], c=c) for k in range(2)]
            got = [sb(f"e_got{k}", [P, TILES, P], c=c) for k in range(2)]
            hot = [sb(f"e_hot{k}", [P, CHUNK, WINDOW], c=c) for k in range(2)]
            own = [sb(f"e_own{k}", [P, CHUNK, BLOCKS], BF16, c=c) for k in range(2)]
            ranked = sb("e_ranked", [P, CHUNK, BLOCKS], c=c)
            rank = sb("e_rank", [P, CHUNK], c=c)
            slot = sb("e_slot", [P, CHUNK], c=c)
            away = sb("e_away", [P, CHUNK], c=c)
            carry = sb("e_carry", [1, BLOCKS], BF16, c=c)
            to_row = [sb(f"e_to_row{k}", [P, CHUNK], I32, c=c) for k in range(SLOTS)]
            hidden = sb("e_hidden", [P, COLS], c=c)
            flow = sb("e_flow", [P, CHUNK, D], c=c)
            rec = [sb(f"e_rec{k}", [P, CHUNK, REC], BF16, c=c) for k in range(SLOTS)]
            bwd = [sb(f"e_bwd{k}", [P, CHUNK, D], c=c) for k in range(2)]
            b1 = sb("e_b1", [P, 1], c=c)
            w2 = sb("e_w2", [P, 2 * D], c=c)
            b2 = sb("e_b2", [1, CHUNK, 2 * D], c=c)
            old = [sb(f"e_old{k}", [WINDOW, D], c=c) for k in range(2)]
            new = [sb(f"e_new{k}", [WINDOW, D], c=c) for k in range(2)]
            p_hidden = c.enter_context(nc.psum_tensor("e_p_hidden", [P, 2, BANK], F32))
            p_flow = c.enter_context(nc.psum_tensor("e_p_flow", [P, BANK], F32))
            p_rank = c.enter_context(nc.psum_tensor("e_p_rank", [P, BANK], F32))
            p_carry = c.enter_context(nc.psum_tensor("e_p_carry", [1, BANK], F32))
            p_sum = [c.enter_context(nc.psum_tensor(f"e_p_sum{k}", [WINDOW, BANK], F32)) for k in range(2)]

            s_in, s_used, s_old = ([sem(f"e_{n}{k}", c) for k in range(2)] for n in ("in", "used", "old"))
            s_got = [[sem(f"e_got{k}_{m}") for m in range(CHUNKS)] for k in range(2)]
            s_recs = [sem(f"e_recs{q}") for q in range(2)]
            (s_w, s_const, s_hot_t, s_step, s_hidden, s_relu, s_flow, s_flowed, s_summed, s_ranked, s_carried, s_sent,
             s_stored, s_turn, s_worst, s_split) = (sem(f"e_{n}", c) for n in (
                 "weights", "const", "hot_t", "step", "hidden", "relu", "flow", "flowed", "summed", "ranked", "carried",
                 "sent", "stored", "turn", "worst", "split"))
            LOADS = 8
            STEPS = 11

            worst_row = sb("e_worst_row", [1, P * CHUNK], c=c)
            top, held = sb("e_top", [1, 1], c=c), sb("e_held", [1, 1], c=c)
            s_fits, s_turn_v, s_worst_in = (sem(f"e_{n}", c) for n in ("fits", "worst_step", "worst_in"))
            WEIGHTS = 4 + 2 * (2 + CHUNK)

            with nc.Block() as block:
                @block.sync
                def _(sp):
                    for k in range(2):
                        for n, w1 in enumerate((a["L0_gnn_W1f"], a["L0_gnn_W1b"])):
                            sp.dma_start(w_e[k][WINDOW:P, n * H:(n + 1) * H], w1[2 * D:2 * D + DE]).then_inc(s_w, DMA)
                    sp.wait_ge(s_const, 1)
                    for n, (w, b, bb) in enumerate((("W2f", "b1f", "b2f"), ("W2b", "b1b", "b2b"))):
                        sp.dma_start(w2[n * H:(n + 1) * H, n * D:(n + 1) * D], a[f"L0_gnn_{w}"]).then_inc(s_w, DMA)
                        sp.dma_start(b1[n * H:(n + 1) * H, :], a[f"L0_gnn_{b}"].rearrange("(h o) -> h o", o=1)).then_inc(s_w, DMA)
                        for t in range(CHUNK):
                            sp.dma_start(b2[0:1, t, n * D:(n + 1) * D], a[f"L0_gnn_{bb}"].rearrange("(o h) -> o h", o=1)).then_inc(s_w, DMA)
                    sp.wait_ge(s_w, WEIGHTS * DMA)

                    def attributes(g):
                        return a["edge_attr_16"][g] if isinstance(g, int) else a["edge_attr_16"][bass.ds(g, 1)].rearrange("o f n -> (o f) n")

                    def load(k, g, i):
                        base = fetch_base(sp, g)
                        sp.wait_ge(s_used[k], i + 1)
                        sp.dma_start(src_i[k][:, :], at_group(a["src"], g)).then_inc(s_in[k], DMA)
                        sp.dma_start(bins[k][:, :], at_group(bin_cols, g)).then_inc(s_in[k], DMA)
                        sp.dma_start(starts[k][:, :], at_group(start_cols, g)).then_inc(s_in[k], DMA)
                        sp.dma_start(places[k][:, :, :].rearrange("p t w -> p (t w)"),
                                     at_group(place_cols.rearrange("g p t w -> g p (t w)"), g)).then_inc(s_in[k], DMA)
                        sp.dma_start(local[k][:, :], at_group(local_cols, g)).then_inc(s_in[k], DMA)
                        sp.dma_start(flat(local_row[k][:, :, :]), row_group(local_rows, g)).then_inc(s_in[k], DMA)
                        sp.dma_start(flat(hot_t[k][WINDOW:P, :, :]), attributes(g)).then_inc(s_in[k], DMA)
                        sp.dma_start(w_e[k][0:WINDOW, :], window_rows(sp, pre_dst, base)).then_inc(s_in[k], DMA)

                    def add_window(k, g, i):
                        base = fetch_base(sp, g)
                        rows = window_rows(sp, fwd_sum, base)
                        sp.dma_start(old[k][:, :], rows).then_inc(s_old[k], DMA)
                        sp.wait_ge(s_used[k], i + 2)
                        sp.dma_start(rows, new[k][:, :]).then_inc(s_stored, DMA)
                        sp.wait_ge(s_stored, (g + 1) * DMA)
                        sp.sem_inc(s_turn, 1)

                    def fast():
                        load(0, 0, 0)
                        with sp.Fori(0, PAIRS) as i:
                            load(1, i * 2 + 1, i)
                            add_window(0, i * 2, i)
                            load(0, i * 2 + 2, i + 1)
                            add_window(1, i * 2 + 1, i)
                        add_window(0, NG - 1, PAIRS)

                    when_fast(sp, fast)
                    sp.wait_ge(s_worst, 1)
                    sp.dma_start(worst_rank, worst[:, :]).then_inc(s_worst_in, DMA)
                    sp.wait_ge(s_worst_in, DMA)
                    sp.dma_start(worst_row[:, :], worst_rank.rearrange("p t -> (p t)").rearrange("(o n) -> o n", o=1)).then_inc(s_worst_in, DMA)

                @block.gpsimd
                def _(pool):
                    def gather(k, t):
                        nc.gpsimd.indirect_dma_start(
                            out=got[k][:, t, :], out_offset=None, in_=pre_src,
                            in_offset=bass.IndirectOffsetOnAxis(ap=src_i[k][:, t:t + 1], axis=0)).then_inc(s_got[k][t // CHUNK], DMA)

                    def group(k, i, following):
                        if following is not None:
                            pool.wait_ge(s_in[1 - k], following * (LOADS * DMA) + LOADS * DMA)
                            pool.sem_inc(s_turn, 1)
                        for m in range(CHUNKS):
                            if following is not None:
                                for t in range(m * CHUNK, (m + 1) * CHUNK):
                                    gather(1 - k, t)
                            j = k * CHUNKS + m
                            n = i * (2 * CHUNKS) + j
                            pool.wait_ge(s_step, n * STEPS + STEPS)
                            pool.wait_ge(s_split, n * 3 + 6)
                            if not isinstance(n, int) or n:
                                pool.wait_ge(s_recs[(j + 1) % 2], (i * CHUNKS + (j + 1) // 2) * (CHUNK * DMA))
                            pool.sem_inc(s_turn, 1)
                            for t in range(CHUNK):
                                nc.gpsimd.indirect_dma_start(
                                    out=records, out_offset=bass.IndirectOffsetOnAxis(ap=to_row[j % SLOTS][:, t:t + 1], axis=0),
                                    in_=rec[j % SLOTS].ap().bitcast(F32)[:, t, :], in_offset=None).then_inc(s_recs[j % 2], DMA)
                            pool.sem_inc(s_sent, 1)

                    def fast():
                        pool.sem_inc(s_sent, SLOTS - 1)
                        pool.wait_ge(s_in[0], LOADS * DMA)
                        for t in range(TILES):
                            gather(0, t)
                        group(0, 0, 0)
                        group(1, 0, 1)
                        with pool.Fori(1, PAIRS) as i:
                            group(0, i, i)
                            group(1, i, i + 1)
                        group(0, PAIRS, None)
                        for q in range(2):
                            pool.wait_ge(s_recs[q], ((NC + 1 - q) // 2) * (CHUNK * DMA))

                    pool.wait_ge(emptied, (EARLY + TURNS) * DMA)
                    when_fast(pool, fast)

                @block.vector
                def _(dve):
                    nc.vector.memset(w2[:, :], 0.0).then_inc(s_const, 1)
                    nc.vector.memset(carry[:, :], 0.0).then_inc(s_const, 1)
                    nc.vector.memset(bwd[1][:, :, :], 0.0).then_inc(s_const, 1)
                    nc.vector.memset(rec[SLOTS - 1][:, :, :], 0.0).then_inc(s_const, 1)

                    def split(j, n):
                        flows, parts = bwd[(j - 1) % 2], rec[(j - 1) % SLOTS]
                        dve.wait_ge(s_flowed, n + 1)
                        nc.vector.tensor_tensor(flows[:, :, :], flows[:, :, :], parts[:, :, 0:D], ALU.subtract).then_inc(s_split, 1)
                        dve.wait_ge(s_split, n * 3 + 1)
                        nc.vector.tensor_copy(parts[:, :, D:2 * D], flows[:, :, :]).then_inc(s_split, 1)
                        dve.wait_ge(s_split, n * 3 + 2)
                        nc.vector.tensor_tensor(parts[:, :, 2 * D:3 * D], flows[:, :, :], parts[:, :, D:2 * D], ALU.subtract).then_inc(s_split, 1)

                    def chunk(k, m, i):
                        j = k * CHUNKS + m
                        n = i * (2 * CHUNKS) + j
                        q = j % 2
                        part = slice(m * CHUNK, (m + 1) * CHUNK)
                        count = [0]

                        def add(ins):
                            count[0] += 1
                            ins.then_inc(s_step, 1)
                            dve.wait_ge(s_step, n * STEPS + count[0])

                        dve.wait_ge(s_summed, n + 1)
                        nc.vector.tensor_tensor(own[q][:, :, :], column[:, 0:BLOCKS].unsqueeze(1).to_broadcast([P, CHUNK, BLOCKS]),
                                                bins[k][:, part].unsqueeze(2).to_broadcast([P, CHUNK, BLOCKS]), ALU.is_equal).then_inc(s_step, 1)
                        nc.vector.tensor_scalar(hot_t[k][0:WINDOW, part, :], local_row[k][0:WINDOW, part, :],
                                                row_id[0:WINDOW, 0:1], None, ALU.is_equal).then_inc(s_step, 1)
                        nc.vector.tensor_tensor(hot[q][:, :, :], column[:, 0:WINDOW].unsqueeze(1).to_broadcast([P, CHUNK, WINDOW]),
                                                local[k][:, part].unsqueeze(2).to_broadcast([P, CHUNK, WINDOW]), ALU.is_equal).then_inc(s_step, 1)
                        dve.wait_ge(s_sent, n + 1)
                        nc.vector.tensor_copy(rec[j % SLOTS][:, :, PARTS * D:REC], places[k][:, part, :]).then_inc(s_step, 1)
                        count[0] = 4
                        split(j, n)
                        dve.wait_ge(s_ranked, n + 1)
                        dve.wait_ge(s_step, n * STEPS + 4)
                        shape = [P, CHUNK, BLOCKS]
                        add(nc.vector.tensor_tensor(ranked[:, :, :], p_rank[:, 0:CHUNK * BLOCKS].rearrange("p (t b) -> p t b", t=CHUNK),
                                                    own[q][:, :, :], ALU.mult))
                        add(nc.vector.tensor_reduce(rank[:, :], ranked[:, :, :], AX, ALU.add))
                        add(nc.vector.scalar_tensor_tensor(out=slot[:, :], in0=rank[:, :], scalar=float(SPANS), in1=starts[k][:, part],
                                                           op0=ALU.mult, op1=ALU.add))
                        at = span_no[:, n:n + 1] if isinstance(n, int) else span_no[:, bass.ds(n, 1)]
                        add(nc.vector.tensor_scalar(slot[:, :], slot[:, :], at, None, ALU.add))
                        add(nc.vector.tensor_tensor(away[:, :], spare_record[:, :], slot[:, :], ALU.subtract))
                        add(nc.vector.scalar_tensor_tensor(out=away[:, :], in0=rank[:, :], scalar=float(CAPACITY), in1=away[:, :],
                                                           op0=ALU.is_ge, op1=ALU.mult))
                        nc.vector.tensor_tensor(worst[:, :], worst[:, :], rank[:, :], ALU.max).then_inc(s_turn_v, 1)
                        add(nc.vector.tensor_tensor(to_row[j % SLOTS][:, :], slot[:, :], away[:, :], ALU.add))

                    def add_old(k, i):
                        dve.wait_ge(s_summed, (i * 2 + (k + 1)) * CHUNKS + 2)
                        dve.wait_ge(s_old[k], i * DMA + DMA)
                        nc.vector.tensor_tensor(new[k][:, :], p_sum[k][:, 0:D], old[k][:, :], ALU.add).then_inc(s_used[k], 1)

                    def fast():
                        for k in range(2):
                            dve.sem_inc(s_used[k], 1)
                        with dve.Fori(0, PAIRS) as i:
                            for k in range(2):
                                dve.wait_ge(s_in[k], i * (LOADS * DMA) + LOADS * DMA)
                                for m in range(CHUNKS):
                                    chunk(k, m, i)
                                add_old(k, i)
                        dve.wait_ge(s_in[0], (PAIRS + 1) * LOADS * DMA)
                        for m in range(CHUNKS):
                            chunk(0, m, PAIRS)
                        split(CHUNKS, NC)
                        add_old(0, PAIRS)

                    when_fast(dve, fast)
                    dve.sem_inc(s_worst, 1)
                    step = Chain(dve, s_fits)
                    dve.wait_ge(s_worst_in, 2 * DMA)
                    step(nc.vector.tensor_reduce(top[:, :], worst_row[:, :], AX, ALU.max))
                    step(nc.vector.tensor_scalar(top[:, :], top[:, :], float(CAPACITY), None, ALU.is_lt))
                    step(nc.vector.tensor_copy(held[:, :], flag[:, :]))
                    step(nc.vector.tensor_tensor(held[:, :], held[:, :], top[:, :], ALU.mult))
                    step(nc.vector.tensor_copy(all_fit[:, :], held[:, :]))

                @block.scalar
                def _(act):
                    act.wait_ge(s_w, WEIGHTS * DMA)

                    def chunk(k, m, i):
                        j = k * CHUNKS + m
                        n = i * (2 * CHUNKS) + j
                        act.wait_ge(s_ranked, n + 1)
                        at = keep[0:1, n:n + 1] if isinstance(n, int) else keep[0:1, bass.ds(n, 1)]
                        nc.scalar.activation(carry[:, :], p_carry[:, 0:BLOCKS], ACT.Copy, scale=at).then_inc(s_carried, 1)
                        act.wait_ge(s_hidden, n + 1)
                        for bank, (t0, t1) in enumerate(BANKS):
                            last = nc.scalar.activation(hidden[:, t0 * P:t1 * P], p_hidden[:, bank, 0:(t1 - t0) * P], ACT.Relu,
                                                        bias=b1[:, 0:1])
                        last.then_inc(s_relu, 1)
                        act.wait_ge(s_flow, n + 1)
                        flows = p_flow[:, 0:CHUNK * 2 * D].rearrange("p (t f) -> p t f", t=CHUNK)
                        nc.scalar.activation(flow[:, :, :], flows[:, :, 0:D], ACT.Relu)
                        nc.scalar.activation(bwd[j % 2][:, :, :], flows[:, :, D:2 * D], ACT.Relu)
                        act.wait_ge(s_sent, n + 1)
                        nc.scalar.activation(rec[j % SLOTS][:, :, 0:D], flows[:, :, D:2 * D], ACT.Relu).then_inc(s_flowed, 1)

                    def fast():
                        act.wait_ge(s_const, 4)
                        act.sem_inc(s_flowed, 1)
                        with act.Fori(0, PAIRS) as i:
                            for k in range(2):
                                for m in range(CHUNKS):
                                    chunk(k, m, i)
                        for m in range(CHUNKS):
                            chunk(0, m, PAIRS)

                    when_fast(act, fast)

                @block.tensor
                def _(pe):
                    pe.wait_ge(s_w, WEIGHTS * DMA)
                    pe.wait_ge(s_const, 2)

                    def chunk(k, m, i):
                        j = k * CHUNKS + m
                        n = i * (2 * CHUNKS) + j
                        q = j % 2
                        pe.wait_ge(s_step, n * STEPS + 1)
                        pe.wait_ge(s_carried, n + 1)
                        counted = p_rank[:, 0:CHUNK * BLOCKS].rearrange("p (t b) -> p t b", t=CHUNK)
                        nc.tensor.matmul(counted, ones[0:1, :], carry[0:1, :].unsqueeze(1).to_broadcast([1, CHUNK, BLOCKS]), start=True, stop=False)
                        for t in range(CHUNK):
                            nc.tensor.matmul(counted[:, t, :], behind[:, :], own[q][:, t, :], start=False, stop=False)
                        for t in range(CHUNK - 1):
                            nc.tensor.matmul(counted[:, t + 1:CHUNK, :], ones[:, :],
                                             own[q][:, t:t + 1, :].to_broadcast([P, CHUNK - 1 - t, BLOCKS]), start=False, stop=t == CHUNK - 2)
                        nc.tensor.matmul(p_carry[:, 0:BLOCKS], ones[0:1, 0:1], carry[0:1, :], start=True, stop=False)
                        for t in range(CHUNK):
                            last = nc.tensor.matmul(p_carry[:, 0:BLOCKS], ones[:, 0:1], own[q][:, t, :], start=False, stop=t == CHUNK - 1)
                        last.then_inc(s_ranked, 1)

                        first = m * CHUNK
                        pe.wait_ge(s_got[k][m], i * (CHUNK * DMA) + CHUNK * DMA)
                        pe.wait_ge(s_step, n * STEPS + 2)
                        edge_mlp(pe, n, w_e[k], lambda t0, t1: flat(hot_t[k][:, first + t0:first + t1, :]),
                                 [lambda t: got[k][:, first + t, :]], p_hidden, p_flow, hidden, w2, b2, s_hidden, s_relu, s_flow)
                        pe.wait_ge(s_flowed, n + 2)
                        pe.wait_ge(s_step, n * STEPS + 3)
                        if m == 0:
                            pe.wait_ge(s_used[k], i + 1)
                        for t in range(CHUNK):
                            last = nc.tensor.matmul(p_sum[k][:, 0:D], hot[q][:, t, :], flow[:, t, :],
                                                    start=m == 0 and t == 0, stop=m == CHUNKS - 1 and t == CHUNK - 1)
                        last.then_inc(s_summed, 1)

                    def group(k, i):
                        pe.wait_ge(s_in[k], i * (LOADS * DMA) + LOADS * DMA)
                        for m in range(CHUNKS):
                            chunk(k, m, i)

                    def fast():
                        pe.sem_inc(s_summed, 2)
                        pe.sem_inc(s_carried, 1)
                        with pe.Fori(0, PAIRS) as i:
                            group(0, i)
                            group(1, i)
                        group(0, PAIRS)

                    when_fast(pe, fast)
            cleared([*s_in, *s_used, *s_old, s_w, s_const, s_hot_t, s_step, s_hidden, s_relu, s_flow, s_flowed, s_summed,
                     s_ranked, s_carried, s_sent, s_stored, s_turn, s_worst, s_split, s_fits, s_turn_v, s_worst_in])

        with ExitStack() as c:
            BIN = DEEP * SPANS
            UNITS, RING = (14, 7) if BLOCKS % 14 == 0 else (4, 4)
            assert BLOCKS % UNITS == 0
            rec = [sb(f"s_rec{r}", [P, DEEP, SPANS, REC], BF16, c=c) for r in range(RING)]
            hot = [sb(f"s_hot{k}", [P, P, BIN], BF16, c=c) for k in range(2)]
            source = [sb(f"s_source{k}", [P, BIN], BF16, c=c) for k in range(2)]
            local = [sb(f"s_local{k}", [P, DEEP, SPANS, 2], c=c) for k in range(2)]
            wide = sb("s_wide", [PARTS * D, P], c=c)
            total = [sb(f"s_total{k}", [P, D], c=c) for k in range(2)]
            p_wide = [c.enter_context(nc.psum_tensor(f"s_p_wide{k}", [PARTS * D, BANK], F32)) for k in range(2)]
            p_total = c.enter_context(nc.psum_tensor("s_p_total", [P, BANK], F32))
            w_e = sb("g_w1", [P, P], c=c)
            hot_t = sb("g_hot_t", [P, CHUNK, P], c=c)
            g_rows = [sb(f"g_row{n}", [P, CHUNK, P], c=c) for n in range(2)]
            g_ints = [sb(f"g_int{n}", [P, CHUNK], I32, c=c) for n in range(2)]
            g_cols = [sb(f"g_col{n}", [P, CHUNK], c=c) for n in range(2)]
            got = [sb(f"g_got{n}", [P, CHUNK, P], c=c) for n in range(2)]
            same = [sb(f"g_same{n}", [P, CHUNK, P], c=c) for n in range(2)]
            earlier = sb("g_earlier", [P, CHUNK, P], c=c)
            twin, away = sb("g_twin", [P, CHUNK], c=c), sb("g_away", [P, CHUNK], c=c)
            to_row = [sb(f"g_to_row{n}", [P, CHUNK], I32, c=c) for n in range(2)]
            hidden = sb("g_hidden", [P, COLS], c=c)
            flow = sb("g_flow", [P, CHUNK, 2 * D], c=c)
            merged = [sb(f"g_merged{n}", [P, CHUNK, D], c=c) for n in range(2)]
            b1, w2, b2 = sb("g_b1", [P, 1], c=c), sb("g_w2", [P, 2 * D], c=c), sb("g_b2", [1, CHUNK, 2 * D], c=c)
            p_hidden = c.enter_context(nc.psum_tensor("g_p_hidden", [P, 2, BANK], F32))
            p_flow = c.enter_context(nc.psum_tensor("g_p_flow", [P, BANK], F32))
            p_merged = c.enter_context(nc.psum_tensor("g_p_merged", [P, BANK], F32))
            s_in = [sem(f"s_in{r}", c) for r in range(RING)]
            g_got, g_added = ([sem(f"g_{n}{d}") for d in range(2)] for n in ("got", "added"))
            s_hot, s_total, s_taken, s_local, s_wide, s_copied = (
                sem(f"s_{n}", c) for n in ("hot", "total", "taken", "local", "wide", "copied"))
            s_stored = [sem(f"s_stored{k}", c) for k in range(2)]
            g_w, g_step, g_relu, g_flow, g_flowed, g_copied, g_free, g_turn = (
                sem(f"g_{n}", c) for n in ("weights", "step", "relu", "flow", "flowed", "copied", "free", "turn"))
            g_zeroed, g_merged, g_hidden = s_hot, s_total, s_taken
            g_in, g_loads = s_in[0:2], (3, 4)
            WEIGHTS = 2 + 2 * (2 + CHUNK)

            with nc.Block() as block:
                @block.sync
                def _(sp):
                    def block_records(b):
                        return records[bass.ds(b * STRIDE, STRIDE)].rearrange("(d p s) c -> p d (s c)", d=DEEP, p=P)

                    def fast():
                        def slot(r):
                            return rec[r].ap().bitcast(F32).rearrange("p d s c -> p d (s c)")

                        for r in range(RING):
                            sp.dma_start(slot(r), records[r * STRIDE:(r + 1) * STRIDE].rearrange("(d p s) c -> p d (s c)", d=DEEP, p=P)).then_inc(s_in[r], DMA)
                        with sp.Fori(0, BLOCKS // UNITS) as i:
                            for u in range(UNITS):
                                sp.wait_ge(s_local, i * UNITS + (u + 1))
                                sp.sem_inc(g_turn, 1)
                                sp.wait_ge(s_wide, i * UNITS + (u + 3))
                                sp.sem_inc(g_turn, 1)
                                sp.wait_ge(s_hot, i * (2 * UNITS) + (2 * u + 1))
                                sp.sem_inc(g_turn, 1)
                                following = (i * UNITS + (u + RING)) % BLOCKS
                                sp.dma_start(slot(u % RING), block_records(following)).then_inc(s_in[u % RING], DMA)
                        for r in range(RING):
                            sp.wait_ge(s_in[r], (BLOCKS // RING + 1) * DMA)

                    def general():
                        for n, w1 in enumerate((a["L0_gnn_W1f"], a["L0_gnn_W1b"])):
                            sp.dma_start(w_e[WINDOW:P, n * H:(n + 1) * H], w1[2 * D:2 * D + DE]).then_inc(g_w, DMA)
                        sp.wait_ge(g_zeroed, 3)
                        for n, (w, b, bb) in enumerate((("W2f", "b1f", "b2f"), ("W2b", "b1b", "b2b"))):
                            sp.dma_start(w2[n * H:(n + 1) * H, n * D:(n + 1) * D], a[f"L0_gnn_{w}"]).then_inc(g_w, DMA)
                            sp.dma_start(b1[n * H:(n + 1) * H, :], a[f"L0_gnn_{b}"].rearrange("(h o) -> h o", o=1)).then_inc(g_w, DMA)
                            for t in range(CHUNK):
                                sp.dma_start(b2[0:1, t, n * D:(n + 1) * D], a[f"L0_gnn_{bb}"].rearrange("(o h) -> o h", o=1)).then_inc(g_w, DMA)
                        with sp.Fori(0, NG) as g:
                            features = a["edge_attr_16"][bass.ds(g, 1)].rearrange("o f n -> (o f) n")
                            for m in range(CHUNKS):
                                part = slice(m * CHUNK, (m + 1) * CHUNK)
                                sp.wait_ge(g_free, g * CHUNKS + (m + 1))
                                for n, (ints, cols, rows) in enumerate(((a["src"], src_cols, src_rows), (a["dst"], dst_cols, dst_rows))):
                                    sp.dma_start(g_ints[n][:, :], at_group(ints, g)[:, part]).then_inc(g_in[n], DMA)
                                    sp.dma_start(g_cols[n][:, :], at_group(cols, g)[:, part]).then_inc(g_in[n], DMA)
                                    sp.dma_start(flat(g_rows[n][:, :, :]), row_group(rows, g, m * CHUNK, CHUNK)).then_inc(g_in[n], DMA)
                                sp.dma_start(flat(hot_t[WINDOW:P, :, :]), features[:, m * COLS:(m + 1) * COLS]).then_inc(g_in[1], DMA)

                    both_paths(sp, all_fit, fast, general)

                @block.gpsimd
                def _(pool):
                    def fast():
                        pool.sem_inc(g_turn, 1)

                    def general():
                        pool.sem_inc(g_free, 1)
                        with pool.Fori(0, NG) as g:
                            for m in range(CHUNKS):
                                n = g * CHUNKS + m
                                for d in range(2):
                                    pool.wait_ge(g_in[d], n * (g_loads[d] * DMA) + g_loads[d] * DMA)
                                pool.sem_inc(g_turn, 1)
                                for t in range(CHUNK):
                                    for d, table in enumerate((pre_src, pre_dst[0:n_nodes])):
                                        nc.gpsimd.indirect_dma_start(
                                            out=got[d][:, t, :], out_offset=None, in_=table,
                                            in_offset=bass.IndirectOffsetOnAxis(ap=g_ints[d][:, t:t + 1], axis=0)).then_inc(g_got[d], DMA)
                                pool.wait_ge(g_copied, n * 2 + 2)
                                pool.sem_inc(g_turn, 1)
                                for t in range(CHUNK):
                                    for d, table in enumerate((bwd_sum, fwd_general)):
                                        nc.gpsimd.indirect_dma_start(
                                            out=table, out_offset=bass.IndirectOffsetOnAxis(ap=to_row[d][:, t:t + 1], axis=0),
                                            in_=merged[d][:, t, :], in_offset=None, compute_op=ALU.add).then_inc(g_added[d], DMA)
                                    for d in range(2):
                                        pool.wait_ge(g_added[d], n * (CHUNK * DMA) + (t + 1) * DMA)
                                    pool.sem_inc(g_turn, 1)
                                pool.sem_inc(g_free, 1)

                    both_paths(pool, all_fit, fast, general)

                @block.vector
                def _(dve):
                    def fast():
                        with dve.Fori(0, BLOCKS // UNITS) as i:
                            for u in range(UNITS):
                                k, r = u % 2, u % RING
                                dve.wait_ge(s_in[r], i * (UNITS // RING * DMA) + (u // RING + 1) * DMA)
                                nc.vector.tensor_copy(source[k][:, :], rec[r][:, :, :, PARTS * D].rearrange("p d s -> p (d s)")).then_inc(s_hot, 1)
                                dve.wait_ge(s_hot, i * (2 * UNITS) + (2 * u + 1))
                                dve.wait_ge(s_wide, i * UNITS + (u + 1))
                                nc.vector.tensor_tensor(hot[k][:, :, :], column_s[:, :, :], source[k][:, :].unsqueeze(1).to_broadcast([P, P, BIN]),
                                                        ALU.is_equal).then_inc(s_hot, 1)

                    def general():
                        nc.vector.memset(hot_t[0:WINDOW, :, :], 0.0).then_inc(g_zeroed, 1)
                        nc.vector.memset(w_e[0:WINDOW, :], 0.0).then_inc(g_zeroed, 1)
                        nc.vector.memset(w2[:, :], 0.0).then_inc(g_zeroed, 1)
                        with dve.Fori(0, NG) as g:
                            for m in range(CHUNKS):
                                n = g * CHUNKS + m
                                for d in range(2):
                                    dve.wait_ge(g_in[d], n * (g_loads[d] * DMA) + g_loads[d] * DMA)
                                for d in range(2):
                                    merge_steps(dve, g_step, n * 12 + 6 * d, g_cols[d][:, :], g_rows[d], same[d], earlier, twin, away, to_row[d])
                                dve.wait_ge(g_merged, n + 1)
                                for d in range(2):
                                    nc.vector.tensor_copy(merged[d][:, :, :], p_merged[:, d * CHUNK * D:(d + 1) * CHUNK * D].rearrange(
                                        "p (t f) -> p t f", t=CHUNK)).then_inc(g_copied, 1)

                    both_paths(dve, all_fit, fast, general)

                @block.scalar
                def _(act):
                    def fast():
                        for k in range(2):
                            act.sem_inc(s_stored[k], 2 * DMA)
                        with act.Fori(0, BLOCKS // UNITS) as i:
                            for u in range(UNITS):
                                k, r = u % 2, u % RING
                                b = i * UNITS + u
                                act.wait_ge(s_in[r], i * (UNITS // RING * DMA) + (u // RING + 1) * DMA)
                                act.wait_ge(s_stored[k], i * (UNITS * DMA) + (u // 2 + 1) * (2 * DMA))
                                nc.scalar.activation(local[k][:, :, :, :], rec[r][:, :, :, PARTS * D:REC], ACT.Copy).then_inc(s_local, 1)
                                act.wait_ge(s_wide, i * UNITS + (u + 3))
                                nc.scalar.activation(wide[:, :], p_wide[k][:, 0:P], ACT.Copy).then_inc(s_copied, 1)
                                act.wait_ge(s_total, i * UNITS + (u + 1))
                                nc.scalar.activation(total[k][:, :], p_total[:, 0:D], ACT.Copy).then_inc(s_taken, 1)
                                act.wait_ge(s_taken, i * UNITS + (u + 1))
                                act.dma_start(bwd_sum[bass.ds(b * P, P)], total[k][:, :]).then_inc(s_stored[k], DMA)
                                act.dma_start(local_table[bass.ds(b, 1)].rearrange("o p n -> (o p) n"),
                                              local[k][:, :, :, :].rearrange("p d s w -> p (d s w)")).then_inc(s_stored[k], DMA)
                        for k in range(2):
                            act.wait_ge(s_stored[k], (BLOCKS + 2) * DMA)

                    def general():
                        act.wait_ge(g_w, WEIGHTS * DMA)
                        with act.Fori(0, NC) as n:
                            act.wait_ge(g_hidden, n + 1)
                            for bank, (t0, t1) in enumerate(BANKS):
                                last = nc.scalar.activation(hidden[:, t0 * P:t1 * P], p_hidden[:, bank, 0:(t1 - t0) * P], ACT.Relu,
                                                            bias=b1[:, 0:1])
                            last.then_inc(g_relu, 1)
                            act.wait_ge(g_flow, n + 1)
                            nc.scalar.activation(flow[:, :, :], p_flow[:, 0:CHUNK * 2 * D].rearrange("p (t f) -> p t f", t=CHUNK),
                                                 ACT.Relu).then_inc(g_flowed, 1)

                    both_paths(act, all_fit, fast, general)

                @block.tensor
                def _(pe):
                    def fast():
                        pe.sem_inc(s_wide, 2)
                        with pe.Fori(0, BLOCKS // UNITS) as i:
                            for u in range(UNITS):
                                k, r = u % 2, u % RING
                                pe.wait_ge(s_in[r], i * (UNITS // RING * DMA) + (u // RING + 1) * DMA)
                                pe.wait_ge(s_hot, i * (2 * UNITS) + (2 * u + 2))
                                for t in range(BIN):
                                    d, s = divmod(t, SPANS)
                                    last = nc.tensor.matmul(p_wide[k][:, 0:P], rec[r][:, d, s, 0:PARTS * D], hot[k][:, :, t],
                                                            start=t == 0, stop=t == BIN - 1)
                                last.then_inc(s_wide, 1)
                                pe.wait_ge(s_copied, i * UNITS + (u + 1))
                                nc.tensor.matmul(p_total[:, 0:D], wide[:, :], gather_parts[0:PARTS * D, 0:D], start=True, stop=True).then_inc(s_total, 1)

                    def general():
                        pe.wait_ge(g_w, WEIGHTS * DMA)
                        pe.wait_ge(g_zeroed, 3)
                        with pe.Fori(0, NC) as n:
                            for d in range(2):
                                pe.wait_ge(g_in[d], n * (g_loads[d] * DMA) + g_loads[d] * DMA)
                            for d in range(2):
                                pe.wait_ge(g_got[d], n * (CHUNK * DMA) + CHUNK * DMA)
                            edge_mlp(pe, n, w_e, lambda t0, t1: flat(hot_t[:, t0:t1, :]),
                                     [lambda t: got[0][:, t, :], lambda t: got[1][:, t, :]], p_hidden, p_flow, hidden, w2, b2,
                                     g_hidden, g_relu, g_flow)
                            pe.wait_ge(g_flowed, n + 1)
                            pe.wait_ge(g_step, n * 12 + 12)
                            for d in range(2):
                                for t in range(CHUNK):
                                    at = (d * CHUNK + t) * D
                                    last = nc.tensor.matmul(p_merged[:, at:at + D], same[d][:, t, :], flow[:, t, (1 - d) * D:(2 - d) * D],
                                                            start=True, stop=True)
                            last.then_inc(g_merged, 1)

                    both_paths(pe, all_fit, fast, general)
            cleared([*s_in, s_hot, s_total, s_taken, *s_stored, s_local, s_wide, s_copied, g_w, g_step, g_relu, g_flow, g_flowed, g_copied, g_free, g_turn])


        with ExitStack() as c:
            both = sb("both", [LANES, PER, 2 * D], c=c)
            part = [sb(f"part{n}", [LANES, PER, D], c=c) for n in range(3)]
            b2 = sb("b2n", [LANES, D], c=c)
            p_in, v = sem("part_in"), sem("part_v")
            with nc.Block() as block:
                @block.sync
                def _(sp):
                    def load(n, table):
                        sp.dma_start(part[n][:, :, :], table[0:n_nodes].rearrange("(p j) f -> p j f", p=LANES)).then_inc(p_in, DMA)

                    both_paths(sp, all_fit, lambda: load(0, fwd_sum), lambda: load(0, fwd_general))
                    load(1, bwd_sum)
                    sp.dma_start(b2[:, :], a["L0_gnn_b2n"].rearrange("(o f) -> o f", o=1).to_broadcast([LANES, D])).then_inc(p_in, DMA)

                @block.vector
                def _(dve):
                    dve.wait_ge(p_in, 3 * DMA)
                    step = Chain(dve, v)
                    step(nc.vector.tensor_copy(both[:, :, 0:D], part[0][:, :, :]))
                    step(nc.vector.tensor_copy(both[:, :, D:2 * D], part[1][:, :, :]))
            taken = part[0]
            node_mlp("mlp0", both, 2 * D, a["L0_gnn_W1n"], a["L0_gnn_b1n"], a["L0_gnn_W2n"], ACT.Relu, taken)
            t = (sb("mean1", [LANES, PER], c=c), sb("var1", [LANES, PER], c=c), part[1], part[2])
            v, ready, rooted, stored = (sem(n) for n in ("n1_v", "n1_ready", "n1_root", "n1_stored"))
            with nc.Block() as block:
                @block.vector
                def _(dve):
                    step = Chain(dve, v)
                    step(nc.vector.tensor_tensor(taken[:, :, :], taken[:, :, :],
                                                 b2[:, :].unsqueeze(1).to_broadcast([LANES, PER, D]), ALU.add))
                    step(nc.vector.tensor_scalar(taken[:, :, :], taken[:, :, :], 0.0, None, ALU.max))
                    step(nc.vector.tensor_tensor(x[:, :, :], x[:, :, :], taken[:, :, :], ALU.add))
                    layernorm(step, rooted, ready, 1, t)
                    dve.sem_inc(ready, 1)

                @block.scalar
                def _(act):
                    root(act, ready, rooted, t[1][:, :], 1)

                @block.sync
                def _(sp):
                    sp.wait_ge(ready, 2)
                    sp.dma_start(feats[0][0:n_nodes].rearrange("(p j) f -> p j f", p=LANES), h[:, :, :]).then_inc(stored, DMA)
                    sp.wait_ge(stored, DMA)

        weighted_sum("l1", feats[0][0:n_nodes], sums[0], a["edge_weight"])

        def node_step(tag, constants, kept, ops, roots, total, width=D):
            with ExitStack() as c:
                summed = sb(f"{tag}_summed", [LANES, PER, width], c=c)
                t = scratch(c, tag)
                extra = {n: sb(f"{tag}_{n}", list(shape), c=c) for n, (shape, _) in constants.items()}
                s_in, v, ready, rooted, stored = (sem(f"{tag}_{n}") for n in ("sums_in", "v", "ready", "root", "stored"))
                with nc.Block() as block:
                    @block.sync
                    def _(sp):
                        sp.dma_start(summed[:, :, :], total[0:n_nodes].rearrange("(p j) f -> p j f", p=LANES)).then_inc(s_in, DMA)
                        for n, (_, ap) in constants.items():
                            sp.dma_start(extra[n][:, :], ap).then_inc(s_in, DMA)
                        if kept is not None:
                            sp.wait_ge(ready, roots + 1)
                            sp.dma_start(kept[0], kept[1][:, :, :]).then_inc(stored, DMA)
                            sp.wait_ge(stored, DMA)

                    @block.vector
                    def _(dve):
                        dve.wait_ge(s_in, (1 + len(constants)) * DMA)
                        step = Chain(dve, v)
                        ops(dve, step, summed, t, extra, ready, rooted)
                        dve.sem_inc(ready, 1)

                    @block.scalar
                    def _(act):
                        for n in range(roots):
                            root(act, ready, rooted, (t[1], t[0])[n][:, :], n + 1)

        def node_rows(table):
            return table[0:n_nodes].rearrange("(p j) f -> p j f", p=LANES)

        def spread(ap):
            return ap.rearrange("(o f) -> o f", o=1).to_broadcast([LANES, ap.shape[0]])

        def after_l1(dve, step, summed, t, extra, ready, rooted):
            step(nc.vector.tensor_tensor(x[:, :, :], x[:, :, :], summed[:, :, :], ALU.add))
            layernorm(step, rooted, ready, 1, t)

        node_step("n2", {}, (node_rows(feats[1]), h), after_l1, 1, sums[0])

        counted_sum("l2", feats[1], sums[1], widths[1])

        def after_l2(dve, step, summed, t, extra, ready, rooted):
            eps1 = extra["eps"]
            step(nc.vector.tensor_scalar(eps1[:, :], eps1[:, :], 1.0, None, ALU.add))
            step(nc.vector.scalar_tensor_tensor(out=h[:, :, :], in0=h[:, :, :], scalar=eps1[:, 0:1], in1=summed[:, :, 0:D],
                                                op0=ALU.mult, op1=ALU.add))
            step(nc.vector.tensor_tensor(x[:, :, :], x[:, :, :], h[:, :, :], ALU.add))
            layernorm(step, rooted, ready, 1, t)
            mean = t[0]
            step(nc.vector.tensor_scalar(mean[:, :], summed[:, :, D], 1.0, None, ALU.add))
            step(nc.vector.reciprocal(inv_deg[:, :], mean[:, :]))
            dve.sem_inc(ready, 1)
            dve.wait_ge(rooted, 2)
            step(nc.vector.reciprocal(inv_sqrt[:, :], mean[:, :]))
            step(nc.vector.tensor_tensor(t[2][:, :, :], h[:, :, :], over(inv_sqrt), ALU.mult))

        with ExitStack() as keep:
            scaled = sb("scaled", [LANES, PER, D], c=keep)

            def after_l2_store(dve, step, summed, t, extra, ready, rooted):
                after_l2(dve, step, summed, t, extra, ready, rooted)
                step(nc.vector.tensor_copy(scaled[:, :, :], t[2][:, :, :]))

            node_step("n3", {"eps": ((LANES, 1), spread(a["L2_gnn_eps"]))}, (node_rows(feats[2]), scaled), after_l2_store,
                      2, sums[1], widths[1])

            counted_sum("l3a", feats[2], sums[2], widths[2])

            def after_l3a(dve, step, summed, t, extra, ready, rooted):
                step(nc.vector.tensor_tensor(summed[:, :, :], summed[:, :, :], over(inv_sqrt), ALU.mult))
                step(nc.vector.tensor_tensor(scaled[:, :, :], h[:, :, :], over(inv_deg), ALU.mult))
                step(nc.vector.tensor_tensor(scaled[:, :, :], scaled[:, :, :], summed[:, :, :], ALU.add))

            node_step("n4", {}, None, after_l3a, 0, sums[2])
            node_mlp("mlp3", scaled, D, a["L3_gnn_W1"], a["L3_gnn_b1"], a["L3_gnn_W2"], ACT.Identity, h)
            v, stored = sem("n5_v"), sem("n5_stored")
            with nc.Block() as block:
                @block.vector
                def _(dve):
                    nc.vector.tensor_tensor(scaled[:, :, :], h[:, :, :], over(inv_sqrt), ALU.mult).then_inc(v, 1)

                @block.sync
                def _(sp):
                    sp.wait_ge(v, 1)
                    sp.dma_start(node_rows(feats[3]), scaled[:, :, :]).then_inc(stored, DMA)
                    sp.wait_ge(stored, DMA)

            counted_sum("l3b", feats[3], sums[3], widths[3])

            def after_l3b(dve, step, summed, t, extra, ready, rooted):
                step(nc.vector.tensor_tensor(summed[:, :, :], summed[:, :, :], over(inv_sqrt), ALU.mult))
                step(nc.vector.tensor_tensor(h[:, :, :], h[:, :, :], over(inv_deg), ALU.mult))
                step(nc.vector.tensor_tensor(h[:, :, :], h[:, :, :], summed[:, :, :], ALU.add))
                step(nc.vector.tensor_tensor(h[:, :, :], h[:, :, :], extra["b2"][:, :].unsqueeze(1).to_broadcast([LANES, PER, D]), ALU.add))
                step(nc.vector.tensor_scalar(h[:, :, :], h[:, :, :], 0.0, None, ALU.max))
                step(nc.vector.tensor_tensor(x[:, :, :], x[:, :, :], h[:, :, :], ALU.add))

            node_step("n6", {"b2": ((LANES, D), spread(a["L3_gnn_b2"]))}, (out.rearrange("(p j) f -> p j f", p=LANES), x), after_l3b,
                      0, sums[3])
    return nc



def kernel(**inputs):
    import concourse.bacc as bacc
    from concourse.bass_utils import run_bass_kernel_spmd

    n_nodes, n_edges = inputs["x"].shape[0], inputs["src"].shape[0]
    groups = n_edges // GROUP
    arrays = {name: np.ascontiguousarray(value) for name, value in inputs.items()}
    for name in ("src", "dst", "edge_weight"):
        arrays[name] = arrays[name].reshape(groups, P, TILES)
    arrays["edge_attr_16"] = np.ascontiguousarray(
        arrays["edge_attr_16"].reshape(groups, P, TILES, DE).transpose(0, 3, 2, 1)).reshape(groups, DE, GROUP)
    nc = bacc.Bacc("TRN2", target_bir_lowering=False, num_devices=1)
    aps = {name: nc.dram_tensor(f"in_{name}", value.shape, mybir.dt.from_np(value.dtype), kind="ExternalInput").ap()
           for name, value in arrays.items()}
    out = nc.dram_tensor("out", (n_nodes, D), F32, kind="ExternalOutput").ap()
    build(nc, aps, out, n_nodes, n_edges)
    result = run_bass_kernel_spmd(nc, [{f"in_{name}": value for name, value in arrays.items()}], core_ids=[0])
    return result.results[0]["out"]
```
